# Optimizing a Trainium2 kernel written in Bass

```python
import numpy as np
import jax
import jax.numpy as jnp

def _softmax(x, axis=-1):
    return jax.nn.softmax(x, axis=axis)

def _gelu(x):
    return jax.nn.gelu(x, approximate=True)

def _silu(x):
    return jax.nn.silu(x)

def _sigmoid(x):
    return jax.nn.sigmoid(x)

def _layernorm(x, axis=-1, eps=1e-05):
    m = jnp.mean(x, axis=axis, keepdims=True)
    v = jnp.var(x, axis=axis, keepdims=True)
    return (x - m) / jnp.sqrt(v + eps)

def _scatter_add(tgt, idx, src, axis=0):
    return tgt.at[idx].add(src)

def _segment_sum(src, seg, n):
    return jax.ops.segment_sum(src, seg, n)
kernel_name = 'mk_perceiver_d1_seqx_r2_bdd742'

def setup_inputs(seed: int=0):
    np.random.seed(seed)
    _w = jnp.asarray

    def _rec_inputs():
        import jax
        import jax.numpy as jnp
        _rk = jax.random.key(seed)
        x = -0.0002928 + 1 * jax.random.normal(jax.random.fold_in(_rk, 1), (32, 32, 512), jnp.float32)
        _lenS = 32 - jax.random.randint(jax.random.fold_in(_rk, 7), (32,), 0, max(1, 32 // 4) + 1, jnp.int32)
        _lenS2 = 257 - jax.random.randint(jax.random.fold_in(_rk, 8), (32,), 0, max(1, 257 // 4) + 1, jnp.int32)
        _ctx_1024P = jax.random.normal(jax.random.fold_in(_rk, 11), (32, 16, 512), jnp.float32)
        _ctx_1024c = jax.random.dirichlet(jax.random.fold_in(_rk, 511), 0.3 * jnp.ones((16,), jnp.float32), (32, 257))
        _ctx_1024t = jnp.einsum('bsk,bkd->bsd', _ctx_1024c, _ctx_1024P)
        _ctx_1024t = _ctx_1024t * jax.lax.rsqrt(jnp.mean(jnp.square(_ctx_1024t)) + 1e-12) * 0.953939
        ctx_1024 = -1.39393e-06 + 0.999914 * (_ctx_1024t + 0.3 * jax.random.normal(jax.random.fold_in(_rk, 611), (32, 257, 512), jnp.float32))
        _validS = jnp.arange(32)[None, :] < _lenS[:, None]
        _validS2 = jnp.arange(257)[None, :] < _lenS2[:, None]
        _causal = jnp.tril(jnp.ones((32, 32), dtype=bool))
        mask_Bx1xSxS2_bf1 = jnp.ones((32, 1, 32, 257), dtype=bool)
        return (x, ctx_1024, mask_Bx1xSxS2_bf1)
    x, ctx_1024, mask_Bx1xSxS2_bf1 = _rec_inputs()

    def _L0_xattn_setup():
        import jax, jax.numpy as jnp
        import numpy as np
        D_MODEL = 512
        N_HEADS = 16
        HEAD_DIM = D_MODEL // N_HEADS
        MAX_LEN = 1024
        MAX_REL = MAX_LEN - 1

        def _relative_bias(rel_emb, tgt_len, src_len):
            rel_pos = jnp.arange(tgt_len)[:, None] - jnp.arange(src_len)[None, :]
            rel_pos = jnp.clip(rel_pos, -MAX_REL, MAX_REL) + MAX_REL
            bias = rel_emb[rel_pos]
            return jnp.transpose(bias, (2, 0, 1))[None]
        key = jax.random.key(seed)
        ks = jax.random.split(key, 12)
        B, T, S = (2, 1024, 1024)
        s = 1.0 / np.sqrt(D_MODEL)
        inp = {'query': jax.random.normal(ks[0], (B, T, D_MODEL), jnp.float32), 'key': jax.random.normal(ks[1], (B, S, D_MODEL), jnp.float32), 'value': jax.random.normal(ks[2], (B, S, D_MODEL), jnp.float32), 'attn_mask': jnp.ones((B, 1, T, S), dtype=bool), 'Wq': jax.random.normal(ks[3], (D_MODEL, D_MODEL), jnp.float32) * s, 'bq': jnp.zeros((D_MODEL,), jnp.float32), 'Wk': jax.random.normal(ks[4], (D_MODEL, D_MODEL), jnp.float32) * s, 'bk': jnp.zeros((D_MODEL,), jnp.float32), 'Wv': jax.random.normal(ks[5], (D_MODEL, D_MODEL), jnp.float32) * s, 'bv': jnp.zeros((D_MODEL,), jnp.float32), 'Wo': jax.random.normal(ks[6], (D_MODEL, D_MODEL), jnp.float32) * s, 'bo': jnp.zeros((D_MODEL,), jnp.float32), 'rel_emb': jax.random.normal(ks[7], (2 * MAX_REL + 1, N_HEADS), jnp.float32) * 0.02}
        return inp
    _L0_xattn_all = _L0_xattn_setup()
    _L0_xattn_in = {k: v for k, v in _L0_xattn_all.items() if k in ('Wq', 'bq', 'Wk', 'bk', 'Wv', 'bv', 'Wo', 'bo', 'rel_emb')}
    del _L0_xattn_all

    def _L0_attn_setup():
        import jax, jax.numpy as jnp
        import numpy as np
        import math
        T, N, D, H = (1024, 2, 512, 16)
        HD = D // H
        key = jax.random.key(seed)
        k1, k2, k3, k4, k5 = jax.random.split(key, 5)
        scale = 0.02
        return {'x': jax.random.normal(k1, (T, N, D), dtype=jnp.float32), 'q_weight': jax.random.normal(k2, (D, H, HD), dtype=jnp.float32) * scale, 'v_weight': jax.random.normal(k3, (D, H, HD), dtype=jnp.float32) * scale, 'out_w': jax.random.normal(k4, (D, D), dtype=jnp.float32) * scale, 'out_b': jax.random.normal(k5, (D,), dtype=jnp.float32) * scale}
    _L0_attn_all = _L0_attn_setup()
    _L0_attn_in = {k: v for k, v in _L0_attn_all.items() if k in ('q_weight', 'v_weight', 'out_w', 'out_b')}
    del _L0_attn_all

    def _L0_ffn_setup():
        import jax, jax.numpy as jnp
        import numpy as np
        DIM = 512
        HIDDEN = 1536
        SCALE = 1.0 / 127.0

        def _dequant(w_int, dtype):
            return w_int.astype(dtype) * jnp.asarray(SCALE, dtype)
        key = jax.random.key(seed)
        k_x, k_g, k_u, k_d = jax.random.split(key, 4)
        x = jax.random.normal(k_x, (4, 1024, DIM), dtype=jnp.float32)
        w_gate = jax.random.randint(k_g, (HIDDEN, DIM), -127, 128, dtype=jnp.int32)
        w_up = jax.random.randint(k_u, (HIDDEN, DIM), -127, 128, dtype=jnp.int32)
        w_down = jax.random.randint(k_d, (DIM, HIDDEN), -127, 128, dtype=jnp.int32)
        return {'x': x, 'w_gate': w_gate, 'w_up': w_up, 'w_down': w_down}
    _L0_ffn_all = _L0_ffn_setup()
    _L0_ffn_in = {k: v for k, v in _L0_ffn_all.items() if k in ('w_gate', 'w_up', 'w_down')}
    del _L0_ffn_all
    return {'x': x, 'ctx_1024': ctx_1024, 'mask_Bx1xSxS2_bf1': mask_Bx1xSxS2_bf1, 'L0_xattn_Wq': _L0_xattn_in['Wq'], 'L0_xattn_bq': _L0_xattn_in['bq'], 'L0_xattn_Wk': _L0_xattn_in['Wk'], 'L0_xattn_bk': _L0_xattn_in['bk'], 'L0_xattn_Wv': _L0_xattn_in['Wv'], 'L0_xattn_bv': _L0_xattn_in['bv'], 'L0_xattn_Wo': _L0_xattn_in['Wo'], 'L0_xattn_bo': _L0_xattn_in['bo'], 'L0_xattn_rel_emb': _L0_xattn_in['rel_emb'], 'L0_attn_q_weight': _L0_attn_in['q_weight'], 'L0_attn_v_weight': _L0_attn_in['v_weight'], 'L0_attn_out_w': _L0_attn_in['out_w'], 'L0_attn_out_b': _L0_attn_in['out_b'], 'L0_ffn_w_gate': _L0_ffn_in['w_gate'], 'L0_ffn_w_up': _L0_ffn_in['w_up'], 'L0_ffn_w_down': _L0_ffn_in['w_down']}

def reference(x, ctx_1024, mask_Bx1xSxS2_bf1, L0_xattn_Wq, L0_xattn_bq, L0_xattn_Wk, L0_xattn_bk, L0_xattn_Wv, L0_xattn_bv, L0_xattn_Wo, L0_xattn_bo, L0_xattn_rel_emb, L0_attn_q_weight, L0_attn_v_weight, L0_attn_out_w, L0_attn_out_b, L0_ffn_w_gate, L0_ffn_w_up, L0_ffn_w_down):
    import jax
    import jax.numpy as jnp

    def _L0_xattn_ref(query, key, value, attn_mask, Wq, bq, Wk, bk, Wv, bv, Wo, bo, rel_emb):
        import jax, jax.numpy as jnp
        import numpy as np
        D_MODEL = 512
        N_HEADS = 16
        HEAD_DIM = D_MODEL // N_HEADS
        MAX_LEN = 1024
        MAX_REL = MAX_LEN - 1

        def _relative_bias(rel_emb, tgt_len, src_len):
            rel_pos = jnp.arange(tgt_len)[:, None] - jnp.arange(src_len)[None, :]
            rel_pos = jnp.clip(rel_pos, -MAX_REL, MAX_REL) + MAX_REL
            bias = rel_emb[rel_pos]
            return jnp.transpose(bias, (2, 0, 1))[None]
        B, T, _ = query.shape
        S = key.shape[1]
        scale = HEAD_DIM ** (-0.5)
        q = (query @ Wq.T + bq).reshape(B, T, N_HEADS, HEAD_DIM).transpose(0, 2, 1, 3)
        k = (key @ Wk.T + bk).reshape(B, S, N_HEADS, HEAD_DIM).transpose(0, 2, 1, 3)
        v = (value @ Wv.T + bv).reshape(B, S, N_HEADS, HEAD_DIM).transpose(0, 2, 1, 3)
        scores = jnp.einsum('bhtd,bhsd->bhts', q, k) * scale
        scores = scores + _relative_bias(rel_emb, T, S)
        scores = jnp.where(attn_mask, scores, -jnp.inf)
        weights = jax.nn.softmax(scores, axis=-1)
        out = jnp.einsum('bhts,bhsd->bhtd', weights, v)
        out = out.transpose(0, 2, 1, 3).reshape(B, T, D_MODEL)
        return out @ Wo.T + bo

    def _L0_attn_ref(x, q_weight, v_weight, out_w, out_b):
        import jax, jax.numpy as jnp
        import numpy as np
        import math
        T, N, D, H = (1024, 2, 512, 16)
        HD = D // H
        head_dim = q_weight.shape[-1]
        inv_sqrt_d = 1.0 / math.sqrt(head_dim)
        q = jnp.einsum('tbm,mhd->tbhd', x, q_weight)
        q_sq = jnp.einsum('tbhd,tbhd->tbh', q, q)
        squared_dist = q_sq[:, None] + q_sq[None, :] - 2.0 * jnp.einsum('tbhd,sbhd->tsbh', q, q)
        attn_logits = -squared_dist * inv_sqrt_d
        attn_weights = jax.nn.softmax(attn_logits, axis=1)
        A = jnp.einsum('mhd,nhd->hmn', q_weight, q_weight) * inv_sqrt_d
        XA = jnp.einsum('tbm,hmn->tbhn', x, A)
        PXA = jnp.einsum('tsbh,sbhm->tbhm', attn_weights, XA)
        PXAV = jnp.einsum('tbhm,mhd->tbhd', PXA, v_weight).reshape(x.shape[0], x.shape[1], -1)
        return PXAV @ out_w.T + out_b

    def _L0_ffn_ref(x, w_gate, w_up, w_down):
        import jax, jax.numpy as jnp
        import numpy as np
        DIM = 512
        HIDDEN = 1536
        SCALE = 1.0 / 127.0

        def _dequant(w_int, dtype):
            return w_int.astype(dtype) * jnp.asarray(SCALE, dtype)
        wg = _dequant(w_gate, x.dtype)
        wu = _dequant(w_up, x.dtype)
        wd = _dequant(w_down, x.dtype)
        gate = jnp.einsum('bsd,hd->bsh', x, wg)
        up = jnp.einsum('bsd,hd->bsh', x, wu)
        h = jax.nn.silu(gate) * up
        return jnp.einsum('bsh,dh->bsd', h, wd)
    x = x + _L0_xattn_ref(_layernorm(x, axis=-1), ctx_1024, ctx_1024, mask_Bx1xSxS2_bf1, L0_xattn_Wq, L0_xattn_bq, L0_xattn_Wk, L0_xattn_bk, L0_xattn_Wv, L0_xattn_bv, L0_xattn_Wo, L0_xattn_bo, L0_xattn_rel_emb)
    x = x + _L0_attn_ref(_layernorm(x, axis=-1), L0_attn_q_weight, L0_attn_v_weight, L0_attn_out_w, L0_attn_out_b)
    x = x + _L0_ffn_ref(_layernorm(x, axis=-1), L0_ffn_w_gate, L0_ffn_w_up, L0_ffn_w_down)
    return x

_drawn_inputs = setup_inputs


def setup_inputs(seed=0):
    import zlib

    import numpy as np

    out = dict(_drawn_inputs(seed))
    spreads = {'L0_xattn_bq': (0.0, 0.299),
     'L0_xattn_bk': (0.0, 2.0),
     'L0_xattn_bv': (0.0, 0.1),
     'L0_xattn_bo': (0.0, 0.1)}
    factors = {'L0_xattn_rel_emb': 25.85,
     'L0_attn_q_weight': 8.0,
     'L0_attn_v_weight': 8.0,
     'L0_attn_out_w': 8.0,
     'L0_attn_out_b': 8.0}
    for name, (base, spread) in spreads.items():
        noise = np.random.default_rng([zlib.crc32(name.encode()), seed]).standard_normal(out[name].shape)
        drawn = base * np.exp(spread * noise) if base else spread * noise
        out[name] = jnp.asarray(drawn.astype(out[name].dtype))
    for name, factor in factors.items():
        out[name] = (out[name] * factor).astype(out[name].dtype)
    return out
```

```python
import math
from contextlib import ExitStack

import concourse.bass as bass
from concourse import mybir

ALU = mybir.AluOpType
ACT = mybir.ActivationFunctionType
AX = mybir.AxisListType
F32 = mybir.dt.float32
F32R = mybir.dt.float32r
I32 = mybir.dt.int32
U8 = mybir.dt.uint8

P = 128
BANK = 512
Q32 = 32
HI, LO = 0, 1
PASSES = ((HI, HI), (HI, LO), (LO, HI))


def perceiver_kernel(
    nc, x, ctx_in, mask, wq, bq, wk, bk, wv, bv, wo, bo, rel_emb, q_weight, v_weight, out_w, out_b,
    w_gate, w_up, w_down, out,
):
    NB, T, D = x.shape
    S = ctx_in.shape[1]
    HD = q_weight.shape[2]
    H = q_weight.shape[1]
    HID = w_gate.shape[0]
    DC = D // P
    G = H * HD // P
    HG = P // HD
    TOK = NB * T
    NT = TOK // P
    SF = 2 * P
    SP_ = S + 1
    SC = 3 * P
    NPAIR = NB // 2
    NJ = HID // P
    MAX_REL = (rel_emb.shape[0] - 1) // 2
    RL = T + S - 1
    SCALE = float(HD) ** -0.5
    INV = 1.0 / math.sqrt(HD)
    WSCALE = 1.0 / 127.0
    EPS = 1e-5
    assert (T, HD, D, S, NB) == (Q32, Q32, BANK, SF + 1, Q32) and RL <= 288
    RLP = 288

    rel_dram = nc.dram_tensor("rel_scratch", (H, RLP), F32, kind="Internal").ap()
    vtail_dram = nc.dram_tensor("vtail_scratch", (NB, D), F32, kind="Internal").ap()

    with ExitStack() as keep:
        def sb(name, shape, dt=F32, stack=keep):
            return stack.enter_context(nc.sbuf_tensor(name, shape, dt))

        def sem(name):
            return keep.enter_context(nc.semaphore(name))

        bank = [keep.enter_context(nc.psum_tensor(f"bank{i}", [P, BANK], F32)) for i in range(8)]

        ident = sb("ident", [P, P])
        blockmask = sb("blockmask", [P, P])
        eye32 = sb("eye32", [P, Q32])
        halfneg = sb("halfneg", [P, P])
        xres = sb("xres", [P, NT, D])
        stats = sb("stats", [P, NT, 6])
        mv = sb("mv", [P, NT, 2])
        ve = sb("ve", [P, NT])
        std = sb("std", [P, NT])
        r0 = sb("r0", [P, NT])
        r1 = sb("r1", [P, NT])
        r2 = sb("r2", [P, NT])
        rstd = sb("rstd", [P, NT])
        bqs = sb("bqs", [P, G])
        bqc = sb("bqc", [P, G])
        bkc = sb("bkc", [P, G])
        bvc = sb("bvc", [P, G])

        bo_bc = sb("bo_bc", [P, D])
        ob_bc = sb("ob_bc", [P, D])

        ph1 = ExitStack()
        wkT = sb("wkT", [P, 2, DC, D], F32R, ph1)
        wvT = sb("wvT", [P, 2, DC, D], F32R, ph1)
        ctxn = sb("ctxn", [P, 2, DC, D], F32, ph1)
        V = sb("V", [P, 2, 4, D], F32, ph1)
        oT = sb("oT", [P, G, T, NB], F32, ph1)
        relbias = sb("relbias", [P, G, S], F32, ph1)
        biasmask = sb("biasmask", [P, 2, G, S], F32, ph1)
        ctxT = sb("ctxT", [P, 2, DC, BANK], F32R, ph1)
        kT = sb("kT", [P, 2, G, 2, SP_], F32R, ph1)
        vtail = sb("vtail", [P, 2, D], F32, ph1)
        Pn = sb("Pn", [P, 2, G, SC], F32, ph1)
        PT = sb("PT", [P, 2, 3, BANK], F32, ph1)
        qbd = sb("qbd", [P, 2, 2, G, P], F32R, ph1)
        qT = sb("qT", [P, G, TOK], F32, ph1)
        qtmp = sb("qtmp", [P, BANK], F32, ph1)
        ktail = sb("ktail", [P, 2, G, NB], F32R, ph1)
        masku = sb("masku", [P, 2, S], U8, ph1)
        maskf = sb("maskf", [P, 2, S], F32, ph1)
        nmax = sb("nmax", [P, 2, G], F32, ph1)
        ssum = sb("ssum", [P, 2, G], F32, ph1)
        rsum = sb("rsum", [P, 2, G], F32, ph1)
        wk_nat = Pn[:].rearrange("p a g s -> p (a g s)")[:, 0:DC * D].rearrange("p (c n) -> p c n", c=DC)
        wv_nat = PT[:].rearrange("p a c s -> p (a c s)")[:, 0:DC * D].rearrange("p (c n) -> p c n", c=DC)
        wq_nat = biasmask[:].rearrange("p a g s -> p (a g s)")[:, 0:DC * D].rearrange("p (c n) -> p c n", c=DC)
        wqT = V[:, 1]
        maskf_rel = maskf[:].rearrange("p b s -> p (b s)")[0:H, 0:RLP]
        xnT = oT[:].rearrange("p g t b -> p g (t b)")
        tail_nat = ctxn[:, 1, 0]
        ctailT = ctxT[:, :, :, 0:P]
        ph1.close()

        ph2 = ExitStack()
        vw = sb("vw", [P, DC, D], F32, ph2)
        ow_nat = sb("ow_nat", [P, DC, D], F32, ph2)
        owT = sb("owT", [P, DC, D], F32, ph2)
        w2 = sb("w2", [P, G, D], F32, ph2)
        wo_nat = sb("wo_nat", [P, DC, D], F32, ph2)
        qw = sb("qw", [P, DC, D], F32, ph2)
        woT = sb("woT", [P, DC, D], F32, ph2)
        xh_first = sb("xh_first", [P, 4, D], F32, ph2)
        sb("over_oT", [P, G, TOK], F32, ph2)
        q2T = sb("q2T", [P, G, TOK], F32, ph2)
        q2n = sb("q2n", [P, NT, D], F32, ph2)
        mbd = sb("mbd", [P, G, P], F32, ph2)
        q2bd = sb("q2bd", [P, 2, G, 4, HG, Q32], F32, ph2)
        sq = sb("sq", [P, D], F32, ph2)
        qsq = sb("qsq", [P, H], F32, ph2)
        hqsq = sb("hqsq", [P, 2, H], F32, ph2)
        dq = sb("dq", [P, 2, H, Q32], F32, ph2)
        lg = sb("lg", [P, H, Q32], F32, ph2)
        lg2 = sb("lg2", [P, H, Q32], F32, ph2)
        e2 = sb("e2", [P, H, Q32], F32, ph2)
        p2 = sb("p2", [P, H, Q32], F32, ph2)
        p2T = sb("p2T", [P, H, Q32], F32, ph2)
        m2 = sb("m2", [P, H], F32, ph2)
        s2 = sb("s2", [P, H], F32, ph2)
        rs2 = sb("rs2", [P, H], F32, ph2)
        pbd = sb("pbd", [P, H, 4, Q32], F32, ph2)
        zT = sb("zT", [P, G, P], F32, ph2)
        w_int = sb("w_int", [P, 2, 3, D], I32, ph2)
        w_f = sb("w_f", [P, 2, 3, D], F32, ph2)
        ph2.close()
        oT2 = oT[:].rearrange("p g t b -> p g (t b)")
        xn2T = oT2
        xh = (xh_first, wo_nat)

        ph3 = ExitStack()
        wT = sb("wT", [P, 2, 3, 2, D], F32R, ph3)
        sb("over_w2", [P, G, D], F32, ph3)
        xn3T = sb("xn3T", [P, 2, DC, TOK], F32R, ph3)
        xh3 = sb("xh3", [P, NT, D], F32, ph3)
        sg = sb("sg", [P, BANK], F32, ph3)
        hf = sb("hf", [P, BANK], F32, ph3)
        hT = sb("hT", [P, 2, 2, BANK], F32R, ph3)
        ph3.close()

        bc_in = sem("bc_in")
        wk_in, wv_in, wq_in, x_in, tail_in, xr_in, bias_in = (
            sem(n) for n in ("wk_in", "wv_in", "wq_in", "x_in", "tail_in", "xr_in", "bias_in"))
        rel_in, rel_out, relb_in, vt_out = (sem(n) for n in ("rel_in", "rel_out", "relb_in", "vt_out"))
        ctx_in_s = [sem(f"ctx_in{i}") for i in range(2)]
        vtail_in = sem("vtail_in")
        mask_in = sem("mask_in")
        const_made = sem("const_made")
        passed = sem("passed")
        pool_step = sem("pool_step")
        pads_made = sem("pads_made")
        split_filled, hi_made, lo_made = sem("split_filled"), sem("hi_made"), sem("lo_made")
        wq_filled, wq_made = sem("wq_filled"), sem("wq_made")
        xt_filled, xt_made = sem("xt_filled"), sem("xt_made")
        q_filled, q_made = sem("q_filled"), sem("q_made")
        vt_filled, vt_made = sem("vt_filled"), sem("vt_made")
        bq_made = sem("bq_made")
        v_filled, v_made = sem("v_filled"), sem("v_made")
        s_filled, s_biased = sem("s_filled"), sem("s_biased")
        max_made, exp_done, rs_made, norm_done = (
            sem(n) for n in ("max_made", "exp_done", "rs_made", "norm_done"))
        pt_filled, pt_made = sem("pt_filled"), sem("pt_made")
        o_filled, o_moved = sem("o_filled"), sem("o_moved")
        qbd_made, bm_made, ktail_made = sem("qbd_made"), sem("bm_made"), sem("ktail_made")
        ln_step, ln_var, ln_std, xh_made, xh_used = (
            sem(n) for n in ("ln_step", "ln_var", "ln_std", "xh_made", "xh_used"))
        ob_made = sem("ob_made")
        w_b_in = sem("w_b_in")
        w_in2 = sem("w_in2")
        ow_in = sem("ow_in")
        wt_filled, wt_made = sem("wt_filled"), sem("wt_made")
        m_filled, m_made = sem("m_filled"), sem("m_made")
        r1_filled, x1_made = sem("r1_filled"), sem("x1_made")
        xb_made = sem("xb_made")
        x2t_filled, x2t_made = sem("x2t_filled"), sem("x2t_made")
        q2_filled, q2_made = sem("q2_filled"), sem("q2_made")
        qn_filled, qn_made = sem("qn_filled"), sem("qn_made")
        dq_made, l_filled, l_read, e2_made, p2T_made, pbd_made = (
            sem(n) for n in ("dq_made", "l_filled", "l_read", "e2_made", "p2T_made", "pbd_made"))
        l2_made = sem("l2_made")
        q2bd_made = sem("q2bd_made")
        z_filled, z_moved = sem("z_filled"), sem("z_moved")
        dve2 = sem("dve2")
        y_filled, x2_made = sem("y_filled"), sem("x2_made")
        x3_filled, x3_hi, x3_lo = sem("x3_filled"), sem("x3_hi"), sem("x3_lo")
        wi_in = [sem(f"wi_in{i}") for i in range(2)]
        wf_made = sem("wf_made")
        fw_filled, fw_hi, fw_lo = sem("fw_filled"), sem("fw_hi"), sem("fw_lo")
        g_filled, g_made = sem("g_filled"), sem("g_made")
        u_filled, h_made, h_hi, h_lo = sem("u_filled"), sem("h_made"), sem("h_hi"), sem("h_lo")
        d_done, acc_filled, x3_made = sem("d_done"), sem("acc_filled"), sem("x3_made")
        out_stored = sem("out_stored")
        zero_made = sem("zero_made")

        N0 = DC + DC + 2
        QN_BANK = (4, 7, 4, 7, 6, 7, 6, 7)
        O_BANK = (7, 2)
        KEYS_AFTER = (1, 3, 6, 7)
        ORDER = ((0, 0), (1, 0), (0, 1), (1, 1), (0, 2), (0, 3), (1, 2), (1, 3))
        block = keep.enter_context(nc.Block())

        def wait_alone(eng, s, value):
            eng.wait_ge(s, value)
            eng.sem_inc(passed, 1)

        x_bt = x.rearrange("b t m -> (b t) m").rearrange("(i p) m -> p i m", p=P)

        @block.sync
        def _(sp):
            def w_nat(w):
                return w.rearrange("(c p) n -> p c n", p=P)

            sp.dma_start(wk_nat, w_nat(wk)).then_inc(wk_in, 16)
            sp.dma_start(wv_nat, w_nat(wv)).then_inc(wv_in, 16)
            sp.dma_start(xres[:], x_bt).then_inc(x_in, 16)
            sp.wait_ge(zero_made, 1)
            sp.dma_start(tail_nat[0:NB, :], ctx_in[:, SF, :]).then_inc(tail_in, 16)
            sp.dma_start(wq_nat, w_nat(wq)).then_inc(wq_in, 16)
            for dst, src in ((bo_bc, bo), (ob_bc, out_b)):
                sp.dma_start(dst[:], src.rearrange("(o n) -> o n", o=1).to_broadcast([P, D])).then_inc(bc_in, 16)

            def load_ctx(q, par):
                for b in range(2):
                    sp.dma_start(ctxn[:, par, 2 * b:2 * b + 2, :],
                                 ctx_in[2 * q + b, 0:SF, :].rearrange("(c p) m -> p c m", p=P)
                                 ).then_inc(ctx_in_s[par], 16)

            def load_vtail(q):
                sp.dma_start(vtail[0:1, :, :],
                             vtail_dram[bass.ds(2 * q, 2), :].rearrange("(o b) n -> o b n", o=1)
                             ).then_inc(vtail_in, 16)

            def load_mask(q):
                for b in range(2):
                    for h in range(HG):
                        sp.dma_start(masku[h * T:(h + 1) * T, b, :], mask[2 * q + b, 0, :, :]
                                     ).then_inc(mask_in, 16)

            load_ctx(0, 0)
            load_mask(0)
            sp.wait_ge(rel_out, 16)
            for t in range(T):
                src = bass.AP(rel_dram.tensor, T - 1 - t, [[RLP, HG], [HG * RLP, G], [1, S]])
                sp.dma_start(relbias[t:P:T, :, :], src).then_inc(relb_in, 16)
            sp.wait_ge(xt_filled, 8)
            for i in range(NT):
                for t in range(4):
                    sp.dma_start(xres[t * NB:(t + 1) * NB, i, :], x[:, 4 * i + t, :]).then_inc(xr_in, 16)
            sp.wait_ge(split_filled, 2 * DC + 1)
            sp.wait_ge(vt_out, 16)
            load_ctx(1, 1)
            sp.wait_ge(pads_made, 1)
            load_vtail(0)

            def next_ctx(q, par):
                wait_alone(sp, split_filled, N0 + 8 * q + 4)
                load_ctx(q + 2, par)

            def step(p, par, ctx_more):
                wait_alone(sp, bm_made, 2 * p + 2)
                load_mask(p + 1)
                wait_alone(sp, o_filled, 2 * p + 2)
                load_vtail(p + 1)
                if ctx_more:
                    next_ctx(p + 2, par)

            next_ctx(0, 0)
            next_ctx(1, 1)
            with sp.Fori(0, (NPAIR - 4) // 2) as it:
                for u in range(2):
                    step(2 * it + u, u, True)
            for p in range(NPAIR - 4, NPAIR - 1):
                step(p, p % 2, False)

            last = NPAIR - 1
            sp.wait_ge(split_filled, N0 + 8 * last + 8)
            sp.dma_start(wo_nat[:], w_nat(wo)).then_inc(w_b_in, 16)
            sp.wait_ge(v_filled, 4 * last + 4)
            sp.dma_start(ow_nat[:], w_nat(out_w)).then_inc(ow_in, 16)
            sp.dma_start(qw[:], q_weight.rearrange("(c p) h d -> p c (h d)", p=P)).then_inc(w_in2, 16)
            sp.dma_start(vw[:], v_weight.rearrange("(c p) h d -> p c (h d)", p=P)).then_inc(w_in2, 16)

            sp.wait_ge(o_filled, 2 * NPAIR)
            def load_w(j, par):
                sp.dma_start(w_int[:, par, 0, :], w_gate[bass.ds(j * P, P), :]).then_inc(wi_in[par], 16)
                sp.dma_start(w_int[:, par, 1, :], w_up[bass.ds(j * P, P), :]).then_inc(wi_in[par], 16)
                sp.dma_start(w_int[:, par, 2, :].rearrange("p (c k) -> p c k", c=DC),
                             w_down[:, bass.ds(j * P, P)].rearrange("(c p) k -> p c k", p=P)
                             ).then_inc(wi_in[par], 16)

            for half in range(2):
                for j in range(2):
                    if half:
                        sp.wait_ge(wf_made, half * NJ + j - 1)
                    load_w(j, j)
                with sp.Fori(0, (NJ - 2) // 2) as it:
                    for u in range(2):
                        wait_alone(sp, wf_made, 2 * it + (half * NJ + u + 1))
                        load_w(2 * it + (u + 2), u)
            for half in range(2):
                for i in range(4):
                    k = 4 * half + i
                    sp.wait_ge(x3_made, k + 1)
                    for t in range(4):
                        sp.dma_start(out[:, 4 * k + t, :], xres[t * NB:(t + 1) * NB, k, :]
                                     ).then_inc(out_stored, 16)
            sp.wait_ge(out_stored, 16 * 4 * NT)

        @block.gpsimd
        def _(pool):
            step_n = [0]

            def link(ins):
                step_n[0] += 1
                ins.then_inc(pool_step, 1)
                pool.wait_ge(pool_step, step_n[0])

            pool.memset(tail_nat, 0.0).then_inc(zero_made, 1)
            link(pool.memset(ident[:], 0.0))
            link(pool.memset(blockmask[:], 1.0))
            link(pool.memset(eye32[:], 0.0))
            pool.affine_select(out=ident[:], in_=ident[:], compare_op=ALU.not_equal, fill=1.0, base=0,
                               pattern=[[-1, P]], channel_multiplier=1).then_inc(const_made, 1)
            bm3 = blockmask[:].rearrange("p (h d) -> p h d", h=HG)
            link(pool.affine_select(out=bm3, in_=bm3, compare_op=ALU.is_ge, fill=0.0, base=0,
                                    pattern=[[-Q32, HG], [0, Q32]], channel_multiplier=1))
            link(pool.affine_select(out=bm3, in_=bm3, compare_op=ALU.is_ge, fill=0.0, base=Q32 - 1,
                                    pattern=[[Q32, HG], [0, Q32]], channel_multiplier=-1))
            for k in range(HG):
                link(pool.affine_select(out=eye32[:], in_=eye32[:], compare_op=ALU.not_equal, fill=1.0,
                                        base=-Q32 * k, pattern=[[-1, Q32]], channel_multiplier=1))
            pool.tensor_scalar(halfneg[:], blockmask[:], -0.5, None, ALU.mult).then_inc(const_made, 1)

            with nc.allow_non_contiguous_dma(reason="small bias rows, once"):
                for name_ap, w in ((bqc, bq), (bkc, bk), (bvc, bv)):
                    pool.dma_start(name_ap[:], w.rearrange("(g p) -> p g", p=P)).then_inc(bias_in, 16)
                rel_sb = qtmp[0:H, 0:RLP]
                pool.dma_start(rel_sb, rel_emb[MAX_REL + T - RLP:MAX_REL + T, :].rearrange("i h -> h i")
                               ).then_inc(rel_in, 16)
            pool.wait_ge(rel_in, 16)
            link(pool.tensor_copy(maskf_rel, rel_sb[:, ::-1]))
            pool.dma_start(rel_dram, maskf_rel).then_inc(rel_out, 16)
            pool.wait_ge(bias_in, 48)
            pool.tensor_scalar(bqs[:], bqc[:], SCALE, None, ALU.mult).then_inc(bq_made, 1)

            pool.memset(vtail[:], 0.0).then_inc(pads_made, 1)
            for part in range(2):
                pool.memset(kT[:, part, :, :, S:SP_].bitcast(F32), 0.0)
            pool.wait_ge(split_filled, DC)
            pool.memset(Pn[:, :, :, S:SC], 0.0).then_inc(pads_made, 1)

            hmask = blockmask[:].rearrange("p (h d) -> p h d", h=HG)

            def prepare(q, first):
                if not first:
                    pool.wait_ge(s_filled, 8 * q)
                for b in range(2):
                    t3 = qtmp[:].rearrange("p (g h t) -> p g h t", g=G, h=HG)
                    for g in range(G):
                        src = qT[:, g, bass.ds((2 * q + b) * T, T)].unsqueeze(1).to_broadcast([P, HG, T])
                        ins = pool.tensor_tensor(t3[:, g], src, hmask, ALU.mult)
                    ins.then_inc(pool_step, 1)
                    wait_alone(pool, pool_step, step_n[0] + 6 * q + 3 * b + 1)
                    qf = qtmp[:].rearrange("p (g c) -> p g c", g=G)
                    pool.tensor_copy(qbd[:, HI, b], qf).then_inc(pool_step, 1)
                    wait_alone(pool, pool_step, step_n[0] + 6 * q + 3 * b + 2)
                    ins = pool.tensor_tensor(qbd[:, LO, b], qf, qbd[:, HI, b].bitcast(F32), ALU.subtract)
                    ins.then_inc(pool_step, 1)
                    pool.wait_ge(pool_step, step_n[0] + 6 * q + 3 * b + 3)
                for part in range(2):
                    ins = pool.tensor_copy(kT[:, part, :, :, SF],
                                           ktail[:, part, :, bass.ds(2 * q, 2)])
                ins.then_inc(qbd_made, 1)
                wait_alone(pool, mask_in, 16 * 2 * HG * (q + 1))
                pool.tensor_scalar(maskf[:], masku[:], -1.0, 3.0e38, ALU.add, ALU.mult).then_inc(ktail_made, 1)
                wait_alone(pool, ktail_made, 2 * q + 1)
                pool.tensor_scalar(maskf[:], maskf[:], 4.0, None, ALU.mult).then_inc(ktail_made, 1)
                wait_alone(pool, ktail_made, 2 * q + 2)
                for b in range(2):
                    if not first:
                        pool.wait_ge(s_biased, 8 * q)
                    pool.tensor_tensor(biasmask[:, b], relbias[:],
                                       maskf[:, b].unsqueeze(1).to_broadcast([P, G, S]), ALU.add
                                       ).then_inc(bm_made, 1)

            pool.wait_ge(q_made, 8)
            pool.wait_ge(lo_made, N0)
            pool.wait_ge(relb_in, 16 * T)
            prepare(0, True)
            with pool.Fori(1, NPAIR) as q:
                prepare(q, False)

            for i in range(NT):
                if i == 0:
                    pool.wait_ge(xr_in, 16 * 4 * NT)
                    pool.wait_ge(bc_in, 32)
                pool.tensor_tensor(xres[:, i, :], xres[:, i, :], bo_bc[:], ALU.add).then_inc(xb_made, 1)
            pool.wait_ge(o_moved, 2 * NPAIR)
            pool.memset(q2bd[:], 0.0).then_inc(zero_made, 1)
            pool.memset(pbd[:], 0.0).then_inc(zero_made, 1)
            pool.wait_ge(zero_made, 3)
            for i in range(NT):
                pool.wait_ge(q2_made, 4 * (i // 4) + 4)
                if i >= 2:
                    pool.wait_ge(l_filled, i - 1)
                src = q2T[:, :, i * P:(i + 1) * P].rearrange("p g (n s) -> p g n s", n=4)
                for h in range(HG):
                    ins = pool.tensor_copy(q2bd[h * Q32:(h + 1) * Q32, i % 2, :, :, h, :],
                                           src[h * Q32:(h + 1) * Q32])
                ins.then_inc(q2bd_made, 1)
                if i == 3:
                    pool.wait_ge(xh_made, 2 * NT)
                    pool.wait_ge(q2bd_made, 4)
                    for j in range(NT):
                        pool.tensor_tensor(xres[:, j, :], xres[:, j, :], ob_bc[:], ALU.add).then_inc(xb_made, 1)
                    pool.wait_ge(xb_made, 2 * NT)

            pool.wait_ge(q2bd_made, NT)
            def convert(n, j2, half, par):
                pool.wait_ge(wi_in[par], 48 * j2 + 48 * (half * NJ // 2 + 1))
                if not (isinstance(n, int) and n < 2):
                    wait_alone(pool, fw_filled, 3 * n - 3)
                pool.tensor_copy(w_f[:, par], w_int[:, par]).then_inc(wf_made, 1)

            for half in range(2):
                for j in range(2):
                    convert(half * NJ + j, 0, half, j)
                with pool.Fori(0, (NJ - 2) // 2) as it:
                    for u in range(2):
                        convert(2 * it + (half * NJ + 2 + u), it + 1, half, u)

        @block.tensor
        def _(pe):
            def mm3(dst, lhs, rhs, first, last):
                for n, (a, b) in enumerate(PASSES):
                    ins = pe.matmul(dst, lhs(a), rhs(b), start=first and n == 0, stop=last and n == 2)
                return ins

            pe.wait_ge(const_made, 2)
            fill = 0
            for nat, loaded in ((wk_nat, wk_in), (wv_nat, wv_in)):
                pe.wait_ge(loaded, 16)
                for k in range(DC):
                    if fill >= 2:
                        pe.wait_ge(lo_made, fill - 1)
                    for c in range(DC):
                        ins = pe.transpose(bank[fill % 2][:, c * P:(c + 1) * P], nat[:, c, k * P:(k + 1) * P], ident[:])
                    ins.then_inc(split_filled, 1)
                    fill += 1
            pe.wait_ge(tail_in, 16)
            pe.wait_ge(lo_made, fill - 1)
            for k in range(DC):
                ins = pe.transpose(bank[fill % 2][:, k * P:(k + 1) * P], tail_nat[:, k * P:(k + 1) * P], ident[:])
            ins.then_inc(split_filled, 1)
            fill += 1
            pe.wait_ge(wq_in, 16)
            for k in range(DC):
                if k >= 2:
                    pe.wait_ge(wq_made, k - 1)
                for c in range(DC):
                    ins = pe.transpose(bank[2 + k % 2][:, c * P:(c + 1) * P], wq_nat[:, c, k * P:(k + 1) * P], ident[:])
                ins.then_inc(wq_filled, 1)
            pe.wait_ge(lo_made, fill)
            for g in range(G):
                for k in range(DC):
                    ins = mm3(bank[fill % 2][:, g * NB:(g + 1) * NB],
                              lambda a: wkT[:, a, k, g * P:(g + 1) * P],
                              lambda b: ctailT[:, b, k, 0:NB], k == 0, k == DC - 1)
            ins.then_inc(split_filled, 1)
            fill += 1
            for k in range(DC):
                ins = mm3(bank[4][:], lambda a: ctailT[:, a, k, :], lambda b: wvT[:, b, k, :],
                          k == 0, k == DC - 1)
            ins.then_inc(vt_filled, 1)
            for n in range(8):
                half, k = divmod(n, DC)
                pe.wait_ge(xh_made, 4 * half + 4)
                if n >= 2:
                    pe.wait_ge(xt_made, n - 1)
                for c in range(4):
                    ins = pe.transpose(bank[6 + n % 2][:, c * P:(c + 1) * P],
                                       xres[:, 4 * half + c, k * P:(k + 1) * P], ident[:])
                ins.then_inc(xt_filled, 1)
            pe.wait_ge(wq_made, DC)
            for n in range(8):
                half, g = divmod(n, G)
                pe.wait_ge(xt_made, 4 * half + 4)
                if n >= 2:
                    pe.wait_ge(q_made, n - 1)
                for k in range(DC):
                    ins = pe.matmul(bank[2 + n % 2][:], wqT[:, k, g * P:(g + 1) * P],
                                    xnT[:, k, half * BANK:(half + 1) * BANK], start=k == 0, stop=k == DC - 1)
                ins.then_inc(q_filled, 1)
            assert fill == N0
            pe.wait_ge(vt_made, 1)
            pe.wait_ge(q_made, 8)

            def turn(q, par, m):
                pe.wait_ge(lo_made, N0 + 8 * q + m - 1)
                for i in range(4):
                    ins = pe.transpose(bank[m % 2][:, i * P:(i + 1) * P],
                                       ctxn[:, par, i, m * P:(m + 1) * P], ident[:])
                ins.then_inc(split_filled, 1)

            def keys(q, g):
                pe.wait_ge(lo_made, N0 + 8 * q + 4 + max(g - 1, 0))
                for m in range(DC):
                    ins = mm3(bank[g % 2][:], lambda a: wkT[:, a, m, g * P:(g + 1) * P],
                              lambda b: ctxT[:, b, m, :], m == 0, m == DC - 1)
                ins.then_inc(split_filled, 1)

            def values(q, i, first):
                if not (first and i < 2):
                    pe.wait_ge(v_made, 4 * q + i - 1)
                for m in range(DC):
                    ins = mm3(bank[2 + i % 2][:], lambda a: ctxT[:, a, m, i * P:(i + 1) * P],
                              lambda b: wvT[:, b, m, :], m == 0, m == DC - 1)
                ins.then_inc(v_filled, 1)

            def scores(p, n, first):
                b, g = ORDER[n]
                if n == 0:
                    pe.wait_ge(lo_made, N0 + 8 * p + 8)
                    pe.wait_ge(qbd_made, p + 1)
                if not (first and n < 2):
                    pe.wait_ge(s_biased, 8 * p + n - 1)
                ins = mm3(bank[4 + n % 2][:, 0:SP_], lambda a: qbd[:, a, b, g, :],
                          lambda c: kT[:, c, g, b, :], True, True)
                ins.then_inc(s_filled, 1)

            def probs_turn(p, b, c):
                n = 3 * b + c
                if c == 0:
                    pe.wait_ge(norm_done, 2 * p + b + 1)
                if n >= 2:
                    pe.wait_ge(pt_made, 6 * p + n - 1)
                for g in range(G):
                    ins = pe.transpose(bank[(6, 5)[n % 2]][:, g * P:(g + 1) * P], Pn[:, b, g, c * P:(c + 1) * P],
                                       ident[:])
                ins.then_inc(pt_filled, 1)

            def attend(p, par, b, first=False, more=True):
                pe.wait_ge(pt_made, 6 * p + 3 * b + 3)
                if b == 0:
                    pe.wait_ge(v_made, 4 * p + 4)
                    vt_wait(p, par)
                else:
                    pe.wait_ge(v_made, 4 * p + (8 if more else 4))
                if b == 0 and not first:
                    pe.wait_ge(o_moved, 2 * p)
                for g in range(G):
                    cols = slice(g * P, (g + 1) * P)
                    for c in range(3):
                        lhs = V[:, par, 2 * b + c, cols] if c < 2 else vtail[:, b, cols]
                        ins = pe.matmul(bank[O_BANK[b]][:, cols], lhs, PT[:, b, c, cols], start=c == 0, stop=c == 2)
                ins.then_inc(o_filled, 1)

            def vt_wait(p, par):
                pe.wait_ge(vtail_in, 16 * p + 16)

            def ctx_wait(q, par):
                pe.wait_ge(ctx_in_s[par], 16 * q + 32 - 16 * par)

            def project(q, par):
                ctx_wait(q, par)
                for m in range(DC):
                    turn(q, par, m)
                for g in range(G):
                    keys(q, g)
                for i in range(4):
                    values(q, i, True)

            def step(p, par, first=False, more=True):
                q = p + 1
                for n in range(8):
                    scores(p, n, first)
                    if n in KEYS_AFTER:
                        keys(q, KEYS_AFTER.index(n))
                if not first:
                    pe.wait_ge(o_moved, 2 * p)
                for i in range(4):
                    values(q, i, False)
                    probs_turn(p, i // 3, i % 3)
                if more:
                    ctx_wait(p + 2, par)
                    turn(p + 2, par, 0)
                probs_turn(p, 1, 1)
                if more:
                    turn(p + 2, par, 1)
                probs_turn(p, 1, 2)
                if more:
                    turn(p + 2, par, 2)
                attend(p, par, 0, first)
                if more:
                    turn(p + 2, par, 3)
                attend(p, par, 1)

            project(0, 0)
            ctx_wait(1, 1)
            for m in range(DC):
                turn(1, 1, m)
            step(0, 0, first=True)
            with pe.Fori(0, (NPAIR - 4) // 2) as it:
                for u in range(2):
                    step(2 * it + 1 + u, (1 + u) % 2)
            step(NPAIR - 3, 1)
            step(NPAIR - 2, 0, more=False)
            last = NPAIR - 1

            def turn_weight(n):
                nat, k = (wo_nat, ow_nat)[n // DC], n % DC
                if k == 0:
                    pe.wait_ge((w_b_in, ow_in)[n // DC], 16)
                if n >= 2:
                    pe.wait_ge(wt_made, n - 1)
                for c in range(DC):
                    ins = pe.transpose(bank[n % 2][:, c * P:(c + 1) * P], nat[:, c, k * P:(k + 1) * P], ident[:])
                ins.then_inc(wt_filled, 1)

            for g in range(G):
                scores(last, 2 * g, False)
                scores(last, 2 * g + 1, False)
                turn_weight(g)
            for c in range(3):
                probs_turn(last, 0, c)
                turn_weight(4 + c)
            probs_turn(last, 1, 0)
            turn_weight(7)
            probs_turn(last, 1, 1)
            attend(last, 1, 0)
            probs_turn(last, 1, 2)
            pe.wait_ge(w_in2, 32)
            for g in range(G):
                cols = slice(g * P, (g + 1) * P)
                for k in range(DC):
                    ins = pe.matmul(bank[3][:, cols], vw[:, k, cols], qw[:, k, cols], start=k == 0, stop=k == DC - 1)
            ins.then_inc(m_filled, 1)
            attend(last, 1, 1, more=False)
            pe.wait_ge(m_made, 1)
            for g in range(G):
                pe.wait_ge(wt_made, 2 * DC + max(g - 1, 0))
                ins = pe.matmul(bank[g % 2][:], mbd[:, g, :], owT[:, g, :], start=True, stop=True)
                ins.then_inc(wt_filled, 1)

            pe.wait_ge(ob_made, 4)
            for i in range(NT):
                if i >= 2:
                    pe.wait_ge(x1_made, i - 1)
                for k in range(DC):
                    ins = pe.matmul(bank[2 + i % 2][:], oT2[:, k, i * P:(i + 1) * P], woT[:, k, :],
                                    start=k == 0, stop=k == DC - 1)
                ins.then_inc(r1_filled, 1)

            pe.wait_ge(wt_made, 3 * DC)

            def turn_x2(half):
                pe.wait_ge(xh_made, 8 + 4 * half + 4)
                for k in range(DC):
                    n = DC * half + k
                    if n >= 2:
                        pe.wait_ge(x2t_made, n - 1)
                    for c in range(4):
                        ins = pe.transpose(bank[n % 2][:, c * P:(c + 1) * P],
                                           xh[half][:, c, k * P:(k + 1) * P], ident[:])
                    ins.then_inc(x2t_filled, 1)

            def queries2(half):
                pe.wait_ge(x2t_made, 4 * half + 4)
                for g in range(G):
                    n = G * half + g
                    if n >= 2:
                        pe.wait_ge(q2_made, n - 1)
                    for k in range(DC):
                        ins = pe.matmul(bank[5 + n % 2][:], qw[:, k, g * P:(g + 1) * P],
                                        xn2T[:, k, half * BANK:(half + 1) * BANK], start=k == 0, stop=k == DC - 1)
                    ins.then_inc(q2_filled, 1)

            def turn_q2(i):
                pe.wait_ge(q2_made, 4 * (i // 4) + 4)
                if i >= 2:
                    pe.wait_ge(qn_made, i - 1)
                for g in range(G):
                    ins = pe.transpose(bank[QN_BANK[i]][:, g * P:(g + 1) * P],
                                       q2T[:, g, i * P:(i + 1) * P], ident[:])
                ins.then_inc(qn_filled, 1)

            def logits2(i):
                pe.wait_ge(dq_made, i + 1)
                pe.wait_ge(q2bd_made, i + 1)
                if i == 0:
                    pe.wait_ge(x2t_made, 8)
                if i >= 2:
                    pe.wait_ge(l_read, i - 1)
                L = bank[i % 2]
                pe.matmul(L[:], halfneg[:], dq[:, i % 2].rearrange("p h s -> p (h s)"), start=True, stop=False,
                          skip_group_check=True)
                for n in range(4):
                    for g in range(G):
                        ins = pe.matmul(L[n * Q32:(n + 1) * Q32, g * P:(g + 1) * P],
                                        q2T[:, g, i * P + n * Q32:i * P + (n + 1) * Q32],
                                        q2bd[:, i % 2, g, n].rearrange("p h s -> p (h s)"),
                                        start=False, stop=g == G - 1, skip_group_check=True)
                ins.then_inc(l_filled, 1)

            def attend2(i):
                pe.wait_ge(pbd_made, i + 1)
                if i >= 1:
                    pe.wait_ge(z_moved, i)
                for h in range(H):
                    g, r = divmod(h, HG)
                    ins = pe.matmul(bank[2][r * Q32:(r + 1) * Q32, g * P:(g + 1) * P],
                                    q2n[:, i, h * HD:(h + 1) * HD], pbd[:, h].rearrange("p n t -> p (n t)"),
                                    start=True, stop=True, skip_group_check=True)
                ins.then_inc(z_filled, 1)

            def project2(i):
                pe.wait_ge(z_moved, i + 1)
                if i == 0:
                    pe.wait_ge(qn_made, 4)
                if i >= 2:
                    pe.wait_ge(x2_made, i - 1)
                for g in range(G):
                    ins = pe.matmul(bank[3 + i % 2][:], zT[:, g, :], w2[:, g, :], start=g == 0, stop=g == G - 1)
                ins.then_inc(y_filled, 1)

            turn_x2(0)
            queries2(0)
            turn_x2(1)
            for i in range(4):
                turn_q2(i)
            logits2(0)
            logits2(1)
            queries2(1)
            for i in range(NT):
                attend2(i)
                if i < 4:
                    turn_q2(4 + i)
                if i + 2 < NT:
                    logits2(i + 2)
                project2(i)

            def turn_x3(half):
                pe.wait_ge(xh_made, 16 + 4 * half + 4)
                if half == 0:
                    pe.wait_ge(qn_made, NT)
                else:
                    pe.wait_ge(x2_made, NT)
                    pe.wait_ge(x3_lo, 4)
                for k in range(DC):
                    if half == 0 and k >= 2:
                        pe.wait_ge(x3_lo, k - 1)
                    b = bank[4 + k] if half else bank[5 + k % 2]
                    for c in range(4):
                        ins = pe.transpose(b[:, c * P:(c + 1) * P], xh3[:, 4 * half + c, k * P:(k + 1) * P], ident[:])
                    ins.then_inc(x3_filled, 1)

            def weights(n, par, w, first=False):
                if w == 0:
                    pe.wait_ge(wf_made, n + 1)
                k = 3 * n + w
                if not (isinstance(n, int) and k < 2):
                    pe.wait_ge(fw_lo, k - 1)
                for c in range(DC):
                    ins = pe.transpose(bank[(3 * par + w) % 2][:, c * P:(c + 1) * P],
                                       w_f[:, par, w, c * P:(c + 1) * P], ident[:])
                ins.then_inc(fw_filled, 1)

            def gate_up(n, par, half, w, filled, freed):
                pe.wait_ge(fw_lo, 3 * n + w + 1)
                if not (isinstance(n, int) and n < 1):
                    pe.wait_ge(freed, n)
                for k in range(DC):
                    ins = mm3(bank[2 + w][:], lambda a: wT[:, par, w, a, k * P:(k + 1) * P],
                              lambda b: xn3T[:, b, k, half * BANK:(half + 1) * BANK], k == 0, k == DC - 1)
                ins.then_inc(filled, 1)

            def down(n, par, first, last):
                pe.wait_ge(h_lo, n + 1)
                pe.wait_ge(fw_lo, 3 * n + 3)
                for t in range(4):
                    ins = mm3(bank[4 + t][:], lambda a: hT[:, par, a, t * P:(t + 1) * P],
                              lambda b: wT[:, par, 2, b, :], first, last)
                ins.then_inc(d_done, 1)

            def ffn_step(n, par, half, prev, first_down=False, more=True):
                if more:
                    weights(n + 1, 1 - par, 0)
                gate_up(n, par, half, 0, g_filled, g_made)
                if more:
                    weights(n + 1, 1 - par, 1)
                gate_up(n, par, half, 1, u_filled, h_made)
                if more:
                    weights(n + 1, 1 - par, 2)
                if prev:
                    down(n - 1, 1 - par, first_down, False)

            turn_x3(0)
            pe.wait_ge(l_read, NT)
            pe.wait_ge(z_moved, NT)
            pe.wait_ge(x2_made, NT)
            for w in range(3):
                weights(0, 0, w)
            pe.wait_ge(x3_lo, 4)
            for half in range(2):
                base = half * NJ
                ffn_step(base, 0, half, False)
                if half:
                    pe.wait_ge(x3_made, 4)
                else:
                    turn_x3(1)
                    pe.wait_ge(x3_lo, 8)
                ffn_step(base + 1, 1, half, True, first_down=True)
                with pe.Fori(0, (NJ - 4) // 2) as it:
                    for u in range(2):
                        ffn_step(2 * it + (base + 2 + u), u, half, True)
                ffn_step(base + NJ - 2, 0, half, True)
                ffn_step(base + NJ - 1, 1, half, True, more=half == 0)
                down(base + NJ - 1, 1, False, True)

        @block.scalar
        def _(act):
            fill = 0
            for dst in (wkT, wvT):
                for k in range(DC):
                    act.wait_ge(split_filled, fill + 1)
                    act.copy(dst[:, HI, k, :], bank[fill % 2][:]).then_inc(hi_made, 1)
                    fill += 1
            act.wait_ge(split_filled, fill + 1)
            act.copy(ctailT[:, HI], bank[fill % 2][:].rearrange("p (k r) -> p k r", k=DC)).then_inc(hi_made, 1)
            fill += 1
            for k in range(DC):
                act.wait_ge(wq_filled, k + 1)
                act.copy(wqT[:, k, :], bank[2 + k % 2][:]).then_inc(wq_made, 1)
            act.wait_ge(split_filled, fill + 1)
            act.wait_ge(bias_in, 48)
            for g in range(G):
                ins = act.activation(ktail[:, HI, g, :], bank[fill % 2][:, g * NB:(g + 1) * NB], ACT.Identity,
                                     bias=bkc[:, g:g + 1])
            ins.then_inc(hi_made, 1)
            act.wait_ge(vt_filled, 1)
            act.wait_ge(tail_in, 16)
            vt_sb = ctxn[:, 1, 1, :]
            act.copy(vt_sb, bank[4][:]).then_inc(vt_made, 1)
            act.wait_ge(vt_made, 1)
            act.dma_start(vtail_dram, vt_sb[0:NB, :]).then_inc(vt_out, 16)
            act.wait_ge(ln_var, 1)
            act.activation(std[:], ve[:], ACT.Sqrt).then_inc(ln_std, 1)
            act.wait_ge(bq_made, 1)
            for n in range(8):
                half, g = divmod(n, G)
                act.wait_ge(q_filled, n + 1)
                act.activation(qT[:, g, half * BANK:(half + 1) * BANK], bank[2 + n % 2][:], ACT.Identity,
                               bias=bqs[:, g:g + 1], scale=SCALE).then_inc(q_made, 1)

            def turn_hi(q, m):
                act.wait_ge(split_filled, N0 + 8 * q + m + 1)
                act.copy(ctxT[:, HI, m, :], bank[m % 2][:]).then_inc(hi_made, 1)

            def keys_hi(q, g):
                act.wait_ge(split_filled, N0 + 8 * q + 4 + g + 1)
                act.activation(kT[:, HI, g, :, 0:SF], bank[g % 2][:].rearrange("p (b s) -> p b s", b=2),
                               ACT.Identity, bias=bkc[:, g:g + 1]).then_inc(hi_made, 1)

            def values_out(q, par, i):
                act.wait_ge(v_filled, 4 * q + i + 1)
                act.copy(V[:, par, i, :], bank[2 + i % 2][:]).then_inc(v_made, 1)

            def exps(p, b):
                act.wait_ge(max_made, 2 * p + b + 1)
                for g in range(G):
                    act.activation(Pn[:, b, g, 0:S], Pn[:, b, g, 0:S], ACT.Exp, bias=nmax[:, b, g:g + 1],
                                   accum_out=ssum[:, b, g:g + 1]).then_inc(exp_done, 1)

            def out_move(p, b):
                act.wait_ge(o_filled, 2 * p + b + 1)
                for h in range(HG):
                    rows = slice(h * Q32, (h + 1) * Q32)
                    src = bank[O_BANK[b]][rows, :].rearrange("p (g h t) -> p g h t", g=G, h=HG)[:, :, h, :]
                    ins = act.copy(oT[rows, :, :, bass.ds(2 * p + b, 1)], src.unsqueeze(3))
                ins.then_inc(o_moved, 1)

            for m in range(DC):
                turn_hi(0, m)
            for g in range(G):
                keys_hi(0, g)
            for i in range(4):
                values_out(0, 0, i)

            for m in range(DC):
                turn_hi(1, m)

            def step(p, par, more=True):
                keys_hi(p + 1, 0)
                keys_hi(p + 1, 1)
                exps(p, 0)
                keys_hi(p + 1, 2)
                keys_hi(p + 1, 3)
                exps(p, 1)
                for i in range(4):
                    values_out(p + 1, 1 - par, i)
                if more:
                    for m in range(3):
                        turn_hi(p + 2, m)
                out_move(p, 0)
                if more:
                    turn_hi(p + 2, 3)
                out_move(p, 1)

            act.wait_ge(pads_made, 2)
            step(0, 0)
            with act.Fori(0, (NPAIR - 4) // 2) as it:
                for u in range(2):
                    step(2 * it + 1 + u, (1 + u) % 2)
            step(NPAIR - 3, 1)
            step(NPAIR - 2, 0, more=False)
            last = NPAIR - 1

            def weight_out(n):
                dst, k = (woT, owT, w2)[n // DC], n % DC
                act.wait_ge(wt_filled, n + 1)
                act.copy(dst[:, k, :], bank[n % 2][:]).then_inc(wt_made, 1)

            for n in range(4):
                weight_out(n)
            exps(last, 0)
            exps(last, 1)
            for n in range(4, 8):
                weight_out(n)
            out_move(last, 0)
            out_move(last, 1)
            for n in range(8, 12):
                weight_out(n)

            def sqrt_(half, n):
                act.wait_ge(ln_var, n)
                act.activation(std[:, 4 * half:4 * half + 4], ve[:, 4 * half:4 * half + 4], ACT.Sqrt
                               ).then_inc(ln_std, 1)

            def x2t_out(half):
                for k in range(DC):
                    n = DC * half + k
                    act.wait_ge(x2t_filled, n + 1)
                    act.copy(xn2T[:, k, half * BANK:(half + 1) * BANK], bank[n % 2][:]).then_inc(x2t_made, 1)

            def q2_out(half, groups):
                for g in groups:
                    n = G * half + g
                    act.wait_ge(q2_filled, n + 1)
                    act.copy(q2T[:, g, half * BANK:(half + 1) * BANK], bank[5 + n % 2][:]).then_inc(q2_made, 1)

            def qn_out(i):
                act.wait_ge(qn_filled, i + 1)
                act.copy(q2n[:, i, :], bank[QN_BANK[i]][:]).then_inc(qn_made, 1)

            def z_out(i):
                act.wait_ge(z_filled, i + 1)
                if i >= 1:
                    act.wait_ge(y_filled, i)
                act.copy(zT[:].rearrange("p g c -> p (g c)"), bank[2][:]).then_inc(z_moved, 1)

            def exps2(i):
                act.wait_ge(l2_made, i + 1)
                act.activation(e2[:], lg2[:], ACT.Exp, scale=2.0 * INV).then_inc(e2_made, 1)

            def pbd_out(i):
                act.wait_ge(p2T_made, i + 1)
                if i >= 1:
                    act.wait_ge(z_filled, i)
                for n in range(4):
                    rows = slice(n * Q32, (n + 1) * Q32)
                    ins = act.copy(pbd[rows, :, n, :], p2T[rows, :, :])
                ins.then_inc(pbd_made, 1)

            def x3_out(half):
                for k in range(DC):
                    n = DC * half + k
                    act.wait_ge(x3_filled, n + 1)
                    b = bank[4 + k] if half else bank[5 + k % 2]
                    act.copy(xn3T[:, HI, k, half * BANK:(half + 1) * BANK], b[:]).then_inc(x3_hi, 1)

            sqrt_(0, 2)
            sqrt_(1, 3)
            x2t_out(0)
            q2_out(0, range(G))
            x2t_out(1)
            for i in range(4):
                qn_out(i)
            q2_out(1, (0,))
            exps2(0)
            q2_out(1, (1,))
            act.wait_ge(zero_made, 3)
            pbd_out(0)
            q2_out(1, (2, 3))
            for i in range(NT):
                if i < 4:
                    qn_out(4 + i)
                if i + 1 < NT:
                    exps2(i + 1)
                if i == 5:
                    sqrt_(0, 4)
                z_out(i)
                if i + 1 < NT:
                    pbd_out(i + 1)

            x3_out(0)

            def w_hi(n, par, w):
                act.wait_ge(fw_filled, 3 * n + w + 1)
                if w == 2 and not (isinstance(n, int) and n < 2):
                    act.wait_ge(d_done, n - 1)
                act.copy(wT[:, par, w, HI, :], bank[(3 * par + w) % 2][:]).then_inc(fw_hi, 1)

            def ffn_step(n, par, more=True, turned=False):
                if more:
                    w_hi(n + 1, 1 - par, 0)
                act.wait_ge(g_filled, n + 1)
                if not (isinstance(n, int) and n < 1):
                    act.wait_ge(h_made, n)
                act.activation(sg[:], bank[2][:], ACT.Silu, scale=WSCALE).then_inc(g_made, 1)
                if more:
                    w_hi(n + 1, 1 - par, 1)
                act.wait_ge(h_made, n + 1)
                act.copy(hT[:, par, HI, :], hf[:]).then_inc(h_hi, 1)
                if more:
                    w_hi(n + 1, 1 - par, 2)
                if turned:
                    x3_out(1)

            for w in range(3):
                w_hi(0, 0, w)
            sqrt_(1, 5)
            ffn_step(0, 0, turned=True)
            ffn_step(1, 1)
            with act.Fori(1, NJ - 1) as it:
                for u in range(2):
                    ffn_step(2 * it + u, u)
            ffn_step(2 * NJ - 2, 0)
            ffn_step(2 * NJ - 1, 1, more=False)

        @block.vector
        def _(dve):
            ln_n = [0]
            xh_n = [0]

            def link(ins):
                ln_n[0] += 1
                ins.then_inc(ln_step, 1)
                dve.wait_ge(ln_step, ln_n[0])

            def newton(r):
                link(dve.reciprocal(r0[:, r], std[:, r]))
                link(dve.tensor_tensor(r1[:, r], r0[:, r], r0[:, r], ALU.mult))
                link(dve.tensor_tensor(r2[:, r], r1[:, r], ve[:, r], ALU.mult))
                link(dve.tensor_scalar(r1[:, r], r2[:, r], -0.5, 1.5, ALU.mult, ALU.add))
                link(dve.tensor_tensor(rstd[:, r], r1[:, r], r0[:, r], ALU.mult))

            def layernorm(tiles, dst, slot, stds):
                lo, n = tiles[0], len(tiles)
                for i in tiles:
                    ins = dve.bn_stats(stats[:, i, :], xres[:, i, :])
                link(ins)
                for i in tiles:
                    ins = dve.bn_aggr(mv[:, i, :], stats[:, i, :])
                link(ins)
                r = slice(lo, lo + n)
                dve.tensor_scalar(ve[:, r], mv[:, r, 1], EPS, None, ALU.add).then_inc(ln_var, 1)
                dve.wait_ge(ln_std, stds)
                newton(r)
                for i in tiles:
                    dve.tensor_scalar(dst[:, i - slot, :], xres[:, i, :], mv[:, i, 0:1], rstd[:, i:i + 1],
                                      ALU.subtract, ALU.mult).then_inc(xh_made, 1)

            fill = 0
            for dst in (wkT, wvT):
                for k in range(DC):
                    dve.wait_ge(hi_made, fill + 1)
                    dve.tensor_tensor(dst[:, LO, k, :], bank[fill % 2][:], dst[:, HI, k, :].bitcast(F32), ALU.subtract
                                      ).then_inc(lo_made, 1)
                    fill += 1
            dve.wait_ge(hi_made, fill + 1)
            dve.tensor_tensor(ctailT[:, LO], bank[fill % 2][:].rearrange("p (k r) -> p k r", k=DC),
                              ctailT[:, HI].bitcast(F32), ALU.subtract).then_inc(lo_made, 1)
            fill += 1
            dve.wait_ge(hi_made, fill + 1)
            for g in range(G):
                ins = dve.scalar_tensor_tensor(ktail[:, LO, g, :], bank[fill % 2][:, g * NB:(g + 1) * NB],
                                               bkc[:, g:g + 1], ktail[:, HI, g, :].bitcast(F32), ALU.add, ALU.subtract)
            ins.then_inc(lo_made, 1)
            dve.wait_ge(x_in, 16)
            layernorm(range(NT), xres, 0, 1)
            for n in range(8):
                half, k = divmod(n, DC)
                dve.wait_ge(xt_filled, n + 1)
                dve.tensor_copy(xnT[:, k, half * BANK:(half + 1) * BANK], bank[6 + n % 2][:]).then_inc(xt_made, 1)

            def turn_lo(q, m):
                dve.wait_ge(hi_made, N0 + 8 * q + m + 1)
                dve.tensor_tensor(ctxT[:, LO, m, :], bank[m % 2][:], ctxT[:, HI, m, :].bitcast(F32), ALU.subtract
                                  ).then_inc(lo_made, 1)

            def keys_lo(q, g):
                dve.wait_ge(hi_made, N0 + 8 * q + 4 + g + 1)
                dve.scalar_tensor_tensor(kT[:, LO, g, :, 0:SF], bank[g % 2][:].rearrange("p (b s) -> p b s", b=2),
                                         bkc[:, g:g + 1], kT[:, HI, g, :, 0:SF].bitcast(F32),
                                         ALU.add, ALU.subtract).then_inc(lo_made, 1)

            def bias_in_(p, n):
                b, g = ORDER[n]
                dve.wait_ge(s_filled, 8 * p + n + 1)
                if g == 0:
                    dve.wait_ge(bm_made, 2 * p + b + 1)
                dve.tensor_tensor(Pn[:, b, g, 0:S], bank[4 + n % 2][:, 0:S], biasmask[:, b, g, :], ALU.add
                                  ).then_inc(s_biased, 1)

            def maxes(p, b):
                dve.wait_ge(s_biased, 8 * p + 6 + 2 * b)
                dve.tensor_reduce(nmax[:, b, :], Pn[:, b, :, 0:S], AX.X, ALU.max, negate=True).then_inc(max_made, 1)

            def norm(p, b):
                dve.wait_ge(exp_done, 8 * p + 4 * b + 4)
                dve.reciprocal(rsum[:, b, :], ssum[:, b, :]).then_inc(rs_made, 1)
                dve.wait_ge(rs_made, 2 * p + b + 1)
                for g in range(G):
                    ins = dve.tensor_scalar(Pn[:, b, g, 0:S], Pn[:, b, g, 0:S], rsum[:, b, g:g + 1], None, ALU.mult)
                ins.then_inc(norm_done, 1)

            def probs_out(p, n):
                dve.wait_ge(pt_filled, 6 * p + n + 1)
                dve.tensor_copy(PT[:, n // 3, n % 3, :], bank[(6, 5)[n % 2]][:]).then_inc(pt_made, 1)

            for m in range(DC):
                turn_lo(0, m)
            for g in range(G):
                keys_lo(0, g)
            for m in range(DC):
                turn_lo(1, m)

            def step(p, keys_more=True, turn_more=True):
                for n in range(8):
                    bias_in_(p, n)
                    if keys_more and n in (1, 3):
                        keys_lo(p + 1, n // 2)
                    if n == 5:
                        maxes(p, 0)
                if keys_more:
                    keys_lo(p + 1, 2)
                maxes(p, 1)
                if keys_more:
                    keys_lo(p + 1, 3)
                norm(p, 0)
                for n in range(6):
                    if turn_more and n >= 4:
                        turn_lo(p + 2, n - 4)
                    probs_out(p, n)
                    if n == 0:
                        norm(p, 1)
                if turn_more:
                    turn_lo(p + 2, 2)
                    turn_lo(p + 2, 3)

            with dve.Fori(0, NPAIR - 2) as p:
                step(p)
            step(NPAIR - 2, turn_more=False)
            step(NPAIR - 1, keys_more=False, turn_more=False)

            dve.wait_ge(m_filled, 1)
            dve.scalar_tensor_tensor(mbd[:], bank[3][:].rearrange("p (g c) -> p g c", g=G), INV,
                                     blockmask[:].unsqueeze(1).to_broadcast([P, G, P]), ALU.mult, ALU.mult
                                     ).then_inc(m_made, 1)

            dve.wait_ge(o_moved, 2 * NPAIR)
            for g in range(G):
                dve.tensor_scalar(oT2[:, g, :], oT2[:, g, :], bvc[:, g:g + 1], None, ALU.add).then_inc(ob_made, 1)

            def ln_start(half):
                lo = 4 * half
                for i in range(lo, lo + 4):
                    ins = dve.bn_aggr(mv[:, i, :], stats[:, i, :])
                link(ins)
                dve.tensor_scalar(ve[:, lo:lo + 4], mv[:, lo:lo + 4, 1], EPS, None, ALU.add).then_inc(ln_var, 1)

            def ln_end(half, dst, stds):
                lo = 4 * half
                dve.wait_ge(ln_std, stds)
                newton(slice(lo, lo + 4))
                for i in range(lo, lo + 4):
                    dve.tensor_scalar(dst[:, i - lo, :], xres[:, i, :], mv[:, i, 0:1], rstd[:, i:i + 1],
                                      ALU.subtract, ALU.mult).then_inc(xh_made, 1)

            def ln_tiles(half, dst, stds):
                ln_start(half)
                ln_end(half, dst, stds)

            for i in range(NT):
                dve.wait_ge(r1_filled, i + 1)
                dve.wait_ge(xb_made, i + 1)
                dve.tensor_tensor(xres[:, i, :], bank[2 + i % 2][:], xres[:, i, :], ALU.add).then_inc(x1_made, 1)
                dve.wait_ge(x1_made, i + 1)
                link(dve.bn_stats(stats[:, i, :], xres[:, i, :]))
                if i == 3:
                    ln_tiles(0, xh_first, 2)
            ln_tiles(1, wo_nat, 3)
            steps = [0]

            def link2(ins):
                steps[0] += 1
                ins.then_inc(dve2, 1)
                dve.wait_ge(dve2, steps[0])

            def hs(ap):
                return ap.unsqueeze(2).to_broadcast([P, H, Q32])

            def squares(i):
                dve.wait_ge(qn_made, i + 1)
                link2(dve.tensor_tensor(sq[:], q2n[:, i, :], q2n[:, i, :], ALU.mult))
                link2(dve.tensor_reduce(qsq[:], sq[:].rearrange("p (h d) -> p h d", h=H), AX.X, ALU.add))

            def norms(i):
                if i >= 2:
                    dve.wait_ge(l_filled, i - 1)
                dve.tensor_tensor(dq[:, i % 2], hs(qsq[:]), eye32[:].unsqueeze(1).to_broadcast([P, H, Q32]),
                                  ALU.mult).then_inc(dq_made, 1)
                link2(dve.tensor_scalar(hqsq[:, i % 2], qsq[:], -0.5, None, ALU.mult))

            def block2_out(i):
                dve.wait_ge(y_filled, i + 1)
                dve.wait_ge(xb_made, NT + i + 1)
                dve.tensor_tensor(xres[:, i, :], bank[3 + i % 2][:], xres[:, i, :], ALU.add).then_inc(x2_made, 1)
                dve.wait_ge(x2_made, i + 1)
                link(dve.bn_stats(stats[:, i, :], xres[:, i, :]))

            for i in range(2):
                squares(i)
                norms(i)
            for i in range(NT):
                dve.wait_ge(l_filled, i + 1)
                dve.tensor_tensor(lg[:], bank[i % 2][:].rearrange("p (h s) -> p h s", h=H), hs(hqsq[:, i % 2]),
                                  ALU.add).then_inc(l_read, 1)
                dve.wait_ge(l_read, i + 1)
                link2(dve.tensor_reduce(m2[:], lg[:], AX.X, ALU.max))
                dve.tensor_tensor(lg2[:], lg[:], hs(m2[:]), ALU.subtract).then_inc(l2_made, 1)
                if i + 2 < NT:
                    squares(i + 2)
                dve.wait_ge(e2_made, i + 1)
                link2(dve.tensor_reduce(s2[:], e2[:], AX.X, ALU.add))
                link2(dve.reciprocal(rs2[:], s2[:]))
                link2(dve.tensor_tensor(p2[:], e2[:], hs(rs2[:]), ALU.mult))
                if i:
                    dve.wait_ge(pbd_made, i)
                dve.transpose(p2T[:].rearrange("p h s -> p (h s)"), p2[:].rearrange("p h s -> p (h s)")
                              ).then_inc(p2T_made, 1)
                if i + 2 < NT:
                    norms(i + 2)
                if i >= 1:
                    block2_out(i - 1)
                if i == 5:
                    ln_start(0)
                if i == 6:
                    ln_end(0, xh3[:, 0:4], 4)
            block2_out(NT - 1)

            def x3_low(half):
                cols = slice(half * BANK, (half + 1) * BANK)
                for k in range(DC):
                    b = bank[4 + k] if half else bank[5 + k % 2]
                    dve.wait_ge(x3_hi, 4 * half + k + 1)
                    dve.tensor_tensor(xn3T[:, LO, k, cols], b[:], xn3T[:, HI, k, cols].bitcast(F32),
                                      ALU.subtract).then_inc(x3_lo, 1)

            x3_low(0)

            def w_lo(n, par, w):
                dve.wait_ge(fw_hi, 3 * n + w + 1)
                dve.tensor_tensor(wT[:, par, w, LO, :], bank[(3 * par + w) % 2][:], wT[:, par, w, HI, :].bitcast(F32),
                                  ALU.subtract).then_inc(fw_lo, 1)

            def ffn_step(n, par, more=True):
                if more:
                    w_lo(n + 1, 1 - par, 0)
                    w_lo(n + 1, 1 - par, 1)
                dve.wait_ge(u_filled, n + 1)
                dve.wait_ge(g_made, n + 1)
                if not (isinstance(n, int) and n < 1):
                    dve.wait_ge(h_lo, n)
                dve.scalar_tensor_tensor(hf[:], bank[3][:], WSCALE, sg[:], ALU.mult, ALU.mult).then_inc(h_made, 1)
                dve.wait_ge(h_hi, n + 1)
                dve.tensor_tensor(hT[:, par, LO, :], hf[:], hT[:, par, HI, :].bitcast(F32), ALU.subtract
                                  ).then_inc(h_lo, 1)
                if more:
                    w_lo(n + 1, 1 - par, 2)

            for w in range(3):
                w_lo(0, 0, w)
            ln_tiles(1, xh3[:, 4:8], 5)
            for half in range(2):
                base = half * NJ
                ffn_step(base, 0)
                if half == 0:
                    x3_low(1)
                ffn_step(base + 1, 1)
                with dve.Fori(1, NJ // 2 - 1) as it:
                    for u in range(2):
                        ffn_step(2 * it + (base + u), u)
                ffn_step(base + NJ - 2, 0)
                ffn_step(base + NJ - 1, 1, more=half == 0)
                dve.wait_ge(d_done, base + NJ)
                for t in range(4):
                    i = 4 * half + t
                    dve.scalar_tensor_tensor(xres[:, i, :], bank[4 + t][:], WSCALE, xres[:, i, :],
                                             ALU.mult, ALU.add).then_inc(x3_made, 1)


_INS = ["x", "ctx_1024", "mask_Bx1xSxS2_bf1", "L0_xattn_Wq", "L0_xattn_bq", "L0_xattn_Wk", "L0_xattn_bk",
        "L0_xattn_Wv", "L0_xattn_bv", "L0_xattn_Wo", "L0_xattn_bo", "L0_xattn_rel_emb", "L0_attn_q_weight",
        "L0_attn_v_weight", "L0_attn_out_w", "L0_attn_out_b", "L0_ffn_w_gate", "L0_ffn_w_up", "L0_ffn_w_down"]
_OUTS = [((32, 32, 512), "float32")]


def kernel(**inputs):
    import numpy as _np
    import concourse.bacc as _bacc
    from concourse.bass_utils import run_bass_kernel_spmd as _run

    nc = _bacc.Bacc("TRN2", target_bir_lowering=False, num_devices=1)
    arrays, args = {}, []
    for name in _INS:
        a = _np.ascontiguousarray(inputs[name])
        if a.dtype == _np.bool_:
            a = a.view(_np.uint8)
        arrays[f"in_{name}"] = a
        args.append(nc.dram_tensor(f"in_{name}", a.shape, mybir.dt.from_np(a.dtype), kind="ExternalInput").ap())
    for i, (shape, dtype) in enumerate(_OUTS):
        args.append(nc.dram_tensor(f"out_{i}", shape, mybir.dt.from_np(_np.dtype(dtype)), kind="ExternalOutput").ap())
    perceiver_kernel(nc, *args)
    r = _run(nc, [arrays], core_ids=[0])
    return r.results[0]["out_0"]
```

```python
import math
from contextlib import ExitStack

import concourse.bass as bass
from concourse import mybir

ALU = mybir.AluOpType
ACT = mybir.ActivationFunctionType
AX = mybir.AxisListType
F32 = mybir.dt.float32
F32R = mybir.dt.float32r
I32 = mybir.dt.int32
U8 = mybir.dt.uint8

P = 128
BANK = 512
Q32 = 32
HI, LO = 0, 1
PASSES = ((HI, HI), (HI, LO), (LO, HI))


def perceiver_kernel(
    nc, x, ctx_in, mask, wq, bq, wk, bk, wv, bv, wo, bo, rel_emb, q_weight, v_weight, out_w, out_b,
    w_gate, w_up, w_down, out,
):
    NB, T, D = x.shape
    S = ctx_in.shape[1]
    HD = q_weight.shape[2]
    H = q_weight.shape[1]
    HID = w_gate.shape[0]
    DC = D // P
    G = H * HD // P
    HG = P // HD
    TOK = NB * T
    NT = TOK // P
    SF = 2 * P
    SP_ = S + 1
    NPAIR = NB // 2
    NJ = HID // P
    MAX_REL = (rel_emb.shape[0] - 1) // 2
    RL = T + S - 1
    SCALE = float(HD) ** -0.5
    INV = 1.0 / math.sqrt(HD)
    WSCALE = 1.0 / 127.0
    EPS = 1e-5
    WK = HID * D // (NB // 2) // P
    W_EXACT = 256
    assert (T, HD, D, S, NB) == (Q32, Q32, BANK, SF + 1, Q32) and RL <= 288
    RLP = 288

    rel_dram = nc.dram_tensor("rel_scratch", (H, RLP), F32, kind="Internal").ap()

    with ExitStack() as keep:
        def sb(name, shape, dt=F32, stack=keep):
            return stack.enter_context(nc.sbuf_tensor(name, shape, dt))

        def sem(name):
            return keep.enter_context(nc.semaphore(name))

        bank = [keep.enter_context(nc.psum_tensor(f"bank{i}", [P, BANK], F32)) for i in range(8)]

        ident = sb("ident", [P, P])
        blockmask = sb("blockmask", [P, P])
        eye32 = sb("eye32", [P, Q32])
        halfneg = sb("halfneg", [P, P])
        xres = sb("xres", [P, NT, D])
        stats = sb("stats", [P, NT, 6])
        mv = sb("mv", [P, NT, 2])
        ve = sb("ve", [P, NT])
        std = sb("std", [P, NT])
        r0 = sb("r0", [P, NT])
        r1 = sb("r1", [P, NT])
        r2 = sb("r2", [P, NT])
        rstd = sb("rstd", [P, NT])
        bqs = sb("bqs", [P, G])
        bqc = sb("bqc", [P, G])
        bkc = sb("bkc", [P, G])
        bvc = sb("bvc", [P, G])

        wmax = sb("wmax", [P, NPAIR])
        wtop = sb("wtop", [P, 1])
        wtop1 = sb("wtop1", [1, 1])
        wide = sb("wide", [1, 1], I32)

        ob_bc = sb("ob_bc", [P, D])

        ph1 = ExitStack()
        wkT = sb("wkT", [P, 2, DC, D], F32R, ph1)
        wvT = sb("wvT", [P, 2, DC, D], F32R, ph1)
        ctxn = sb("ctxn", [P, 2, DC, D], F32, ph1)
        V = sb("V", [P, 2, 4, D], F32, ph1)
        oT = sb("oT", [P, G, T, NB], F32, ph1)
        relbias = sb("relbias", [P, G, S], F32, ph1)
        biasmask = sb("biasmask", [P, 2, G, S], F32, ph1)
        ctxT = sb("ctxT", [P, 2, DC, BANK], F32R, ph1)
        kT = sb("kT", [P, 2, G, 2, SP_], F32R, ph1)
        Pn = sb("Pn", [P, 2, G, SP_], F32, ph1)
        PT = sb("PT", [P, 2, 2, BANK], F32, ph1)
        vtailT = sb("vtailT", [P, NB, G], F32, ph1)
        ptdiag = sb("ptdiag", [P, 2, G, T], F32, ph1)
        otail = sb("otail", [P, 2, G, T], F32, ph1)
        qbd = sb("qbd", [P, 2, 2, G, P], F32R, ph1)
        qT = sb("qT", [P, G, TOK], F32, ph1)
        qtmp = sb("qtmp", [P, BANK], F32, ph1)
        ktail = sb("ktail", [P, 2, G, NB], F32R, ph1)
        masku = sb("masku", [P, 2, S], U8, ph1)
        maskf = sb("maskf", [P, 2, S], F32, ph1)
        nmax = sb("nmax", [P, 2, G], F32, ph1)
        w_scan = sb("w_scan", [P, 3, WK], I32, ph1)
        ssum = sb("ssum", [P, 2, G], F32, ph1)
        rsum = sb("rsum", [P, 2, G], F32, ph1)
        wk_nat = Pn[:].rearrange("p a g s -> p (a g s)")[:, 0:DC * D].rearrange("p (c n) -> p c n", c=DC)
        wv_nat = PT[:].rearrange("p a c s -> p (a c s)")[:, 0:DC * D].rearrange("p (c n) -> p c n", c=DC)
        wq_nat = biasmask[:].rearrange("p a g s -> p (a g s)")[:, 0:DC * D].rearrange("p (c n) -> p c n", c=DC)
        wqT = V[:, 1]
        maskf_rel = maskf[:].rearrange("p b s -> p (b s)")[0:H, 0:RLP]
        xnT = oT[:].rearrange("p g t b -> p g (t b)")
        vt_sb = ctxn[:, 1, 1]
        tkeys_sb = ctxn[:, 1, 2]
        tail_nat = ctxn[:, 1, 0]
        ctailT = ctxT[:, :, :, 0:P]
        ph1.close()

        ph2 = ExitStack()
        vw = sb("vw", [P, DC, D], F32, ph2)
        ow_nat = sb("ow_nat", [P, DC, D], F32, ph2)
        owT = sb("owT", [P, DC, D], F32, ph2)
        w2 = sb("w2", [P, G, D], F32, ph2)
        wo_nat = sb("wo_nat", [P, DC, D], F32, ph2)
        qw = sb("qw", [P, DC, D], F32, ph2)
        woT = sb("woT", [P, DC, D], F32, ph2)
        xh_first = sb("xh_first", [P, 4, D], F32, ph2)
        sb("over_oT", [P, G, TOK], F32, ph2)
        q2T = sb("q2T", [P, G, TOK], F32, ph2)
        q2n = sb("q2n", [P, NT, D], F32, ph2)
        mbd = sb("mbd", [P, G, P], F32, ph2)
        q2bd = sb("q2bd", [P, 2, G, 4, HG, Q32], F32, ph2)
        sq = sb("sq", [P, D], F32, ph2)
        qsq = sb("qsq", [P, H], F32, ph2)
        hqsq = sb("hqsq", [P, 2, H], F32, ph2)
        dq = sb("dq", [P, 2, H, Q32], F32, ph2)
        lg = sb("lg", [P, H, Q32], F32, ph2)
        lg2 = sb("lg2", [P, H, Q32], F32, ph2)
        e2 = sb("e2", [P, H, Q32], F32, ph2)
        p2 = sb("p2", [P, H, Q32], F32, ph2)
        p2T = sb("p2T", [P, H, Q32], F32, ph2)
        m2 = sb("m2", [P, H], F32, ph2)
        s2 = sb("s2", [P, H], F32, ph2)
        rs2 = sb("rs2", [P, H], F32, ph2)
        pbd = sb("pbd", [P, H, 4, Q32], F32, ph2)
        zT = sb("zT", [P, G, P], F32, ph2)
        w_int = sb("w_int", [P, 2, 3, D], I32, ph2)
        w_f = sb("w_f", [P, 2, 3, D], F32, ph2)
        ph2.close()
        oT2 = oT[:].rearrange("p g t b -> p g (t b)")
        xn2T = oT2
        xh = (xh_first, wo_nat)

        ph3 = ExitStack()
        wT = sb("wT", [P, 2, 3, 2, D], F32R, ph3)
        sb("over_w2", [P, G, D], F32, ph3)
        xn3T = sb("xn3T", [P, 2, DC, TOK], F32R, ph3)
        xh3 = sb("xh3", [P, NT, D], F32, ph3)
        sg = sb("sg", [P, BANK], F32, ph3)
        hf = sb("hf", [P, BANK], F32, ph3)
        hT = sb("hT", [P, 2, 2, BANK], F32R, ph3)
        ph3.close()

        bc_in = sem("bc_in")
        scan_in, scanned, wtop_made, wtop_filled, wide_made = (
            sem(n) for n in ("scan_in", "scanned", "wtop_made", "wtop_filled", "wide_made"))
        wk_in, wv_in, wq_in, x_in, tail_in, xr_in, bias_in = (
            sem(n) for n in ("wk_in", "wv_in", "wq_in", "x_in", "tail_in", "xr_in", "bias_in"))
        rel_in, rel_out, relb_in = (sem(n) for n in ("rel_in", "rel_out", "relb_in"))
        ctx_in_s = [sem(f"ctx_in{i}") for i in range(2)]
        mask_in = sem("mask_in")
        const_made = sem("const_made")
        passed = sem("passed")
        pool_step = sem("pool_step")
        split_filled, hi_made, lo_made = sem("split_filled"), sem("hi_made"), sem("lo_made")
        wq_filled, wq_made = sem("wq_filled"), sem("wq_made")
        xt_filled, xt_made = sem("xt_filled"), sem("xt_made")
        q_filled, q_made = sem("q_filled"), sem("q_made")
        vt_filled, vt_made = sem("vt_filled"), sem("vt_made")
        ptdiag_made, tail_filled, otail_made, tail_added = (
            sem(n) for n in ("ptdiag_made", "tail_filled", "otail_made", "tail_added"))
        bq_made = sem("bq_made")
        v_filled, v_made = sem("v_filled"), sem("v_made")
        s_filled, s_biased = sem("s_filled"), sem("s_biased")
        max_made, exp_done, rs_made, norm_done = (
            sem(n) for n in ("max_made", "exp_done", "rs_made", "norm_done"))
        pt_filled, pt_made = sem("pt_filled"), sem("pt_made")
        o_filled, o_moved = sem("o_filled"), sem("o_moved")
        qbd_made, bm_made, ktail_made = sem("qbd_made"), sem("bm_made"), sem("ktail_made")
        ln_step, ln_var, ln_std, xh_made, xh_used = (
            sem(n) for n in ("ln_step", "ln_var", "ln_std", "xh_made", "xh_used"))
        ob_made = sem("ob_made")
        w_b_in = sem("w_b_in")
        w_in2 = sem("w_in2")
        ow_in = sem("ow_in")
        wt_filled, wt_made = sem("wt_filled"), sem("wt_made")
        m_filled, m_made = sem("m_filled"), sem("m_made")
        r1_filled, x1_made = sem("r1_filled"), sem("x1_made")
        xb_made = sem("xb_made")
        x2t_filled, x2t_made = sem("x2t_filled"), sem("x2t_made")
        q2_filled, q2_made = sem("q2_filled"), sem("q2_made")
        qn_filled, qn_made = sem("qn_filled"), sem("qn_made")
        dq_made, l_filled, l_read, e2_made, p2T_made, pbd_made = (
            sem(n) for n in ("dq_made", "l_filled", "l_read", "e2_made", "p2T_made", "pbd_made"))
        l2_made = sem("l2_made")
        q2bd_made = sem("q2bd_made")
        z_filled, z_moved = sem("z_filled"), sem("z_moved")
        dve2 = sem("dve2")
        y_filled, x2_made = sem("y_filled"), sem("x2_made")
        x3_filled, x3_hi, x3_lo = sem("x3_filled"), sem("x3_hi"), sem("x3_lo")
        wi_in = [sem(f"wi_in{i}") for i in range(2)]
        wf_made = sem("wf_made")
        fw_filled, fw_hi, fw_lo = sem("fw_filled"), sem("fw_hi"), sem("fw_lo")
        g_filled, g_made = sem("g_filled"), sem("g_made")
        u_filled, h_made, h_hi, h_lo = sem("u_filled"), sem("h_made"), sem("h_hi"), sem("h_lo")
        d_done, acc_filled, x3_made = sem("d_done"), sem("acc_filled"), sem("x3_made")
        out_stored = sem("out_stored")
        zero_made = sem("zero_made")

        N0 = DC + DC + 2
        F_CTX0, F_WV, F_TAIL = DC, 3 * DC, 4 * DC
        QN_BANK = (4, 7, 4, 7, 6, 7, 6, 7)
        O_BANK = (7, 2)
        KEYS_AFTER = (1, 3, 6, 7)
        ORDER = ((0, 0), (1, 0), (0, 1), (1, 1), (0, 2), (0, 3), (1, 2), (1, 3))
        block = keep.enter_context(nc.Block())

        def at(q):
            return F_CTX0 if isinstance(q, int) and q == 0 else N0 + 8 * q

        def wait_alone(eng, s, value):
            eng.wait_ge(s, value)
            eng.sem_inc(passed, 1)

        x_bt = x.rearrange("b t m -> (b t) m").rearrange("(i p) m -> p i m", p=P)

        @block.sync
        def _(sp):
            def w_nat(w):
                return w.rearrange("(c p) n -> p c n", p=P)

            def load_bias(src):
                sp.dma_start(ob_bc[:], src.rearrange("(o n) -> o n", o=1).to_broadcast([P, D])).then_inc(bc_in, 16)

            def load_ctx(q, par):
                for b in range(2):
                    sp.dma_start(ctxn[:, par, 2 * b:2 * b + 2, :],
                                 ctx_in[2 * q + b, 0:SF, :].rearrange("(c p) m -> p c m", p=P)
                                 ).then_inc(ctx_in_s[par], 16)

            def load_mask(q):
                for b in range(2):
                    for h in range(HG):
                        sp.dma_start(masku[h * T:(h + 1) * T, b, :], mask[2 * q + b, 0, :, :]
                                     ).then_inc(mask_in, 16)

            sp.dma_start(wk_nat, w_nat(wk)).then_inc(wk_in, 16)
            load_ctx(0, 0)
            sp.dma_start(wv_nat, w_nat(wv)).then_inc(wv_in, 16)
            sp.dma_start(xres[:], x_bt).then_inc(x_in, 16)
            sp.dma_start(wq_nat, w_nat(wq)).then_inc(wq_in, 16)
            sp.wait_ge(zero_made, 1)
            sp.dma_start(tail_nat[0:NB, :], ctx_in[:, SF, :]).then_inc(tail_in, 16)
            load_mask(0)
            load_bias(bo)
            sp.wait_ge(rel_out, 16)
            for t in range(T):
                src = bass.AP(rel_dram.tensor, T - 1 - t, [[RLP, HG], [HG * RLP, G], [1, S]])
                sp.dma_start(relbias[t:P:T, :, :], src).then_inc(relb_in, 16)
            sp.wait_ge(xt_filled, 8)
            for i in range(NT):
                for t in range(4):
                    sp.dma_start(xres[t * NB:(t + 1) * NB, i, :], x[:, 4 * i + t, :]).then_inc(xr_in, 16)
            sp.wait_ge(split_filled, F_TAIL + 2)
            sp.wait_ge(vt_filled, 3)
            load_ctx(1, 1)

            def next_ctx(q, par):
                wait_alone(sp, split_filled, N0 + 8 * q + 4)
                load_ctx(q + 2, par)

            def load_scan(q):
                for k, w in enumerate((w_gate, w_up, w_down)):
                    flat = w.rearrange("a b -> (a b)").rearrange("(s p k) -> p s k", p=P, k=WK)
                    sp.dma_start(w_scan[:, k:k + 1, :], flat[:, bass.ds(q, 1), :]).then_inc(scan_in, 16)

            def step(p, par, ctx_more):
                wait_alone(sp, bm_made, 2 * p + 2)
                load_mask(p + 1)
                if ctx_more:
                    next_ctx(p + 2, par)
                wait_alone(sp, scanned, p + 1)
                load_scan(p + 1)

            load_scan(0)
            next_ctx(0, 0)
            next_ctx(1, 1)
            with sp.Fori(0, (NPAIR - 4) // 2) as it:
                for u in range(2):
                    step(2 * it + u, u, True)
            for p in range(NPAIR - 4, NPAIR - 1):
                if p == NPAIR - 2:
                    sp.wait_ge(split_filled, N0 + 8 * (NPAIR - 1) + 4)
                    sp.dma_start(wo_nat[:], w_nat(wo)).then_inc(w_b_in, 16)
                    sp.dma_start(qw[:], q_weight.rearrange("(c p) h d -> p c (h d)", p=P)).then_inc(w_in2, 16)
                step(p, p % 2, False)

            last = NPAIR - 1
            sp.wait_ge(split_filled, N0 + 8 * last + 8)
            sp.dma_start(vw[:], v_weight.rearrange("(c p) h d -> p c (h d)", p=P)).then_inc(w_in2, 16)
            sp.dma_start(ow_nat[:], w_nat(out_w)).then_inc(ow_in, 16)

            sp.wait_ge(xb_made, NT)
            load_bias(out_b)

            sp.wait_ge(o_filled, 2 * NPAIR)
            def load_w(j, par):
                sp.dma_start(w_int[:, par, 0, :], w_gate[bass.ds(j * P, P), :]).then_inc(wi_in[par], 16)
                sp.dma_start(w_int[:, par, 1, :], w_up[bass.ds(j * P, P), :]).then_inc(wi_in[par], 16)
                sp.dma_start(w_int[:, par, 2, :].rearrange("p (c k) -> p c k", c=DC),
                             w_down[:, bass.ds(j * P, P)].rearrange("(c p) k -> p c k", p=P)
                             ).then_inc(wi_in[par], 16)

            for half in range(2):
                for j in range(2):
                    if half:
                        sp.wait_ge(wf_made, half * NJ + j - 1)
                    load_w(j, j)
                with sp.Fori(0, (NJ - 2) // 2) as it:
                    for u in range(2):
                        wait_alone(sp, wf_made, 2 * it + (half * NJ + u + 1))
                        load_w(2 * it + (u + 2), u)
            for half in range(2):
                for i in range(4):
                    k = 4 * half + i
                    sp.wait_ge(x3_made, k + 1)
                    for t in range(4):
                        sp.dma_start(out[:, 4 * k + t, :], xres[t * NB:(t + 1) * NB, k, :]
                                     ).then_inc(out_stored, 16)
            sp.wait_ge(out_stored, 16 * 4 * NT)

        @block.gpsimd
        def _(pool):
            step_n = [0]

            def link(ins):
                step_n[0] += 1
                ins.then_inc(pool_step, 1)
                pool.wait_ge(pool_step, step_n[0])

            pool.memset(tail_nat, 0.0).then_inc(zero_made, 1)
            link(pool.memset(ident[:], 0.0))
            link(pool.memset(blockmask[:], 1.0))
            link(pool.memset(eye32[:], 0.0))
            pool.affine_select(out=ident[:], in_=ident[:], compare_op=ALU.not_equal, fill=1.0, base=0,
                               pattern=[[-1, P]], channel_multiplier=1).then_inc(const_made, 1)
            bm3 = blockmask[:].rearrange("p (h d) -> p h d", h=HG)
            link(pool.affine_select(out=bm3, in_=bm3, compare_op=ALU.is_ge, fill=0.0, base=0,
                                    pattern=[[-Q32, HG], [0, Q32]], channel_multiplier=1))
            link(pool.affine_select(out=bm3, in_=bm3, compare_op=ALU.is_ge, fill=0.0, base=Q32 - 1,
                                    pattern=[[Q32, HG], [0, Q32]], channel_multiplier=-1))
            for k in range(HG):
                link(pool.affine_select(out=eye32[:], in_=eye32[:], compare_op=ALU.not_equal, fill=1.0,
                                        base=-Q32 * k, pattern=[[-1, Q32]], channel_multiplier=1))
            pool.tensor_scalar(halfneg[:], blockmask[:], -0.5, None, ALU.mult).then_inc(const_made, 1)

            with nc.allow_non_contiguous_dma(reason="small bias rows, once"):
                for name_ap, w in ((bqc, bq), (bkc, bk), (bvc, bv)):
                    pool.dma_start(name_ap[:], w.rearrange("(g p) -> p g", p=P)).then_inc(bias_in, 16)
                rel_sb = qtmp[0:H, 0:RLP]
                pool.dma_start(rel_sb, rel_emb[MAX_REL + T - RLP:MAX_REL + T, :].rearrange("i h -> h i")
                               ).then_inc(rel_in, 16)
            pool.wait_ge(rel_in, 16)
            link(pool.tensor_copy(maskf_rel, rel_sb[:, ::-1]))
            pool.dma_start(rel_dram, maskf_rel).then_inc(rel_out, 16)
            pool.wait_ge(bias_in, 48)
            pool.tensor_scalar(bqs[:], bqc[:], SCALE, None, ALU.mult).then_inc(bq_made, 1)

            for part in range(2):
                pool.memset(kT[:, part, :, :, S:SP_].bitcast(F32), 0.0)

            hmask = blockmask[:].rearrange("p (h d) -> p h d", h=HG)

            def block_queries(q, first):
                if not first:
                    pool.wait_ge(s_filled, 8 * q)
                for b in range(2):
                    t3 = qtmp[:].rearrange("p (g h t) -> p g h t", g=G, h=HG)
                    for g in range(G):
                        src = qT[:, g, bass.ds((2 * q + b) * T, T)].unsqueeze(1).to_broadcast([P, HG, T])
                        ins = pool.tensor_tensor(t3[:, g], src, hmask, ALU.mult)
                    ins.then_inc(pool_step, 1)
                    wait_alone(pool, pool_step, step_n[0] + 6 * q + 3 * b + 1)
                    qf = qtmp[:].rearrange("p (g c) -> p g c", g=G)
                    pool.tensor_copy(qbd[:, HI, b], qf).then_inc(pool_step, 1)
                    wait_alone(pool, pool_step, step_n[0] + 6 * q + 3 * b + 2)
                    ins = pool.tensor_tensor(qbd[:, LO, b], qf, qbd[:, HI, b].bitcast(F32), ALU.subtract)
                    ins.then_inc(pool_step, 1)
                    pool.wait_ge(pool_step, step_n[0] + 6 * q + 3 * b + 3)
                for part in range(2):
                    ins = pool.tensor_copy(kT[:, part, :, :, SF],
                                           ktail[:, part, :, bass.ds(2 * q, 2)])
                ins.then_inc(qbd_made, 1)

            def bias_and_mask(q, first):
                wait_alone(pool, mask_in, 16 * 2 * HG * (q + 1))
                pool.tensor_scalar(maskf[:], masku[:], -1.0, 3.0e38, ALU.add, ALU.mult).then_inc(ktail_made, 1)
                wait_alone(pool, ktail_made, 2 * q + 1)
                pool.tensor_scalar(maskf[:], maskf[:], 4.0, None, ALU.mult).then_inc(ktail_made, 1)
                wait_alone(pool, ktail_made, 2 * q + 2)
                for b in range(2):
                    if not first:
                        pool.wait_ge(s_biased, 8 * q)
                    pool.tensor_tensor(biasmask[:, b], relbias[:],
                                       maskf[:, b].unsqueeze(1).to_broadcast([P, G, S]), ALU.add
                                       ).then_inc(bm_made, 1)

            def add_tail(p, p1):
                wait_alone(pool, otail_made, p1)
                wait_alone(pool, o_moved, 2 * p1)
                pair = oT[:, :, :, bass.ds(2 * p, 2)]
                pool.tensor_tensor(pair, pair, otail[:].rearrange("p b g t -> p g t b"), ALU.add
                                   ).then_inc(tail_added, 1)

            pool.wait_ge(split_filled, F_TAIL)
            pool.wait_ge(relb_in, 16 * T)
            pool.wait_ge(wq_filled, DC)
            bias_and_mask(0, True)
            pool.wait_ge(q_made, G)
            pool.wait_ge(lo_made, N0 + 8)
            block_queries(0, True)
            with pool.Fori(1, NPAIR) as q:
                block_queries(q, False)
                bias_and_mask(q, False)
                add_tail(q - 1, q)

            for i in range(NT):
                if i == 0:
                    pool.wait_ge(xr_in, 16 * 4 * NT)
                    pool.wait_ge(bc_in, 16)
                pool.tensor_tensor(xres[:, i, :], xres[:, i, :], ob_bc[:], ALU.add).then_inc(xb_made, 1)
            add_tail(NPAIR - 1, NPAIR)
            pool.memset(q2bd[:], 0.0).then_inc(zero_made, 1)
            pool.memset(pbd[:], 0.0).then_inc(zero_made, 1)
            pool.wait_ge(zero_made, 3)
            for i in range(NT):
                pool.wait_ge(q2_made, 4 * (i // 4) + 4)
                if i >= 2:
                    pool.wait_ge(l_filled, i - 1)
                src = q2T[:, :, i * P:(i + 1) * P].rearrange("p g (n s) -> p g n s", n=4)
                for h in range(HG):
                    ins = pool.tensor_copy(q2bd[h * Q32:(h + 1) * Q32, i % 2, :, :, h, :],
                                           src[h * Q32:(h + 1) * Q32])
                ins.then_inc(q2bd_made, 1)
                if i == 3:
                    pool.wait_ge(xh_made, 2 * NT)
                    pool.wait_ge(bc_in, 32)
                    pool.wait_ge(q2bd_made, 4)
                    for j in range(NT):
                        pool.tensor_tensor(xres[:, j, :], xres[:, j, :], ob_bc[:], ALU.add).then_inc(xb_made, 1)
                    pool.wait_ge(xb_made, 2 * NT)

            pool.wait_ge(q2bd_made, NT)
            def convert(n, j2, half, par):
                pool.wait_ge(wi_in[par], 48 * j2 + 48 * (half * NJ // 2 + 1))
                if not (isinstance(n, int) and n < 2):
                    wait_alone(pool, fw_filled, 3 * n - 3)
                pool.tensor_copy(w_f[:, par], w_int[:, par]).then_inc(wf_made, 1)

            for half in range(2):
                for j in range(2):
                    convert(half * NJ + j, 0, half, j)
                with pool.Fori(0, (NJ - 2) // 2) as it:
                    for u in range(2):
                        convert(2 * it + (half * NJ + 2 + u), it + 1, half, u)

        @block.tensor
        def _(pe):
            def mm3(dst, lhs, rhs, first, last, passes=PASSES):
                for n, (a, b) in enumerate(passes):
                    ins = pe.matmul(dst, lhs(a), rhs(b), start=first and n == 0, stop=last and n == len(passes) - 1)
                return ins

            def turn(q, par, m):
                pe.wait_ge(lo_made, at(q) + m - 1)
                for i in range(4):
                    ins = pe.transpose(bank[m % 2][:, i * P:(i + 1) * P],
                                       ctxn[:, par, i, m * P:(m + 1) * P], ident[:])
                ins.then_inc(split_filled, 1)

            def keys(q, g):
                pe.wait_ge(lo_made, at(q) + 4 + max(g - 1, 0))
                for m in range(DC):
                    ins = mm3(bank[g % 2][:], lambda a: wkT[:, a, m, g * P:(g + 1) * P],
                              lambda b: ctxT[:, b, m, :], m == 0, m == DC - 1)
                ins.then_inc(split_filled, 1)

            def values(q, i, first):
                if not (first and i < 2):
                    pe.wait_ge(v_made, 4 * q + i - 1)
                for m in range(DC):
                    ins = mm3(bank[2 + i % 2][:], lambda a: ctxT[:, a, m, i * P:(i + 1) * P],
                              lambda b: wvT[:, b, m, :], m == 0, m == DC - 1)
                ins.then_inc(v_filled, 1)

            def scores(p, n, first):
                b, g = ORDER[n]
                if n == 0:
                    pe.wait_ge(lo_made, N0 + 8 * p + 8)
                    pe.wait_ge(qbd_made, p + 1)
                    if not first:
                        pe.wait_ge(otail_made, p)
                if not (first and n < 2):
                    pe.wait_ge(s_biased, 8 * p + n - 1)
                ins = mm3(bank[4 + n % 2][:, 0:SP_], lambda a: qbd[:, a, b, g, :],
                          lambda c: kT[:, c, g, b, :], True, True)
                ins.then_inc(s_filled, 1)

            def probs_turn(p, b, c):
                n = 2 * b + c
                if c == 0:
                    pe.wait_ge(norm_done, 2 * p + b + 1)
                if n >= 2:
                    pe.wait_ge(pt_made, 4 * p + n - 1)
                for g in range(G):
                    ins = pe.transpose(bank[(6, 5)[n % 2]][:, g * P:(g + 1) * P], Pn[:, b, g, c * P:(c + 1) * P],
                                       ident[:])
                ins.then_inc(pt_filled, 1)

            def attend(p, par, b, first=False, more=True):
                pe.wait_ge(pt_made, 4 * p + 2 * b + 2)
                if b == 0:
                    pe.wait_ge(v_made, 4 * p + 4)
                else:
                    pe.wait_ge(v_made, 4 * p + (8 if more else 4))
                if b == 0 and not first:
                    pe.wait_ge(o_moved, 2 * p)
                for g in range(G):
                    cols = slice(g * P, (g + 1) * P)
                    for c in range(2):
                        ins = pe.matmul(bank[O_BANK[b]][:, cols], V[:, par, 2 * b + c, cols], PT[:, b, c, cols],
                                        start=c == 0, stop=c == 1)
                ins.then_inc(o_filled, 1)

            def tail(p):
                pe.wait_ge(ptdiag_made, p + 1)
                pe.matmul(bank[4][:, 0:2 * G * T], blockmask[:], ptdiag[:].rearrange("p b g t -> p (b g t)"),
                          start=True, stop=True).then_inc(tail_filled, 1)

            def ctx_wait(q, par):
                pe.wait_ge(ctx_in_s[par], 16 * q + 32 - 16 * par)

            def step(p, par, first=False, more=True):
                q = p + 1
                for n in range(8):
                    scores(p, n, first)
                    if n in KEYS_AFTER:
                        keys(q, KEYS_AFTER.index(n))
                if not first:
                    pe.wait_ge(o_moved, 2 * p)
                for i in range(4):
                    values(q, i, False)
                    probs_turn(p, i // 2, i % 2)
                if more:
                    ctx_wait(p + 2, par)
                    turn(p + 2, par, 0)
                tail(p)
                if more:
                    turn(p + 2, par, 1)
                attend(p, par, 0, first)
                if more:
                    turn(p + 2, par, 2)
                attend(p, par, 1)
                if more:
                    turn(p + 2, par, 3)

            pe.wait_ge(const_made, 2)

            def turn_rows(fill, nat, cols_of):
                if fill >= 2:
                    pe.wait_ge(lo_made, fill - 1)
                for c in range(DC):
                    ins = pe.transpose(bank[fill % 2][:, c * P:(c + 1) * P], cols_of(nat, c), ident[:])
                ins.then_inc(split_filled, 1)

            pe.wait_ge(wk_in, 16)
            for k in range(DC):
                turn_rows(k, wk_nat, lambda nat, c: nat[:, c, k * P:(k + 1) * P])
            ctx_wait(0, 0)
            for m in range(DC):
                turn(0, 0, m)
            for g in range(G):
                keys(0, g)
            pe.wait_ge(wv_in, 16)
            for k in range(DC):
                turn_rows(F_WV + k, wv_nat, lambda nat, c: nat[:, c, k * P:(k + 1) * P])
            pe.wait_ge(lo_made, F_TAIL)
            for i in range(4):
                values(0, i, True)
            pe.wait_ge(wq_in, 16)
            for k in range(DC):
                if k >= 2:
                    pe.wait_ge(wq_made, k - 1)
                for c in range(DC):
                    ins = pe.transpose(bank[4 + k % 2][:, c * P:(c + 1) * P], wq_nat[:, c, k * P:(k + 1) * P], ident[:])
                ins.then_inc(wq_filled, 1)
            pe.wait_ge(tail_in, 16)
            turn_rows(F_TAIL, tail_nat, lambda nat, c: nat[:, c * P:(c + 1) * P])
            for n in range(8):
                half, k = divmod(n, DC)
                pe.wait_ge(xh_made, 4 * half + 4)
                if n >= 2:
                    pe.wait_ge(xt_made, n - 1)
                for c in range(4):
                    ins = pe.transpose(bank[6 + n % 2][:, c * P:(c + 1) * P],
                                       xres[:, 4 * half + c, k * P:(k + 1) * P], ident[:])
                ins.then_inc(xt_filled, 1)
            pe.wait_ge(lo_made, F_TAIL + 1)
            pe.wait_ge(wq_made, DC)
            for w, b in ((wvT, 4), (wkT, 5)):
                for k in range(DC):
                    ins = mm3(bank[b][:], lambda a: ctailT[:, a, k, :], lambda c: w[:, c, k, :], k == 0, k == DC - 1)
                ins.then_inc(vt_filled, 1)
            pe.wait_ge(v_made, 4)

            def queries(n):
                half, g = divmod(n, G)
                pe.wait_ge(xt_made, 4 * half + 4)
                if n >= 2:
                    pe.wait_ge(q_made, n - 1)
                for k in range(DC):
                    ins = pe.matmul(bank[2 + n % 2][:], wqT[:, k, g * P:(g + 1) * P],
                                    xnT[:, k, half * BANK:(half + 1) * BANK], start=k == 0, stop=k == DC - 1)
                ins.then_inc(q_filled, 1)

            queries(0)
            pe.wait_ge(vt_made, 2)
            turn_rows(F_TAIL + 1, tkeys_sb, lambda nat, c: nat[:, c * P:(c + 1) * P])
            for g in range(G):
                ins = pe.transpose(bank[4][:, g * P:(g + 1) * P], vt_sb[:, g * P:(g + 1) * P], ident[:])
            ins.then_inc(vt_filled, 1)
            for n in range(1, 8):
                queries(n)
            pe.wait_ge(q_made, 8)
            ctx_wait(1, 1)
            for m in range(DC):
                turn(1, 1, m)
            step(0, 0, first=True)
            with pe.Fori(0, (NPAIR - 4) // 2) as it:
                for u in range(2):
                    step(2 * it + 1 + u, (1 + u) % 2)
            step(NPAIR - 3, 1)
            step(NPAIR - 2, 0, more=False)
            last = NPAIR - 1

            def turn_weight(n):
                nat, k = (wo_nat, ow_nat)[n // DC], n % DC
                if k == 0:
                    pe.wait_ge((w_b_in, ow_in)[n // DC], 16)
                if n >= 2:
                    pe.wait_ge(wt_made, n - 1)
                for c in range(DC):
                    ins = pe.transpose(bank[n % 2][:, c * P:(c + 1) * P], nat[:, c, k * P:(k + 1) * P], ident[:])
                ins.then_inc(wt_filled, 1)

            for g in range(G):
                scores(last, 2 * g, False)
                scores(last, 2 * g + 1, False)
                turn_weight(g)
            pe.wait_ge(w_in2, 32)
            for g in range(G):
                cols = slice(g * P, (g + 1) * P)
                for k in range(DC):
                    ins = pe.matmul(bank[3][:, cols], vw[:, k, cols], qw[:, k, cols], start=k == 0, stop=k == DC - 1)
            ins.then_inc(m_filled, 1)
            for n in range(4):
                probs_turn(last, n // 2, n % 2)
                turn_weight(4 + n)
            tail(last)
            attend(last, 1, 0)
            attend(last, 1, 1, more=False)
            pe.wait_ge(wtop_made, 1)
            pe.transpose(bank[6][0:1, 0:P], wtop[:], ident[:]).then_inc(wtop_filled, 1)
            pe.wait_ge(m_made, 1)
            for g in range(G):
                pe.wait_ge(wt_made, 2 * DC + max(g - 1, 0))
                ins = pe.matmul(bank[g % 2][:], mbd[:, g, :], owT[:, g, :], start=True, stop=True)
                ins.then_inc(wt_filled, 1)

            pe.wait_ge(ob_made, 4)
            for i in range(NT):
                if i >= 2:
                    pe.wait_ge(x1_made, i - 1)
                for k in range(DC):
                    ins = pe.matmul(bank[2 + i % 2][:], oT2[:, k, i * P:(i + 1) * P], woT[:, k, :],
                                    start=k == 0, stop=k == DC - 1)
                ins.then_inc(r1_filled, 1)

            pe.wait_ge(wt_made, 3 * DC)

            def turn_x2(half):
                pe.wait_ge(xh_made, 8 + 4 * half + 4)
                for k in range(DC):
                    n = DC * half + k
                    if n >= 2:
                        pe.wait_ge(x2t_made, n - 1)
                    for c in range(4):
                        ins = pe.transpose(bank[n % 2][:, c * P:(c + 1) * P],
                                           xh[half][:, c, k * P:(k + 1) * P], ident[:])
                    ins.then_inc(x2t_filled, 1)

            def queries2(half, groups):
                pe.wait_ge(x2t_made, 4 * half + 4)
                for g in groups:
                    n = G * half + g
                    if n >= 2:
                        pe.wait_ge(q2_made, n - 1)
                    for k in range(DC):
                        ins = pe.matmul(bank[5 + n % 2][:], qw[:, k, g * P:(g + 1) * P],
                                        xn2T[:, k, half * BANK:(half + 1) * BANK], start=k == 0, stop=k == DC - 1)
                    ins.then_inc(q2_filled, 1)

            def turn_q2(i):
                pe.wait_ge(q2_made, 4 * (i // 4) + 4)
                if i >= 2:
                    pe.wait_ge(qn_made, i - 1)
                for g in range(G):
                    ins = pe.transpose(bank[QN_BANK[i]][:, g * P:(g + 1) * P],
                                       q2T[:, g, i * P:(i + 1) * P], ident[:])
                ins.then_inc(qn_filled, 1)

            def logits2(i):
                pe.wait_ge(dq_made, i + 1)
                pe.wait_ge(q2bd_made, i + 1)
                if i == 0:
                    pe.wait_ge(x2t_made, 8)
                if i >= 2:
                    pe.wait_ge(l_read, i - 1)
                L = bank[i % 2]
                pe.matmul(L[:], halfneg[:], dq[:, i % 2].rearrange("p h s -> p (h s)"), start=True, stop=False,
                          skip_group_check=True)
                for n in range(4):
                    for g in range(G):
                        ins = pe.matmul(L[n * Q32:(n + 1) * Q32, g * P:(g + 1) * P],
                                        q2T[:, g, i * P + n * Q32:i * P + (n + 1) * Q32],
                                        q2bd[:, i % 2, g, n].rearrange("p h s -> p (h s)"),
                                        start=False, stop=g == G - 1, skip_group_check=True)
                ins.then_inc(l_filled, 1)

            def attend2(i):
                pe.wait_ge(pbd_made, i + 1)
                if i >= 1:
                    pe.wait_ge(z_moved, i)
                for h in range(H):
                    g, r = divmod(h, HG)
                    ins = pe.matmul(bank[2][r * Q32:(r + 1) * Q32, g * P:(g + 1) * P],
                                    q2n[:, i, h * HD:(h + 1) * HD], pbd[:, h].rearrange("p n t -> p (n t)"),
                                    start=True, stop=True, skip_group_check=True)
                ins.then_inc(z_filled, 1)

            def project2(i):
                pe.wait_ge(z_moved, i + 1)
                if i == 0:
                    pe.wait_ge(qn_made, 4)
                if i >= 2:
                    pe.wait_ge(x2_made, i - 1)
                for g in range(G):
                    ins = pe.matmul(bank[3 + i % 2][:], zT[:, g, :], w2[:, g, :], start=g == 0, stop=g == G - 1)
                ins.then_inc(y_filled, 1)

            turn_x2(0)
            queries2(0, range(G))
            turn_x2(1)
            for i in range(4):
                turn_q2(i)
            queries2(1, (0, 1))
            logits2(0)
            logits2(1)
            queries2(1, (2, 3))
            for i in range(NT):
                attend2(i)
                if i < 4:
                    turn_q2(4 + i)
                if i + 2 < NT:
                    logits2(i + 2)
                if i < NT - 1:
                    project2(i)

            def turn_x3(half):
                pe.wait_ge(xh_made, 16 + 4 * half + 4)
                if half == 0:
                    pe.wait_ge(qn_made, NT)
                else:
                    pe.wait_ge(x2_made, NT)
                    pe.wait_ge(x3_lo, 4)
                for k in range(DC):
                    if half == 0 and k >= 2:
                        pe.wait_ge(x3_lo, k - 1)
                    b = bank[4 + k] if half else bank[5 + k % 2]
                    for c in range(4):
                        ins = pe.transpose(b[:, c * P:(c + 1) * P], xh3[:, 4 * half + c, k * P:(k + 1) * P], ident[:])
                    ins.then_inc(x3_filled, 1)

            def weights(n, par, w, first=False):
                if w == 0:
                    pe.wait_ge(wf_made, n + 1)
                k = 3 * n + w
                if not (isinstance(n, int) and k < 2):
                    pe.wait_ge(fw_lo, k - 1)
                for c in range(DC):
                    ins = pe.transpose(bank[(3 * par + w) % 2][:, c * P:(c + 1) * P],
                                       w_f[:, par, w, c * P:(c + 1) * P], ident[:])
                ins.then_inc(fw_filled, 1)

            def feed_forward(lhs_w, rhs_w):
                def gate_up(n, par, half, w, filled, freed):
                    pe.wait_ge(fw_lo, 3 * n + w + 1)
                    if not (isinstance(n, int) and n < 1):
                        pe.wait_ge(freed, n)
                    for k in range(DC):
                        ins = mm3(bank[2 + w][:], lambda a: wT[:, par, w, a, k * P:(k + 1) * P],
                                  lambda b: xn3T[:, b, k, half * BANK:(half + 1) * BANK], k == 0, k == DC - 1,
                                  lhs_w)
                    ins.then_inc(filled, 1)

                def down(n, par, first, last):
                    pe.wait_ge(h_lo, n + 1)
                    pe.wait_ge(fw_lo, 3 * n + 3)
                    if first:
                        pe.wait_ge(x3_lo, 2 * DC)
                    for t in range(4):
                        ins = mm3(bank[4 + t][:], lambda a: hT[:, par, a, t * P:(t + 1) * P],
                                  lambda b: wT[:, par, 2, b, :], first, last, rhs_w)
                    ins.then_inc(d_done, 1)

                def ffn_step(n, par, half, prev, first_down=False, more=True):
                    if more:
                        weights(n + 1, 1 - par, 0)
                    gate_up(n, par, half, 0, g_filled, g_made)
                    if more:
                        weights(n + 1, 1 - par, 1)
                    gate_up(n, par, half, 1, u_filled, h_made)
                    if more:
                        weights(n + 1, 1 - par, 2)
                    if prev:
                        down(n - 1, 1 - par, first_down, False)

                for half in range(2):
                    base = half * NJ
                    ffn_step(base, 0, half, False)
                    if half:
                        pe.wait_ge(x3_made, 4)
                    else:
                        turn_x3(1)
                    ffn_step(base + 1, 1, half, True, first_down=True)
                    with pe.Fori(0, (NJ - 4) // 2) as it:
                        for u in range(2):
                            ffn_step(2 * it + (base + 2 + u), u, half, True)
                    ffn_step(base + NJ - 2, 0, half, True)
                    ffn_step(base + NJ - 1, 1, half, True, more=half == 0)
                    down(base + NJ - 1, 1, False, True)

            pe.wait_ge(l_read, NT)
            for w in range(3):
                weights(0, 0, w)
            project2(NT - 1)
            turn_x3(0)
            pe.wait_ge(z_moved, NT)
            pe.wait_ge(x2_made, NT)
            pe.wait_ge(x3_lo, 4)
            pe.wait_ge(wide_made, 2)
            some_wide = pe.value_load(wide[0:1, 0:1], min_val=0, max_val=1)
            with pe.If(some_wide > 0):
                feed_forward(PASSES, PASSES)
            with pe.Else():
                feed_forward(((HI, HI), (HI, LO)), ((HI, HI), (LO, HI)))

        @block.scalar
        def _(act):
            def turn_hi(q, m):
                act.wait_ge(split_filled, at(q) + m + 1)
                act.copy(ctxT[:, HI, m, :], bank[m % 2][:]).then_inc(hi_made, 1)

            def keys_hi(q, g):
                act.wait_ge(split_filled, at(q) + 4 + g + 1)
                act.activation(kT[:, HI, g, :, 0:SF], bank[g % 2][:].rearrange("p (b s) -> p b s", b=2),
                               ACT.Identity, bias=bkc[:, g:g + 1]).then_inc(hi_made, 1)

            def values_out(q, par, i):
                act.wait_ge(v_filled, 4 * q + i + 1)
                act.copy(V[:, par, i, :], bank[2 + i % 2][:]).then_inc(v_made, 1)

            def weight_hi(dst, fill, k):
                act.wait_ge(split_filled, fill + 1)
                act.copy(dst[:, HI, k, :], bank[fill % 2][:]).then_inc(hi_made, 1)

            for k in range(DC):
                weight_hi(wkT, k, k)
            for m in range(DC):
                turn_hi(0, m)
            act.wait_ge(bias_in, 48)
            for g in range(G):
                keys_hi(0, g)
            for k in range(DC):
                weight_hi(wvT, F_WV + k, k)
            for i in range(4):
                values_out(0, 0, i)
                if i == 1:
                    act.wait_ge(ln_var, 1)
                    act.activation(std[:], ve[:], ACT.Sqrt).then_inc(ln_std, 1)
            for k in range(DC):
                act.wait_ge(wq_filled, k + 1)
                act.copy(wqT[:, k, :], bank[4 + k % 2][:]).then_inc(wq_made, 1)
            act.wait_ge(split_filled, F_TAIL + 1)
            act.copy(ctailT[:, HI], bank[F_TAIL % 2][:].rearrange("p (k r) -> p k r", k=DC)).then_inc(hi_made, 1)
            act.wait_ge(vt_filled, 1)
            act.wait_ge(tail_in, 16)
            act.copy(vt_sb, bank[4][:]).then_inc(vt_made, 1)
            act.wait_ge(vt_filled, 2)
            act.copy(tkeys_sb, bank[5][:]).then_inc(vt_made, 1)
            act.wait_ge(bq_made, 1)

            def queries_out(n):
                half, g = divmod(n, G)
                act.wait_ge(q_filled, n + 1)
                act.activation(qT[:, g, half * BANK:(half + 1) * BANK], bank[2 + n % 2][:], ACT.Identity,
                               bias=bqs[:, g:g + 1], scale=SCALE).then_inc(q_made, 1)

            queries_out(0)
            act.wait_ge(split_filled, F_TAIL + 2)
            for g in range(G):
                ins = act.activation(ktail[:, HI, g, :], bank[(F_TAIL + 1) % 2][:, g * P:g * P + NB], ACT.Identity,
                                     bias=bkc[:, g:g + 1])
            ins.then_inc(hi_made, 1)
            act.wait_ge(vt_filled, 3)
            act.copy(vtailT[:].rearrange("p b g -> p g b"),
                     bank[4][:].rearrange("p (g r) -> p g r", g=G)[:, :, 0:NB]).then_inc(vt_made, 1)
            for n in range(1, 8):
                queries_out(n)

            def exps(p, b):
                act.wait_ge(max_made, 2 * p + b + 1)
                for g in range(G):
                    act.activation(Pn[:, b, g, 0:S], Pn[:, b, g, 0:S], ACT.Exp, bias=nmax[:, b, g:g + 1],
                                   accum_out=ssum[:, b, g:g + 1]).then_inc(exp_done, 1)

            def out_move(p, b):
                act.wait_ge(o_filled, 2 * p + b + 1)
                for h in range(HG):
                    rows = slice(h * Q32, (h + 1) * Q32)
                    src = bank[O_BANK[b]][rows, :].rearrange("p (g h t) -> p g h t", g=G, h=HG)[:, :, h, :]
                    ins = act.copy(oT[rows, :, :, bass.ds(2 * p + b, 1)], src.unsqueeze(3))
                ins.then_inc(o_moved, 1)


            for m in range(DC):
                turn_hi(1, m)

            def step(p, par, more=True):
                keys_hi(p + 1, 0)
                keys_hi(p + 1, 1)
                exps(p, 0)
                keys_hi(p + 1, 2)
                keys_hi(p + 1, 3)
                exps(p, 1)
                for i in range(4):
                    values_out(p + 1, 1 - par, i)
                if more:
                    for m in range(3):
                        turn_hi(p + 2, m)
                out_move(p, 0)
                if more:
                    turn_hi(p + 2, 3)
                out_move(p, 1)

            step(0, 0)
            with act.Fori(0, (NPAIR - 4) // 2) as it:
                for u in range(2):
                    step(2 * it + 1 + u, (1 + u) % 2)
            step(NPAIR - 3, 1)
            step(NPAIR - 2, 0, more=False)
            last = NPAIR - 1

            def weight_out(n):
                dst, k = (woT, owT, w2)[n // DC], n % DC
                act.wait_ge(wt_filled, n + 1)
                act.copy(dst[:, k, :], bank[n % 2][:]).then_inc(wt_made, 1)

            for n in range(4):
                weight_out(n)
            exps(last, 0)
            exps(last, 1)
            for n in range(4, 8):
                weight_out(n)
            out_move(last, 0)
            out_move(last, 1)
            for n in range(8, 12):
                weight_out(n)

            def sqrt_(half, n):
                act.wait_ge(ln_var, n)
                act.activation(std[:, 4 * half:4 * half + 4], ve[:, 4 * half:4 * half + 4], ACT.Sqrt
                               ).then_inc(ln_std, 1)

            def x2t_out(half):
                for k in range(DC):
                    n = DC * half + k
                    act.wait_ge(x2t_filled, n + 1)
                    act.copy(xn2T[:, k, half * BANK:(half + 1) * BANK], bank[n % 2][:]).then_inc(x2t_made, 1)

            def q2_out(half, groups):
                for g in groups:
                    n = G * half + g
                    act.wait_ge(q2_filled, n + 1)
                    act.copy(q2T[:, g, half * BANK:(half + 1) * BANK], bank[5 + n % 2][:]).then_inc(q2_made, 1)

            def qn_out(i):
                act.wait_ge(qn_filled, i + 1)
                act.copy(q2n[:, i, :], bank[QN_BANK[i]][:]).then_inc(qn_made, 1)

            def z_out(i):
                act.wait_ge(z_filled, i + 1)
                if i >= 1:
                    act.wait_ge(y_filled, i)
                act.copy(zT[:].rearrange("p g c -> p (g c)"), bank[2][:]).then_inc(z_moved, 1)

            def exps2(i):
                act.wait_ge(l2_made, i + 1)
                act.activation(e2[:], lg2[:], ACT.Exp, scale=2.0 * INV).then_inc(e2_made, 1)

            def pbd_out(i):
                act.wait_ge(p2T_made, i + 1)
                if i >= 1:
                    act.wait_ge(z_filled, i)
                for n in range(4):
                    rows = slice(n * Q32, (n + 1) * Q32)
                    ins = act.copy(pbd[rows, :, n, :], p2T[rows, :, :])
                ins.then_inc(pbd_made, 1)

            def x3_out(half):
                for k in range(DC):
                    n = DC * half + k
                    act.wait_ge(x3_filled, n + 1)
                    b = bank[4 + k] if half else bank[5 + k % 2]
                    act.copy(xn3T[:, HI, k, half * BANK:(half + 1) * BANK], b[:]).then_inc(x3_hi, 1)

            sqrt_(0, 2)
            x2t_out(0)
            sqrt_(1, 3)
            q2_out(0, range(G))
            x2t_out(1)
            for i in range(4):
                qn_out(i)
            q2_out(1, (0,))
            exps2(0)
            q2_out(1, (1,))
            act.wait_ge(zero_made, 3)
            pbd_out(0)
            q2_out(1, (2, 3))
            for i in range(NT):
                if i < 4:
                    qn_out(4 + i)
                if i + 1 < NT:
                    exps2(i + 1)
                z_out(i)
                if i + 1 < NT:
                    pbd_out(i + 1)
                if i == 5:
                    sqrt_(0, 4)

            def w_hi(n, par, w):
                act.wait_ge(fw_filled, 3 * n + w + 1)
                if w == 2 and not (isinstance(n, int) and n < 2):
                    act.wait_ge(d_done, n - 1)
                act.copy(wT[:, par, w, HI, :], bank[(3 * par + w) % 2][:]).then_inc(fw_hi, 1)

            def ffn_step(n, par, more=True, turned=False):
                if more:
                    w_hi(n + 1, 1 - par, 0)
                act.wait_ge(g_filled, n + 1)
                if not (isinstance(n, int) and n < 1):
                    act.wait_ge(h_made, n)
                act.activation(sg[:], bank[2][:], ACT.Silu, scale=WSCALE).then_inc(g_made, 1)
                if more:
                    w_hi(n + 1, 1 - par, 1)
                act.wait_ge(h_made, n + 1)
                act.copy(hT[:, par, HI, :], hf[:]).then_inc(h_hi, 1)
                if more:
                    w_hi(n + 1, 1 - par, 2)
                if turned:
                    x3_out(1)

            for w in range(3):
                w_hi(0, 0, w)
            x3_out(0)
            sqrt_(1, 5)
            ffn_step(0, 0, turned=True)
            ffn_step(1, 1)
            with act.Fori(1, NJ - 1) as it:
                for u in range(2):
                    ffn_step(2 * it + u, u)
            ffn_step(2 * NJ - 2, 0)
            ffn_step(2 * NJ - 1, 1, more=False)

        @block.vector
        def _(dve):
            ln_n = [0]
            xh_n = [0]

            def link(ins):
                ln_n[0] += 1
                ins.then_inc(ln_step, 1)
                dve.wait_ge(ln_step, ln_n[0])

            def newton(r):
                link(dve.reciprocal(r0[:, r], std[:, r]))
                link(dve.tensor_tensor(r1[:, r], r0[:, r], r0[:, r], ALU.mult))
                link(dve.tensor_tensor(r2[:, r], r1[:, r], ve[:, r], ALU.mult))
                link(dve.tensor_scalar(r1[:, r], r2[:, r], -0.5, 1.5, ALU.mult, ALU.add))
                link(dve.tensor_tensor(rstd[:, r], r1[:, r], r0[:, r], ALU.mult))

            def layernorm(tiles, dst, slot, stds):
                lo, n = tiles[0], len(tiles)
                for i in tiles:
                    ins = dve.bn_stats(stats[:, i, :], xres[:, i, :])
                link(ins)
                for i in tiles:
                    ins = dve.bn_aggr(mv[:, i, :], stats[:, i, :])
                link(ins)
                r = slice(lo, lo + n)
                dve.tensor_scalar(ve[:, r], mv[:, r, 1], EPS, None, ALU.add).then_inc(ln_var, 1)
                dve.wait_ge(ln_std, stds)
                newton(r)
                for i in tiles:
                    dve.tensor_scalar(dst[:, i - slot, :], xres[:, i, :], mv[:, i, 0:1], rstd[:, i:i + 1],
                                      ALU.subtract, ALU.mult).then_inc(xh_made, 1)

            def turn_lo(q, m):
                dve.wait_ge(hi_made, at(q) + m + 1)
                dve.tensor_tensor(ctxT[:, LO, m, :], bank[m % 2][:], ctxT[:, HI, m, :].bitcast(F32), ALU.subtract
                                  ).then_inc(lo_made, 1)

            def keys_lo(q, g):
                dve.wait_ge(hi_made, at(q) + 4 + g + 1)
                dve.scalar_tensor_tensor(kT[:, LO, g, :, 0:SF], bank[g % 2][:].rearrange("p (b s) -> p b s", b=2),
                                         bkc[:, g:g + 1], kT[:, HI, g, :, 0:SF].bitcast(F32),
                                         ALU.add, ALU.subtract).then_inc(lo_made, 1)

            def weight_lo(dst, fill, k):
                dve.wait_ge(hi_made, fill + 1)
                dve.tensor_tensor(dst[:, LO, k, :], bank[fill % 2][:], dst[:, HI, k, :].bitcast(F32), ALU.subtract
                                  ).then_inc(lo_made, 1)

            for k in range(DC):
                weight_lo(wkT, k, k)
            for m in range(DC):
                turn_lo(0, m)
            for g in range(G):
                keys_lo(0, g)
            for k in range(DC):
                weight_lo(wvT, F_WV + k, k)
            dve.wait_ge(x_in, 16)
            layernorm(range(NT), xres, 0, 1)
            dve.wait_ge(hi_made, F_TAIL + 1)
            dve.tensor_tensor(ctailT[:, LO], bank[F_TAIL % 2][:].rearrange("p (k r) -> p k r", k=DC),
                              ctailT[:, HI].bitcast(F32), ALU.subtract).then_inc(lo_made, 1)
            for n in range(8):
                half, k = divmod(n, DC)
                dve.wait_ge(xt_filled, n + 1)
                dve.tensor_copy(xnT[:, k, half * BANK:(half + 1) * BANK], bank[6 + n % 2][:]).then_inc(xt_made, 1)
            dve.wait_ge(hi_made, F_TAIL + 2)
            for g in range(G):
                ins = dve.scalar_tensor_tensor(ktail[:, LO, g, :], bank[(F_TAIL + 1) % 2][:, g * P:g * P + NB],
                                               bkc[:, g:g + 1], ktail[:, HI, g, :].bitcast(F32), ALU.add, ALU.subtract)
            ins.then_inc(lo_made, 1)

            def bias_in_(p, n):
                b, g = ORDER[n]
                dve.wait_ge(s_filled, 8 * p + n + 1)
                if g == 0:
                    dve.wait_ge(bm_made, 2 * p + b + 1)
                dve.tensor_tensor(Pn[:, b, g, 0:S], bank[4 + n % 2][:, 0:S], biasmask[:, b, g, :], ALU.add
                                  ).then_inc(s_biased, 1)

            def maxes(p, b):
                dve.wait_ge(s_biased, 8 * p + 6 + 2 * b)
                dve.tensor_reduce(nmax[:, b, :], Pn[:, b, :, 0:S], AX.X, ALU.max, negate=True).then_inc(max_made, 1)

            def norm(p, b):
                dve.wait_ge(exp_done, 8 * p + 4 * b + 4)
                dve.reciprocal(rsum[:, b, :], ssum[:, b, :]).then_inc(rs_made, 1)
                dve.wait_ge(rs_made, 2 * p + b + 1)
                for g in range(G):
                    ins = dve.tensor_scalar(Pn[:, b, g, 0:S], Pn[:, b, g, 0:S], rsum[:, b, g:g + 1], None, ALU.mult)
                ins.then_inc(norm_done, 1)

            def probs_out(p, n):
                dve.wait_ge(pt_filled, 4 * p + n + 1)
                dve.tensor_copy(PT[:, n // 2, n % 2, :], bank[(6, 5)[n % 2]][:]).then_inc(pt_made, 1)

            for m in range(DC):
                turn_lo(1, m)

            def step(p, first=False, keys_more=True, turn_more=True):
                for n in range(8):
                    bias_in_(p, n)
                    if keys_more and n in (2, 4):
                        keys_lo(p + 1, n // 2 - 1)
                    if n == 5:
                        maxes(p, 0)
                if keys_more:
                    keys_lo(p + 1, 2)
                maxes(p, 1)
                if keys_more:
                    keys_lo(p + 1, 3)
                norm(p, 0)
                probs_out(p, 0)
                norm(p, 1)
                dve.wait_ge(norm_done, 2 * p + 2)
                dve.tensor_tensor(ptdiag[:], Pn[:, :, :, SF].unsqueeze(3).to_broadcast([P, 2, G, T]),
                                  eye32[:].unsqueeze(1).unsqueeze(1).to_broadcast([P, 2, G, T]), ALU.mult
                                  ).then_inc(ptdiag_made, 1)
                probs_out(p, 1)
                dve.wait_ge(scan_in, 48 * p + 48)
                dve.tensor_reduce(wmax[:, bass.ds(p, 1)], w_scan[:], AX.XY, ALU.max,
                                  apply_absolute_value=True).then_inc(scanned, 1)
                probs_out(p, 2)
                probs_out(p, 3)
                if turn_more:
                    turn_lo(p + 2, 0)
                dve.wait_ge(tail_filled, p + 1)
                if not first:
                    dve.wait_ge(tail_added, p)
                dve.tensor_tensor(otail[:], bank[4][:, 0:2 * G * T].rearrange("p (b g t) -> p b g t", b=2, g=G),
                                  vtailT[:, bass.ds(2 * p, 2), :].unsqueeze(3).to_broadcast([P, 2, G, T]), ALU.mult
                                  ).then_inc(otail_made, 1)
                if turn_more:
                    for m in range(1, DC):
                        turn_lo(p + 2, m)

            dve.wait_ge(vt_made, 3)
            step(0, first=True)
            with dve.Fori(1, NPAIR - 2) as p:
                step(p)
            step(NPAIR - 2, turn_more=False)
            step(NPAIR - 1, keys_more=False, turn_more=False)
            dve.wait_ge(scanned, NPAIR)
            dve.tensor_reduce(wtop[:], wmax[:], AX.X, ALU.max).then_inc(wtop_made, 1)

            dve.wait_ge(m_filled, 1)
            dve.scalar_tensor_tensor(mbd[:], bank[3][:].rearrange("p (g c) -> p g c", g=G), INV,
                                     blockmask[:].unsqueeze(1).to_broadcast([P, G, P]), ALU.mult, ALU.mult
                                     ).then_inc(m_made, 1)

            dve.wait_ge(wtop_filled, 1)
            dve.tensor_reduce(wtop1[:], bank[6][0:1, 0:P], AX.X, ALU.max).then_inc(wide_made, 1)
            dve.wait_ge(wide_made, 1)
            dve.tensor_scalar(wide[:], wtop1[:], float(W_EXACT), None, ALU.is_gt).then_inc(wide_made, 1)

            dve.wait_ge(tail_added, NPAIR)
            for g in range(G):
                dve.tensor_scalar(oT2[:, g, :], oT2[:, g, :], bvc[:, g:g + 1], None, ALU.add).then_inc(ob_made, 1)

            def ln_start(half):
                lo = 4 * half
                for i in range(lo, lo + 4):
                    ins = dve.bn_aggr(mv[:, i, :], stats[:, i, :])
                link(ins)
                dve.tensor_scalar(ve[:, lo:lo + 4], mv[:, lo:lo + 4, 1], EPS, None, ALU.add).then_inc(ln_var, 1)

            def ln_rstd(half, stds):
                dve.wait_ge(ln_std, stds)
                newton(slice(4 * half, 4 * half + 4))

            def ln_end(half, dst):
                lo = 4 * half
                for i in range(lo, lo + 4):
                    dve.tensor_scalar(dst[:, i - lo, :], xres[:, i, :], mv[:, i, 0:1], rstd[:, i:i + 1],
                                      ALU.subtract, ALU.mult).then_inc(xh_made, 1)

            def ln_tiles(half, dst, stds):
                ln_start(half)
                ln_rstd(half, stds)
                ln_end(half, dst)

            for i in range(NT):
                dve.wait_ge(r1_filled, i + 1)
                dve.wait_ge(xb_made, i + 1)
                dve.tensor_tensor(xres[:, i, :], bank[2 + i % 2][:], xres[:, i, :], ALU.add).then_inc(x1_made, 1)
                dve.wait_ge(x1_made, i + 1)
                link(dve.bn_stats(stats[:, i, :], xres[:, i, :]))
                if i == 3:
                    ln_tiles(0, xh_first, 2)
            ln_tiles(1, wo_nat, 3)
            steps = [0]

            def link2(ins):
                steps[0] += 1
                ins.then_inc(dve2, 1)
                dve.wait_ge(dve2, steps[0])

            def hs(ap):
                return ap.unsqueeze(2).to_broadcast([P, H, Q32])

            def squares(i):
                dve.wait_ge(qn_made, i + 1)
                link2(dve.tensor_tensor(sq[:], q2n[:, i, :], q2n[:, i, :], ALU.mult))
                link2(dve.tensor_reduce(qsq[:], sq[:].rearrange("p (h d) -> p h d", h=H), AX.X, ALU.add))

            def norms(i):
                if i >= 2:
                    dve.wait_ge(l_filled, i - 1)
                dve.tensor_tensor(dq[:, i % 2], hs(qsq[:]), eye32[:].unsqueeze(1).to_broadcast([P, H, Q32]),
                                  ALU.mult).then_inc(dq_made, 1)
                link2(dve.tensor_scalar(hqsq[:, i % 2], qsq[:], -0.5, None, ALU.mult))

            def block2_out(i):
                dve.wait_ge(y_filled, i + 1)
                dve.wait_ge(xb_made, NT + i + 1)
                dve.tensor_tensor(xres[:, i, :], bank[3 + i % 2][:], xres[:, i, :], ALU.add).then_inc(x2_made, 1)
                dve.wait_ge(x2_made, i + 1)
                link(dve.bn_stats(stats[:, i, :], xres[:, i, :]))

            for i in range(2):
                squares(i)
                norms(i)
            for i in range(NT):
                dve.wait_ge(l_filled, i + 1)
                dve.tensor_tensor(lg[:], bank[i % 2][:].rearrange("p (h s) -> p h s", h=H), hs(hqsq[:, i % 2]),
                                  ALU.add).then_inc(l_read, 1)
                dve.wait_ge(l_read, i + 1)
                link2(dve.tensor_reduce(m2[:], lg[:], AX.X, ALU.max))
                dve.tensor_tensor(lg2[:], lg[:], hs(m2[:]), ALU.subtract).then_inc(l2_made, 1)
                if i + 2 < NT:
                    squares(i + 2)
                dve.wait_ge(e2_made, i + 1)
                link2(dve.tensor_reduce(s2[:], e2[:], AX.X, ALU.add))
                link2(dve.reciprocal(rs2[:], s2[:]))
                link2(dve.tensor_tensor(p2[:], e2[:], hs(rs2[:]), ALU.mult))
                if i:
                    dve.wait_ge(pbd_made, i)
                dve.transpose(p2T[:].rearrange("p h s -> p (h s)"), p2[:].rearrange("p h s -> p (h s)")
                              ).then_inc(p2T_made, 1)
                if i + 2 < NT:
                    norms(i + 2)
                if i == 7:
                    ln_rstd(0, 4)
                    ln_end(0, xh3[:, 0:4])
                if i >= 1:
                    block2_out(i - 1)
                if i == 5:
                    ln_start(0)
            def x3_low(half):
                cols = slice(half * BANK, (half + 1) * BANK)
                for k in range(DC):
                    b = bank[4 + k] if half else bank[5 + k % 2]
                    dve.wait_ge(x3_hi, 4 * half + k + 1)
                    dve.tensor_tensor(xn3T[:, LO, k, cols], b[:], xn3T[:, HI, k, cols].bitcast(F32),
                                      ALU.subtract).then_inc(x3_lo, 1)

            def w_lo(n, par, w):
                dve.wait_ge(fw_hi, 3 * n + w + 1)
                dve.tensor_tensor(wT[:, par, w, LO, :], bank[(3 * par + w) % 2][:], wT[:, par, w, HI, :].bitcast(F32),
                                  ALU.subtract).then_inc(fw_lo, 1)

            def ffn_step(n, par, more=True):
                if more:
                    w_lo(n + 1, 1 - par, 0)
                    w_lo(n + 1, 1 - par, 1)
                dve.wait_ge(u_filled, n + 1)
                dve.wait_ge(g_made, n + 1)
                if not (isinstance(n, int) and n < 1):
                    dve.wait_ge(h_lo, n)
                dve.scalar_tensor_tensor(hf[:], bank[3][:], WSCALE, sg[:], ALU.mult, ALU.mult).then_inc(h_made, 1)
                dve.wait_ge(h_hi, n + 1)
                dve.tensor_tensor(hT[:, par, LO, :], hf[:], hT[:, par, HI, :].bitcast(F32), ALU.subtract
                                  ).then_inc(h_lo, 1)
                if more:
                    w_lo(n + 1, 1 - par, 2)

            for w in range(3):
                w_lo(0, 0, w)
            block2_out(NT - 1)
            x3_low(0)
            ln_tiles(1, xh3[:, 4:8], 5)
            for half in range(2):
                base = half * NJ
                ffn_step(base, 0)
                if half == 0:
                    x3_low(1)
                ffn_step(base + 1, 1)
                with dve.Fori(1, NJ // 2 - 1) as it:
                    for u in range(2):
                        ffn_step(2 * it + (base + u), u)
                ffn_step(base + NJ - 2, 0)
                ffn_step(base + NJ - 1, 1, more=half == 0)
                dve.wait_ge(d_done, base + NJ)
                for t in range(4):
                    i = 4 * half + t
                    dve.scalar_tensor_tensor(xres[:, i, :], bank[4 + t][:], WSCALE, xres[:, i, :],
                                             ALU.mult, ALU.add).then_inc(x3_made, 1)


_INS = ["x", "ctx_1024", "mask_Bx1xSxS2_bf1", "L0_xattn_Wq", "L0_xattn_bq", "L0_xattn_Wk", "L0_xattn_bk",
        "L0_xattn_Wv", "L0_xattn_bv", "L0_xattn_Wo", "L0_xattn_bo", "L0_xattn_rel_emb", "L0_attn_q_weight",
        "L0_attn_v_weight", "L0_attn_out_w", "L0_attn_out_b", "L0_ffn_w_gate", "L0_ffn_w_up", "L0_ffn_w_down"]
_OUTS = [((32, 32, 512), "float32")]


def kernel(**inputs):
    import numpy as _np
    import concourse.bacc as _bacc
    from concourse.bass_utils import run_bass_kernel_spmd as _run

    nc = _bacc.Bacc("TRN2", target_bir_lowering=False, num_devices=1)
    arrays, args = {}, []
    for name in _INS:
        a = _np.ascontiguousarray(inputs[name])
        if a.dtype == _np.bool_:
            a = a.view(_np.uint8)
        arrays[f"in_{name}"] = a
        args.append(nc.dram_tensor(f"in_{name}", a.shape, mybir.dt.from_np(a.dtype), kind="ExternalInput").ap())
    for i, (shape, dtype) in enumerate(_OUTS):
        args.append(nc.dram_tensor(f"out_{i}", shape, mybir.dt.from_np(_np.dtype(dtype)), kind="ExternalOutput").ap())
    perceiver_kernel(nc, *args)
    r = _run(nc, [arrays], core_ids=[0])
    return r.results[0]["out_0"]
```

```python
import math
from contextlib import ExitStack

import concourse.bass as bass
from concourse import mybir

ALU = mybir.AluOpType
ACT = mybir.ActivationFunctionType
AX = mybir.AxisListType
F32 = mybir.dt.float32
F32R = mybir.dt.float32r
I32 = mybir.dt.int32
U8 = mybir.dt.uint8

P = 128
BANK = 512
Q32 = 32
HI, LO = 0, 1
PASSES = ((HI, HI), (HI, LO), (LO, HI))


def perceiver_kernel(
    nc, x, ctx_in, mask, wq, bq, wk, bk, wv, bv, wo, bo, rel_emb, q_weight, v_weight, out_w, out_b,
    w_gate, w_up, w_down, out,
):
    NB, T, D = x.shape
    S = ctx_in.shape[1]
    HD = q_weight.shape[2]
    H = q_weight.shape[1]
    HID = w_gate.shape[0]
    DC = D // P
    G = H * HD // P
    HG = P // HD
    TOK = NB * T
    NT = TOK // P
    SF = 2 * P
    SP_ = S + 1
    NPAIR = NB // 2
    NJ = HID // P
    MAX_REL = (rel_emb.shape[0] - 1) // 2
    RL = T + S - 1
    SCALE = float(HD) ** -0.5
    INV = 1.0 / math.sqrt(HD)
    WSCALE = 1.0 / 127.0
    EPS = 1e-5
    WK = HID * D // (NB // 2) // P
    W_EXACT = 256
    assert (T, HD, D, S, NB) == (Q32, Q32, BANK, SF + 1, Q32) and RL <= 288
    RLP = 288

    rel_dram = nc.dram_tensor("rel_scratch", (H, RLP), F32, kind="Internal").ap()

    with ExitStack() as keep:
        def sb(name, shape, dt=F32, stack=keep):
            return stack.enter_context(nc.sbuf_tensor(name, shape, dt))

        def sem(name):
            return keep.enter_context(nc.semaphore(name))

        bank = [keep.enter_context(nc.psum_tensor(f"bank{i}", [P, BANK], F32)) for i in range(8)]

        ident = sb("ident", [P, P])
        blockmask = sb("blockmask", [P, P])
        eye32 = sb("eye32", [P, Q32])
        halfneg = sb("halfneg", [P, P])
        xres = sb("xres", [P, NT, D])
        stats = sb("stats", [P, NT, 6])
        mv = sb("mv", [P, NT, 2])
        ve = sb("ve", [P, NT])
        std = sb("std", [P, NT])
        r0 = sb("r0", [P, NT])
        r1 = sb("r1", [P, NT])
        r2 = sb("r2", [P, NT])
        rstd = sb("rstd", [P, NT])
        bqs = sb("bqs", [P, G])
        bqc = sb("bqc", [P, G])
        bkc = sb("bkc", [P, G])
        bvc = sb("bvc", [P, G])

        wmax = sb("wmax", [P, NPAIR])
        wtop = sb("wtop", [P, 1])
        wtop1 = sb("wtop1", [1, 1])
        wide = sb("wide", [1, 1], I32)

        ob_bc = sb("ob_bc", [P, D])

        ph1 = ExitStack()
        wkT = sb("wkT", [P, 2, DC, D], F32R, ph1)
        wvT = sb("wvT", [P, 2, DC, D], F32R, ph1)
        ctxn = sb("ctxn", [P, 2, DC, D], F32, ph1)
        V = sb("V", [P, 2, 4, D], F32, ph1)
        oT = sb("oT", [P, G, T, NB], F32, ph1)
        relbias = sb("relbias", [P, G, S], F32, ph1)
        biasmask = sb("biasmask", [P, 2, G, S], F32, ph1)
        ctxT = sb("ctxT", [P, 2, DC, BANK], F32R, ph1)
        kT = sb("kT", [P, 2, G, 2, SP_], F32R, ph1)
        Pn = sb("Pn", [P, 2, G, SP_], F32, ph1)
        PT = sb("PT", [P, 2, 2, BANK], F32, ph1)
        vtailT = sb("vtailT", [P, NB, G], F32, ph1)
        ptdiag = sb("ptdiag", [P, 2, G, T], F32, ph1)
        otail = sb("otail", [P, 2, G, T], F32, ph1)
        qbd = sb("qbd", [P, 2, 2, G, P], F32R, ph1)
        qT = sb("qT", [P, G, TOK], F32, ph1)
        qtmp = sb("qtmp", [P, BANK], F32, ph1)
        ktail = sb("ktail", [P, 2, G, NB], F32R, ph1)
        masku = sb("masku", [P, 2, S], U8, ph1)
        maskf = sb("maskf", [P, 2, S], F32, ph1)
        nmax = sb("nmax", [P, 2, G], F32, ph1)
        w_scan = sb("w_scan", [P, 3, WK], I32, ph1)
        ssum = sb("ssum", [P, 2, G], F32, ph1)
        rsum = sb("rsum", [P, 2, G], F32, ph1)
        wk_nat = Pn[:].rearrange("p a g s -> p (a g s)")[:, 0:DC * D].rearrange("p (c n) -> p c n", c=DC)
        wv_nat = PT[:].rearrange("p a c s -> p (a c s)")[:, 0:DC * D].rearrange("p (c n) -> p c n", c=DC)
        wq_nat = biasmask[:].rearrange("p a g s -> p (a g s)")[:, 0:DC * D].rearrange("p (c n) -> p c n", c=DC)
        maskf_rel = maskf[:].rearrange("p b s -> p (b s)")[0:H, 0:RLP]
        vt_sb = ctxn[:, 1, 1]
        tkeys_sb = ctxn[:, 1, 2]
        tail_nat = ctxn[:, 1, 0]
        ctailT = ctxT[:, :, :, 0:P]
        ph1.close()
        ph0 = ExitStack()
        sb("over_wkT_to_V", [P, 7 * DC * D], F32, ph0)
        wqT_hi = sb("wqT_hi", [P, DC, D], F32R, ph0)
        xnT = sb("xnT", [P, DC, TOK], F32R, ph0)
        sb("over_relbias_to_kT", [P, 3 * G * S + 2 * DC * BANK + 4 * G * SP_], F32, ph0)
        xnT_lo0 = sb("xnT_lo0", [P, DC, D], F32R, ph0)
        sb("over_Pn", [P, 2 * G * SP_ - DC * D], F32, ph0)
        wqT_lo = sb("wqT_lo", [P, DC, D], F32R, ph0)
        ph0.close()
        wqT = (wqT_hi, wqT_lo)
        xnT_lo = (xnT_lo0, ctxT[:, 1])

        ph2 = ExitStack()
        MBD_TO_ZT = G * P + 2 * G * 4 * P + 2 * D + NT * H + 2 * H + 2 * H * Q32 + 5 * H * Q32 + 3 * H \
            + H * 4 * Q32 + G * P + 816
        vw = sb("vw", [P, DC, D], F32, ph2)
        ow_nat = sb("ow_nat", [P, DC, D], F32, ph2)
        owT = sb("owT", [P, DC, D], F32, ph2)
        w2 = sb("w2", [P, G, D], F32, ph2)
        wo_nat = sb("wo_nat", [P, DC, D], F32, ph2)
        qw = sb("qw", [P, DC, D], F32, ph2)
        woT = sb("woT", [P, DC, D], F32, ph2)
        xh_first = sb("xh_first", [P, 4, D], F32, ph2)
        sb("over_oT", [P, G, TOK], F32, ph2)
        q2T = sb("q2T", [P, G, TOK], F32, ph2)
        q2n = sb("q2n", [P, NT, D], F32, ph2)
        mbd = sb("mbd", [P, G, P], F32, ph2)
        q2bd = sb("q2bd", [P, 2, G, 4, HG, Q32], F32, ph2)
        sq = sb("sq", [P, 2, D], F32, ph2)
        qsq = sb("qsq", [P, NT, H], F32, ph2)
        hqsq = sb("hqsq", [P, 2, H], F32, ph2)
        dq = sb("dq", [P, 2, H, Q32], F32, ph2)
        lg = sb("lg", [P, H, Q32], F32, ph2)
        lg2 = sb("lg2", [P, H, Q32], F32, ph2)
        e2 = sb("e2", [P, H, Q32], F32, ph2)
        p2 = sb("p2", [P, H, Q32], F32, ph2)
        p2T = sb("p2T", [P, H, Q32], F32, ph2)
        m2 = sb("m2", [P, H], F32, ph2)
        s2 = sb("s2", [P, H], F32, ph2)
        rs2 = sb("rs2", [P, H], F32, ph2)
        pbd = sb("pbd", [P, H, 4, Q32], F32, ph2)
        zT = sb("zT", [P, G, P], F32, ph2)
        sb("under_w_saved", [P, 816], F32, ph2)
        w_int = sb("w_int", [P, 2, 3, D], I32, ph2)
        w_f = sb("w_f", [P, 2, 3, D], F32, ph2)
        ph2.close()
        oT2 = oT[:].rearrange("p g t b -> p g (t b)")
        xh = (xh_first, wo_nat)
        ph2q = ExitStack()
        qwp = sb("qwp", [P, 2, DC, D], F32R, ph2q)
        sb("over_owT_to_q2T", [P, 10 * DC * D], F32, ph2q)
        xn2_hi = sb("xn2_hi", [P, 2, DC, BANK], F32R, ph2q)
        sb("over_mbd_to_zT", [P, MBD_TO_ZT], F32, ph2q)
        xn2_lo = sb("xn2_lo", [P, DC, TOK], F32R, ph2q)
        ph2q.close()

        ph3 = ExitStack()
        wT = sb("wT", [P, 2, 3, 2, D], F32R, ph3)
        sb("over_w2", [P, G, D], F32, ph3)
        xn3T = sb("xn3T", [P, 2, DC, TOK], F32R, ph3)
        xh3 = sb("xh3", [P, NT, D], F32, ph3)
        sg = sb("sg", [P, BANK], F32, ph3)
        hf = sb("hf", [P, BANK], F32, ph3)
        hT = sb("hT", [P, 2, 2, BANK], F32R, ph3)
        w_saved = sb("w_saved", [P, NJ, 3, D], F32, ph3)
        ph3.close()

        bc_in = sem("bc_in")
        scan_in, scanned, wtop_made, wtop_filled, wide_made = (
            sem(n) for n in ("scan_in", "scanned", "wtop_made", "wtop_filled", "wide_made"))
        wk_in = sem("wk_in")
        wv_in, wq_in, x_in, tail_in, xr_in, bias_in = (
            sem(n) for n in ("wv_in", "wq_in", "x_in", "tail_in", "xr_in", "bias_in"))
        rel_in, rel_out, relb_in = (sem(n) for n in ("rel_in", "rel_out", "relb_in"))
        ctx_in_s = [sem(f"ctx_in{i}") for i in range(2)]
        mask_in = sem("mask_in")
        const_made = sem("const_made")
        passed = sem("passed")
        pool_step = sem("pool_step")
        split_filled, hi_made, lo_made = sem("split_filled"), sem("hi_made"), sem("lo_made")
        wv_filled, wv_hi, wv_lo = sem("wv_filled"), sem("wv_hi"), sem("wv_lo")
        wq_filled, wq_hi, wq_lo = sem("wq_filled"), sem("wq_hi"), sem("wq_lo")
        xt_filled, xt_hi, xt_lo = sem("xt_filled"), sem("xt_hi"), sem("xt_lo")
        q_filled, q_made = sem("q_filled"), sem("q_made")
        vt_filled, vt_made = sem("vt_filled"), sem("vt_made")
        ptdiag_made, tail_filled, otail_made, tail_added = (
            sem(n) for n in ("ptdiag_made", "tail_filled", "otail_made", "tail_added"))
        bq_made = sem("bq_made")
        v_filled, v_made = sem("v_filled"), sem("v_made")
        s_filled, s_biased = sem("s_filled"), sem("s_biased")
        max_made, exp_done, rs_made, norm_done = (
            sem(n) for n in ("max_made", "exp_done", "rs_made", "norm_done"))
        pt_filled, pt_made = sem("pt_filled"), sem("pt_made")
        o_filled, o_moved = sem("o_filled"), sem("o_moved")
        qbd_made, bm_made, ktail_made = sem("qbd_made"), sem("bm_made"), sem("ktail_made")
        ln_step, ln_var, ln_std, xh_made = (sem(n) for n in ("ln_step", "ln_var", "ln_std", "xh_made"))
        ob_made = sem("ob_made")
        w_b_in = sem("w_b_in")
        w_in2 = sem("w_in2")
        ow_in = sem("ow_in")
        wt_filled, wt_made = sem("wt_filled"), sem("wt_made")
        m_filled, m_made = sem("m_filled"), sem("m_made")
        r1_filled, x1_made = sem("r1_filled"), sem("x1_made")
        xb_made = sem("xb_made")
        x2t_filled, x2t_hi, x2t_lo = sem("x2t_filled"), sem("x2t_hi"), sem("x2t_lo")
        qw_hi, qw_lo = sem("qw_hi"), sem("qw_lo")
        q2_filled, q2_made = sem("q2_filled"), sem("q2_made")
        qn_filled, qn_made = sem("qn_filled"), sem("qn_made")
        dq_made, l_filled, l_read, e2_made, p2T_made, pbd_made = (
            sem(n) for n in ("dq_made", "l_filled", "l_read", "e2_made", "p2T_made", "pbd_made"))
        l2_made = sem("l2_made")
        q2bd_made = sem("q2bd_made")
        sq_read = sem("sq_read")
        z_filled, z_moved = sem("z_filled"), sem("z_moved")
        dve2 = sem("dve2")
        y_filled, x2_made = sem("y_filled"), sem("x2_made")
        x3_filled, x3_hi, x3_lo = sem("x3_filled"), sem("x3_hi"), sem("x3_lo")
        wi_in = [sem(f"wi_in{i}") for i in range(2)]
        wf_made, w_kept = sem("wf_made"), sem("w_kept")
        fw_filled, fw_hi, fw_lo = sem("fw_filled"), sem("fw_hi"), sem("fw_lo")
        g_filled, g_made = sem("g_filled"), sem("g_made")
        u_filled, h_made, h_hi, h_lo = sem("u_filled"), sem("h_made"), sem("h_hi"), sem("h_lo")
        d_done, acc_filled, x3_made = sem("d_done"), sem("acc_filled"), sem("x3_made")
        out_stored = sem("out_stored")
        zero_made = sem("zero_made")

        N0 = DC + 2
        F_CTX0, F_TAIL = DC, 3 * DC
        QN_BANK = (4, 7, 4, 7, 6, 7, 6, 7)
        WV_AFTER = ((0, 1), (2, 3), (), ())
        X2_BANK = (0, 1, 4, 7)
        X3_BANK = ((5, 6, 7, 3), (4, 5, 6, 7))
        O_BANK = (7, 2)
        KEYS_AFTER = (1, 3, 6, 7)
        ORDER = ((0, 0), (1, 0), (0, 1), (1, 1), (0, 2), (0, 3), (1, 2), (1, 3))
        block = keep.enter_context(nc.Block())

        def at(q):
            return F_CTX0 if isinstance(q, int) and q == 0 else N0 + 8 * q

        def wait_alone(eng, s, value):
            eng.wait_ge(s, value)
            eng.sem_inc(passed, 1)

        x_bt = x.rearrange("b t m -> (b t) m").rearrange("(i p) m -> p i m", p=P)

        @block.sync
        def _(sp):
            def w_nat(w):
                return w.rearrange("(c p) n -> p c n", p=P)

            def load_bias(src):
                sp.dma_start(ob_bc[:], src.rearrange("(o n) -> o n", o=1).to_broadcast([P, D])).then_inc(bc_in, 16)

            def load_ctx(q, par):
                for b in range(2):
                    sp.dma_start(ctxn[:, par, 2 * b:2 * b + 2, :],
                                 ctx_in[2 * q + b, 0:SF, :].rearrange("(c p) m -> p c m", p=P)
                                 ).then_inc(ctx_in_s[par], 16)

            def load_mask(q):
                for b in range(2):
                    for h in range(HG):
                        sp.dma_start(masku[h * T:(h + 1) * T, b, :], mask[2 * q + b, 0, :, :]
                                     ).then_inc(mask_in, 16)

            sp.dma_start(wk_nat, w_nat(wk)).then_inc(wk_in, 16)
            load_ctx(0, 0)
            sp.dma_start(wv_nat, w_nat(wv)).then_inc(wv_in, 16)
            sp.dma_start(xres[:], x_bt).then_inc(x_in, 16)
            sp.dma_start(wq_nat, w_nat(wq)).then_inc(wq_in, 16)
            sp.wait_ge(zero_made, 1)
            sp.dma_start(tail_nat[0:NB, :], ctx_in[:, SF, :]).then_inc(tail_in, 16)
            load_mask(0)
            load_bias(bo)
            sp.wait_ge(rel_out, 16)
            for t in range(T):
                src = bass.AP(rel_dram.tensor, T - 1 - t, [[RLP, HG], [HG * RLP, G], [1, S]])
                sp.dma_start(relbias[t:P:T, :, :], src).then_inc(relb_in, 16)
            sp.wait_ge(xt_filled, 8)
            x_t = x.rearrange("b (i t) m -> t b i m", t=4)
            for t in range(4):
                sp.dma_start(xres[t * NB:(t + 1) * NB, :, :], x_t[t]).then_inc(xr_in, 16)
            sp.wait_ge(split_filled, F_TAIL + 2)
            sp.wait_ge(vt_filled, 3)
            load_ctx(1, 1)

            def next_ctx(q, par):
                wait_alone(sp, split_filled, N0 + 8 * q + 4)
                load_ctx(q + 2, par)

            def load_scan(q):
                for k, w in enumerate((w_gate, w_up, w_down)):
                    flat = w.rearrange("a b -> (a b)").rearrange("(s p k) -> p s k", p=P, k=WK)
                    sp.dma_start(w_scan[:, k:k + 1, :], flat[:, bass.ds(q, 1), :]).then_inc(scan_in, 16)

            def step(p, par, ctx_more):
                wait_alone(sp, bm_made, 2 * p + 2)
                load_mask(p + 1)
                if ctx_more:
                    next_ctx(p + 2, par)
                wait_alone(sp, scanned, p + 1)
                load_scan(p + 1)

            load_scan(0)
            next_ctx(0, 0)
            next_ctx(1, 1)
            with sp.Fori(0, (NPAIR - 4) // 2) as it:
                for u in range(2):
                    step(2 * it + u, u, True)
            for p in range(NPAIR - 4, NPAIR - 1):
                if p == NPAIR - 2:
                    sp.wait_ge(split_filled, N0 + 8 * (NPAIR - 1) + 4)
                    sp.dma_start(wo_nat[:], w_nat(wo)).then_inc(w_b_in, 16)
                    sp.dma_start(qw[:], q_weight.rearrange("(c p) h d -> p c (h d)", p=P)).then_inc(w_in2, 16)
                step(p, p % 2, False)

            last = NPAIR - 1
            sp.wait_ge(split_filled, N0 + 8 * last + 8)
            sp.dma_start(vw[:], v_weight.rearrange("(c p) h d -> p c (h d)", p=P)).then_inc(w_in2, 16)
            sp.dma_start(ow_nat[:], w_nat(out_w)).then_inc(ow_in, 16)

            sp.wait_ge(xb_made, NT)
            load_bias(out_b)

            sp.wait_ge(q2_made, 8)
            def load_w(j, par):
                sp.dma_start(w_int[:, par, 0, :], w_gate[bass.ds(j * P, P), :]).then_inc(wi_in[par], 16)
                sp.dma_start(w_int[:, par, 1, :], w_up[bass.ds(j * P, P), :]).then_inc(wi_in[par], 16)
                sp.dma_start(w_int[:, par, 2, :].rearrange("p (c k) -> p c k", c=DC),
                             w_down[:, bass.ds(j * P, P)].rearrange("(c p) k -> p c k", p=P)
                             ).then_inc(wi_in[par], 16)

            for j in range(2):
                load_w(j, j)
            with sp.Fori(0, (NJ - 2) // 2) as it:
                for u in range(2):
                    wait_alone(sp, wf_made, 6 * it + 3 * (u + 1))
                    load_w(2 * it + (u + 2), u)
            out_t = out.rearrange("b (i t) m -> t b i m", t=4)
            for i in range(0, NT, 2):
                sp.wait_ge(x3_made, i + 2)
                for t in range(4):
                    sp.dma_start(out_t[t][:, i:i + 2, :], xres[t * NB:(t + 1) * NB, i:i + 2, :]
                                 ).then_inc(out_stored, 16)
            sp.wait_ge(out_stored, 16 * 4 * NT // 2)

        @block.gpsimd
        def _(pool):
            step_n = [0]

            def link(ins):
                step_n[0] += 1
                ins.then_inc(pool_step, 1)
                pool.wait_ge(pool_step, step_n[0])

            pool.memset(tail_nat, 0.0).then_inc(zero_made, 1)
            link(pool.memset(ident[:], 0.0))
            link(pool.memset(blockmask[:], 1.0))
            link(pool.memset(eye32[:], 0.0))
            pool.affine_select(out=ident[:], in_=ident[:], compare_op=ALU.not_equal, fill=1.0, base=0,
                               pattern=[[-1, P]], channel_multiplier=1).then_inc(const_made, 1)
            bm3 = blockmask[:].rearrange("p (h d) -> p h d", h=HG)
            link(pool.affine_select(out=bm3, in_=bm3, compare_op=ALU.is_ge, fill=0.0, base=0,
                                    pattern=[[-Q32, HG], [0, Q32]], channel_multiplier=1))
            link(pool.affine_select(out=bm3, in_=bm3, compare_op=ALU.is_ge, fill=0.0, base=Q32 - 1,
                                    pattern=[[Q32, HG], [0, Q32]], channel_multiplier=-1))
            for k in range(HG):
                link(pool.affine_select(out=eye32[:], in_=eye32[:], compare_op=ALU.not_equal, fill=1.0,
                                        base=-Q32 * k, pattern=[[-1, Q32]], channel_multiplier=1))
            pool.tensor_scalar(halfneg[:], blockmask[:], -0.5, None, ALU.mult).then_inc(const_made, 1)

            with nc.allow_non_contiguous_dma(reason="small bias rows, once"):
                for name_ap, w in ((bqc, bq), (bkc, bk), (bvc, bv)):
                    pool.dma_start(name_ap[:], w.rearrange("(g p) -> p g", p=P)).then_inc(bias_in, 16)
                rel_sb = qtmp[0:H, 0:RLP]
                pool.dma_start(rel_sb, rel_emb[MAX_REL + T - RLP:MAX_REL + T, :].rearrange("i h -> h i")
                               ).then_inc(rel_in, 16)
            pool.wait_ge(rel_in, 16)
            link(pool.tensor_copy(maskf_rel, rel_sb[:, ::-1]))
            pool.dma_start(rel_dram, maskf_rel).then_inc(rel_out, 16)
            pool.wait_ge(bias_in, 48)
            pool.tensor_scalar(bqs[:], bqc[:], SCALE, None, ALU.mult).then_inc(bq_made, 1)

            for part in range(2):
                pool.memset(kT[:, part, :, :, S:SP_].bitcast(F32), 0.0)

            hmask = blockmask[:].rearrange("p (h d) -> p h d", h=HG)

            def block_queries(q, first):
                if not first:
                    pool.wait_ge(s_filled, 8 * q)
                for b in range(2):
                    t3 = qtmp[:].rearrange("p (g h t) -> p g h t", g=G, h=HG)
                    for g in range(G):
                        src = qT[:, g, bass.ds((2 * q + b) * T, T)].unsqueeze(1).to_broadcast([P, HG, T])
                        ins = pool.tensor_tensor(t3[:, g], src, hmask, ALU.mult)
                    ins.then_inc(pool_step, 1)
                    wait_alone(pool, pool_step, step_n[0] + 6 * q + 3 * b + 1)
                    qf = qtmp[:].rearrange("p (g c) -> p g c", g=G)
                    pool.tensor_copy(qbd[:, HI, b], qf).then_inc(pool_step, 1)
                    wait_alone(pool, pool_step, step_n[0] + 6 * q + 3 * b + 2)
                    ins = pool.tensor_tensor(qbd[:, LO, b], qf, qbd[:, HI, b].bitcast(F32), ALU.subtract)
                    ins.then_inc(pool_step, 1)
                    pool.wait_ge(pool_step, step_n[0] + 6 * q + 3 * b + 3)
                for part in range(2):
                    ins = pool.tensor_copy(kT[:, part, :, :, SF],
                                           ktail[:, part, :, bass.ds(2 * q, 2)])
                ins.then_inc(qbd_made, 1)

            def bias_and_mask(q, first):
                wait_alone(pool, mask_in, 16 * 2 * HG * (q + 1))
                pool.tensor_scalar(maskf[:], masku[:], -1.0, 3.0e38, ALU.add, ALU.mult).then_inc(ktail_made, 1)
                wait_alone(pool, ktail_made, 2 * q + 1)
                pool.tensor_scalar(maskf[:], maskf[:], 4.0, None, ALU.mult).then_inc(ktail_made, 1)
                wait_alone(pool, ktail_made, 2 * q + 2)
                for b in range(2):
                    if not first:
                        pool.wait_ge(s_biased, 8 * q)
                    pool.tensor_tensor(biasmask[:, b], relbias[:],
                                       maskf[:, b].unsqueeze(1).to_broadcast([P, G, S]), ALU.add
                                       ).then_inc(bm_made, 1)

            def add_tail(p, p1):
                wait_alone(pool, otail_made, p1)
                wait_alone(pool, o_moved, 2 * p1)
                pair = oT[:, :, :, bass.ds(2 * p, 2)]
                pool.tensor_tensor(pair, pair, otail[:].rearrange("p b g t -> p g t b"), ALU.add
                                   ).then_inc(tail_added, 1)

            pool.wait_ge(split_filled, DC)
            pool.wait_ge(relb_in, 16 * T)
            pool.wait_ge(wq_filled, DC)
            bias_and_mask(0, True)
            pool.wait_ge(q_made, G)
            pool.wait_ge(lo_made, N0 + 8)
            block_queries(0, True)
            with pool.Fori(1, NPAIR) as q:
                block_queries(q, False)
                bias_and_mask(q, False)
                add_tail(q - 1, q)

            for i in range(NT):
                if i == 0:
                    pool.wait_ge(xr_in, 16 * 4)
                    pool.wait_ge(bc_in, 16)
                pool.tensor_tensor(xres[:, i, :], xres[:, i, :], ob_bc[:], ALU.add).then_inc(xb_made, 1)
            add_tail(NPAIR - 1, NPAIR)
            pool.memset(pbd[:], 0.0).then_inc(zero_made, 1)
            for i in range(NT):
                pool.wait_ge(q2_made, 4 * (i // 4) + 4)
                if i >= 2:
                    pool.wait_ge(l_filled, i - 1)
                for g in range(G):
                    src = q2T[:, g, i * P:(i + 1) * P].rearrange("p (n s) -> p n s", n=4)
                    ins = pool.tensor_tensor(q2bd[:, i % 2, g], src.unsqueeze(2).to_broadcast([P, 4, HG, Q32]),
                                             hmask.unsqueeze(1).to_broadcast([P, 4, HG, Q32]), ALU.mult)
                ins.then_inc(q2bd_made, 1)
                if i == 1:
                    pool.wait_ge(xh_made, 2 * NT)
                    pool.wait_ge(bc_in, 32)
                for j in (0, 1) if i == 1 else (i,) if i >= 2 else ():
                    pool.tensor_tensor(xres[:, j, :], xres[:, j, :], ob_bc[:], ALU.add).then_inc(xb_made, 1)

            def convert(n, j2, par):
                pool.wait_ge(wi_in[par], 48 * j2 + 48)
                for w in range(3):
                    if not (isinstance(n, int) and n < 2):
                        wait_alone(pool, fw_filled, 3 * n - 5 + w)
                    pool.tensor_copy(w_f[:, par, w], w_int[:, par, w]).then_inc(wf_made, 1)

            for j in range(2):
                convert(j, 0, j)
            with pool.Fori(0, (NJ - 2) // 2) as it:
                for u in range(2):
                    convert(2 * it + (2 + u), it + 1, u)

        @block.tensor
        def _(pe):
            def mm3(dst, lhs, rhs, first, last, passes=PASSES):
                for n, (a, b) in enumerate(passes):
                    ins = pe.matmul(dst, lhs(a), rhs(b), start=first and n == 0, stop=last and n == len(passes) - 1)
                return ins

            def turn(q, par, m):
                pe.wait_ge(lo_made, at(q) + m - 1)
                for i in range(4):
                    ins = pe.transpose(bank[m % 2][:, i * P:(i + 1) * P],
                                       ctxn[:, par, i, m * P:(m + 1) * P], ident[:])
                ins.then_inc(split_filled, 1)

            def keys(q, g):
                pe.wait_ge(lo_made, at(q) + 4 + max(g - 1, 0))
                for m in range(DC):
                    ins = mm3(bank[g % 2][:], lambda a: wkT[:, a, m, g * P:(g + 1) * P],
                              lambda b: ctxT[:, b, m, :], m == 0, m == DC - 1)
                ins.then_inc(split_filled, 1)

            def values(q, i, first):
                if not (first and i < 2):
                    pe.wait_ge(v_made, 4 * q + i - 1)
                for m in range(DC):
                    ins = mm3(bank[2 + i % 2][:], lambda a: ctxT[:, a, m, i * P:(i + 1) * P],
                              lambda b: wvT[:, b, m, :], m == 0, m == DC - 1)
                ins.then_inc(v_filled, 1)

            def scores(p, n, first):
                b, g = ORDER[n]
                if n == 0:
                    pe.wait_ge(lo_made, N0 + 8 * p + 8)
                    pe.wait_ge(qbd_made, p + 1)
                    if not first:
                        pe.wait_ge(otail_made, p)
                if not (first and n < 2):
                    pe.wait_ge(s_biased, 8 * p + n - 1)
                ins = mm3(bank[4 + n % 2][:, 0:SP_], lambda a: qbd[:, a, b, g, :],
                          lambda c: kT[:, c, g, b, :], True, True)
                ins.then_inc(s_filled, 1)

            def probs_turn(p, b, c):
                n = 2 * b + c
                if c == 0:
                    pe.wait_ge(norm_done, 2 * p + b + 1)
                if n >= 2:
                    pe.wait_ge(pt_made, 4 * p + n - 1)
                for g in range(G):
                    ins = pe.transpose(bank[(6, 5)[n % 2]][:, g * P:(g + 1) * P], Pn[:, b, g, c * P:(c + 1) * P],
                                       ident[:])
                ins.then_inc(pt_filled, 1)

            def attend(p, par, b, first=False, more=True):
                pe.wait_ge(pt_made, 4 * p + 2 * b + 2)
                if b == 0:
                    pe.wait_ge(v_made, 4 * p + 4)
                else:
                    pe.wait_ge(v_made, 4 * p + (8 if more else 4))
                if b == 0 and not first:
                    pe.wait_ge(o_moved, 2 * p)
                for g in range(G):
                    cols = slice(g * P, (g + 1) * P)
                    for c in range(2):
                        ins = pe.matmul(bank[O_BANK[b]][:, cols], V[:, par, 2 * b + c, cols], PT[:, b, c, cols],
                                        start=c == 0, stop=c == 1)
                ins.then_inc(o_filled, 1)

            def tail(p):
                pe.wait_ge(ptdiag_made, p + 1)
                pe.matmul(bank[4][:, 0:2 * G * T], blockmask[:], ptdiag[:].rearrange("p b g t -> p (b g t)"),
                          start=True, stop=True).then_inc(tail_filled, 1)

            def ctx_wait(q, par):
                pe.wait_ge(ctx_in_s[par], 16 * q + 32 - 16 * par)

            def step(p, par, first=False, more=True):
                q = p + 1
                for n in range(8):
                    scores(p, n, first)
                    if n in KEYS_AFTER:
                        keys(q, KEYS_AFTER.index(n))
                if not first:
                    pe.wait_ge(o_moved, 2 * p)
                for i in range(4):
                    values(q, i, False)
                    probs_turn(p, i // 2, i % 2)
                if more:
                    ctx_wait(p + 2, par)
                    turn(p + 2, par, 0)
                tail(p)
                if more:
                    turn(p + 2, par, 1)
                attend(p, par, 0, first)
                if more:
                    turn(p + 2, par, 2)
                    turn(p + 2, par, 3)
                attend(p, par, 1)

            pe.wait_ge(const_made, 2)

            def turn_rows(fill, nat, cols_of):
                if fill >= 2:
                    pe.wait_ge(lo_made, fill - 1)
                for c in range(DC):
                    ins = pe.transpose(bank[fill % 2][:, c * P:(c + 1) * P], cols_of(nat, c), ident[:])
                ins.then_inc(split_filled, 1)

            for k in range(DC):
                pe.wait_ge(wk_in, 16)
                turn_rows(k, wk_nat, lambda nat, c: nat[:, c, k * P:(k + 1) * P])
            ctx_wait(0, 0)
            for m in range(DC):
                turn(0, 0, m)
            def turn_weight0(nat, k, b, filled, split):
                if k >= 2:
                    pe.wait_ge(split, k - 1)
                for c in range(DC):
                    ins = pe.transpose(bank[b + k % 2][:, c * P:(c + 1) * P], nat[:, c, k * P:(k + 1) * P], ident[:])
                ins.then_inc(filled, 1)

            for g in range(G):
                keys(0, g)
                if g == 0:
                    pe.wait_ge(wv_in, 16)
                for k in WV_AFTER[g]:
                    turn_weight0(wv_nat, k, 4, wv_filled, wv_lo)
            pe.wait_ge(wv_lo, DC)
            for i in range(4):
                values(0, i, True)
            pe.wait_ge(tail_in, 16)
            turn_rows(F_TAIL, tail_nat, lambda nat, c: nat[:, c * P:(c + 1) * P])

            def turn_x(n):
                half, k = divmod(n, DC)
                pe.wait_ge(xh_made, 4 * half + 4)
                if n >= 2:
                    pe.wait_ge(xt_lo, n - 1)
                for c in range(4):
                    ins = pe.transpose(bank[6 + n % 2][:, c * P:(c + 1) * P],
                                       xres[:, 4 * half + c, k * P:(k + 1) * P], ident[:])
                ins.then_inc(xt_filled, 1)

            for n in range(DC):
                turn_x(n)
            pe.wait_ge(wq_in, 16)
            pe.wait_ge(v_made, 4)
            for w, b in ((wvT, 4), (wkT, 5)):
                for k in (0, 1) if b == 4 else (2, 3):
                    turn_weight0(wq_nat, k, 2, wq_filled, wq_lo)
                if b == 4:
                    pe.wait_ge(lo_made, F_TAIL + 1)
                for k in range(DC):
                    ins = mm3(bank[b][:], lambda a: ctailT[:, a, k, :], lambda c: w[:, c, k, :], k == 0, k == DC - 1)
                ins.then_inc(vt_filled, 1)

            def queries(n):
                half, g = divmod(n, G)
                pe.wait_ge(xt_lo, 4 * half + 4)
                if n >= 2:
                    pe.wait_ge(q_made, n - 1)
                cols = slice(half * BANK, (half + 1) * BANK)
                for k in range(DC):
                    ins = mm3(bank[2 + n % 2][:], lambda a: wqT[a][:, k, g * P:(g + 1) * P],
                              lambda b: xnT_lo[half][:, k, :] if b else xnT[:, k, cols], k == 0, k == DC - 1)
                ins.then_inc(q_filled, 1)

            pe.wait_ge(wq_lo, DC)
            queries(0)
            pe.wait_ge(vt_made, 2)
            turn_rows(F_TAIL + 1, tkeys_sb, lambda nat, c: nat[:, c * P:(c + 1) * P])
            for g in range(G):
                ins = pe.transpose(bank[4][:, g * P:(g + 1) * P], vt_sb[:, g * P:(g + 1) * P], ident[:])
            ins.then_inc(vt_filled, 1)
            for n in (1, 2):
                queries(n)
                turn_x(2 * n + 2)
                turn_x(2 * n + 3)
            for n in range(3, 8):
                queries(n)
            ctx_wait(1, 1)
            for m in range(DC):
                turn(1, 1, m)
            pe.wait_ge(q_made, 8)
            step(0, 0, first=True)
            with pe.Fori(0, (NPAIR - 4) // 2) as it:
                for u in range(2):
                    step(2 * it + 1 + u, (1 + u) % 2)
            step(NPAIR - 3, 1)
            step(NPAIR - 2, 0, more=False)
            last = NPAIR - 1

            def turn_weight(n):
                nat, k = (wo_nat, ow_nat)[n // DC], n % DC
                if k == 0:
                    pe.wait_ge((w_b_in, ow_in)[n // DC], 16)
                if n >= 2:
                    pe.wait_ge(wt_made, n - 1)
                for c in range(DC):
                    ins = pe.transpose(bank[n % 2][:, c * P:(c + 1) * P], nat[:, c, k * P:(k + 1) * P], ident[:])
                ins.then_inc(wt_filled, 1)

            for g in range(G):
                scores(last, 2 * g, False)
                scores(last, 2 * g + 1, False)
                turn_weight(g)
            pe.wait_ge(w_in2, 32)
            for g in range(G):
                cols = slice(g * P, (g + 1) * P)
                for k in range(DC):
                    ins = pe.matmul(bank[3][:, cols], vw[:, k, cols], qw[:, k, cols], start=k == 0, stop=k == DC - 1)
            ins.then_inc(m_filled, 1)
            for n in range(4):
                probs_turn(last, n // 2, n % 2)
                turn_weight(4 + n)
            tail(last)
            attend(last, 1, 0)
            attend(last, 1, 1, more=False)
            pe.wait_ge(wtop_made, 1)
            pe.transpose(bank[6][0:1, 0:P], wtop[:], ident[:]).then_inc(wtop_filled, 1)
            pe.wait_ge(m_made, 1)
            for g in range(G):
                pe.wait_ge(wt_made, 2 * DC + max(g - 1, 0))
                ins = pe.matmul(bank[g % 2][:], mbd[:, g, :], owT[:, g, :], start=True, stop=True)
                ins.then_inc(wt_filled, 1)

            def turn_x2(half):
                pe.wait_ge(xh_made, 8 + 4 * half + 4)
                if half:
                    pe.wait_ge(x2t_lo, DC)
                for k in range(DC):
                    for c in range(4):
                        ins = pe.transpose(bank[X2_BANK[k]][:, c * P:(c + 1) * P],
                                           xh[half][:, c, k * P:(k + 1) * P], ident[:])
                    ins.then_inc(x2t_filled, 1)

            pe.wait_ge(ob_made, 4)
            for i in range(NT):
                if i == 6:
                    pe.wait_ge(wt_made, 3 * DC)
                    turn_x2(0)
                if i >= 2:
                    pe.wait_ge(x1_made, i - 1)
                for k in range(DC):
                    ins = pe.matmul(bank[2 + i % 2][:], oT2[:, k, i * P:(i + 1) * P], woT[:, k, :],
                                    start=k == 0, stop=k == DC - 1)
                ins.then_inc(r1_filled, 1)

            def queries2(half, groups):
                cols = slice(half * BANK, (half + 1) * BANK)
                pe.wait_ge(x2t_lo, 4 * half + 4)
                pe.wait_ge(qw_lo, DC)
                for g in groups:
                    n = G * half + g
                    if n >= 2:
                        pe.wait_ge(q2_made, n - 1)
                    for k in range(DC):
                        ins = mm3(bank[5 + n % 2][:], lambda a: qwp[:, a, k, g * P:(g + 1) * P],
                                  lambda b: xn2_lo[:, k, cols] if b else xn2_hi[:, half, k, :], k == 0, k == DC - 1)
                    ins.then_inc(q2_filled, 1)

            def turn_q2(i):
                pe.wait_ge(q2_made, 4 * (i // 4) + 4)
                if i >= 2:
                    pe.wait_ge(qn_made, i - 1)
                for g in range(G):
                    ins = pe.transpose(bank[QN_BANK[i]][:, g * P:(g + 1) * P],
                                       q2T[:, g, i * P:(i + 1) * P], ident[:])
                ins.then_inc(qn_filled, 1)

            def logits2(i):
                pe.wait_ge(dq_made, i + 1)
                pe.wait_ge(q2bd_made, i + 1)
                if i >= 2:
                    pe.wait_ge(l_read, i - 1)
                L = bank[i % 2]
                pe.matmul(L[:], halfneg[:], dq[:, i % 2].rearrange("p h s -> p (h s)"), start=True, stop=False,
                          skip_group_check=True)
                for n in range(4):
                    for g in range(G):
                        ins = pe.matmul(L[n * Q32:(n + 1) * Q32, g * P:(g + 1) * P],
                                        q2T[:, g, i * P + n * Q32:i * P + (n + 1) * Q32],
                                        q2bd[:, i % 2, g, n].rearrange("p h s -> p (h s)"),
                                        start=False, stop=g == G - 1, skip_group_check=True)
                ins.then_inc(l_filled, 1)

            def attend2(i):
                pe.wait_ge(pbd_made, i + 1)
                if i >= 1:
                    pe.wait_ge(z_moved, i)
                for h in range(H):
                    g, r = divmod(h, HG)
                    ins = pe.matmul(bank[2][r * Q32:(r + 1) * Q32, g * P:(g + 1) * P],
                                    q2n[:, i, h * HD:(h + 1) * HD], pbd[:, h].rearrange("p n t -> p (n t)"),
                                    start=True, stop=True, skip_group_check=True)
                ins.then_inc(z_filled, 1)

            def project2(i):
                pe.wait_ge(z_moved, i + 1)
                if i == 0:
                    pe.wait_ge(qn_made, 4)
                if i >= 2:
                    pe.wait_ge(x2_made, i - 1)
                for g in range(G):
                    ins = pe.matmul(bank[3 + i % 2][:], zT[:, g, :], w2[:, g, :], start=g == 0, stop=g == G - 1)
                ins.then_inc(y_filled, 1)

            queries2(0, (0, 1))
            turn_x2(1)
            queries2(0, (2, 3))
            queries2(1, (0,))
            pe.wait_ge(x2t_lo, 8)
            for i in range(4):
                turn_q2(i)
            queries2(1, (1,))
            logits2(0)
            logits2(1)
            queries2(1, (2, 3))
            for i in range(NT):
                attend2(i)
                if i < 4:
                    turn_q2(4 + i)
                if i + 2 < NT:
                    logits2(i + 2)
                if i < NT - 1:
                    project2(i)

            def turn_x3(half):
                pe.wait_ge(xh_made, 16 + 4 * half + 4)
                if half == 0:
                    pe.wait_ge(qn_made, NT)
                    pe.wait_ge(x2_made, NT - 1)
                else:
                    pe.wait_ge(x2_made, NT)
                    pe.wait_ge(x3_lo, 4)
                for k in range(DC):
                    b = bank[X3_BANK[half][k]]
                    for c in range(4):
                        ins = pe.transpose(b[:, c * P:(c + 1) * P], xh3[:, 4 * half + c, k * P:(k + 1) * P], ident[:])
                    ins.then_inc(x3_filled, 1)

            def weights(n, par, w):
                pe.wait_ge(wf_made, 3 * n + w + 1)
                k = 3 * n + w
                if not (isinstance(n, int) and k < 2):
                    pe.wait_ge(fw_lo, k - 1)
                for c in range(DC):
                    ins = pe.transpose(bank[(3 * par + w) % 2][:, c * P:(c + 1) * P],
                                       w_f[:, par, w, c * P:(c + 1) * P], ident[:])
                ins.then_inc(fw_filled, 1)

            def feed_forward(lhs_w, rhs_w):
                def gate_up(n, par, half, w, filled, freed):
                    pe.wait_ge(fw_lo, 3 * n + w + 1)
                    if not (isinstance(n, int) and n < 1):
                        pe.wait_ge(freed, n)
                    for k in range(DC):
                        ins = mm3(bank[2 + w][:], lambda a: wT[:, par, w, a, k * P:(k + 1) * P],
                                  lambda b: xn3T[:, b, k, half * BANK:(half + 1) * BANK], k == 0, k == DC - 1,
                                  lhs_w)
                    ins.then_inc(filled, 1)

                def down(n, par, first, last):
                    pe.wait_ge(h_lo, n + 1)
                    pe.wait_ge(fw_lo, 3 * n + 3)
                    if first:
                        pe.wait_ge(x3_lo, 2 * DC)
                    for t in range(4):
                        ins = mm3(bank[4 + t][:], lambda a: hT[:, par, a, t * P:(t + 1) * P],
                                  lambda b: wT[:, par, 2, b, :], first, last, rhs_w)
                        if last and t < 3:
                            ins.then_inc(acc_filled, 1)
                    ins.then_inc(d_done, 1)

                def ffn_step(n, par, half, prev, first_down=False, more=True):
                    if more:
                        weights(n + 1, 1 - par, 0)
                    if half == 0 and not prev:
                        pe.wait_ge(x3_lo, DC)
                    gate_up(n, par, half, 0, g_filled, g_made)
                    if more:
                        weights(n + 1, 1 - par, 1)
                    if first_down and half == 0:
                        turn_x3(1)
                    gate_up(n, par, half, 1, u_filled, h_made)
                    if more:
                        weights(n + 1, 1 - par, 2)
                    if prev:
                        down(n - 1, 1 - par, first_down, False)

                for half in range(2):
                    base = half * NJ
                    turned = half == 0
                    ffn_step(base, 0, half, False, more=turned)
                    if half:
                        pe.wait_ge(x3_made, 4)
                    ffn_step(base + 1, 1, half, True, first_down=True, more=turned)
                    with pe.Fori(0, (NJ - 4) // 2) as it:
                        for u in range(2):
                            ffn_step(2 * it + (base + 2 + u), u, half, True, more=turned)
                    ffn_step(base + NJ - 2, 0, half, True, more=turned)
                    ffn_step(base + NJ - 1, 1, half, True, more=False)
                    down(base + NJ - 1, 1, False, True)

            pe.wait_ge(l_read, NT)
            weights(0, 0, 0)
            weights(0, 0, 1)
            turn_x3(0)
            project2(NT - 1)
            weights(0, 0, 2)
            pe.wait_ge(wide_made, 2)
            some_wide = pe.value_load(wide[0:1, 0:1], min_val=0, max_val=1)
            with pe.If(some_wide > 0):
                feed_forward(PASSES, PASSES)
            with pe.Else():
                feed_forward(((HI, HI), (HI, LO)), ((HI, HI), (LO, HI)))

        @block.scalar
        def _(act):
            def turn_hi(q, m):
                act.wait_ge(split_filled, at(q) + m + 1)
                act.copy(ctxT[:, HI, m, :], bank[m % 2][:]).then_inc(hi_made, 1)

            def keys_hi(q, g):
                act.wait_ge(split_filled, at(q) + 4 + g + 1)
                act.activation(kT[:, HI, g, :, 0:SF], bank[g % 2][:].rearrange("p (b s) -> p b s", b=2),
                               ACT.Identity, bias=bkc[:, g:g + 1]).then_inc(hi_made, 1)

            def values_out(q, par, i):
                act.wait_ge(v_filled, 4 * q + i + 1)
                act.copy(V[:, par, i, :], bank[2 + i % 2][:]).then_inc(v_made, 1)

            def weight_hi(dst, fill, k):
                act.wait_ge(split_filled, fill + 1)
                act.copy(dst[:, HI, k, :], bank[fill % 2][:]).then_inc(hi_made, 1)

            for k in range(DC):
                weight_hi(wkT, k, k)
            for m in range(DC):
                turn_hi(0, m)
            act.wait_ge(bias_in, 48)
            for g in range(G):
                keys_hi(0, g)
                for k in WV_AFTER[g]:
                    act.wait_ge(wv_filled, k + 1)
                    act.copy(wvT[:, HI, k, :], bank[4 + k % 2][:]).then_inc(wv_hi, 1)
            for i in range(4):
                values_out(0, 0, i)
                if i == 1:
                    act.wait_ge(ln_var, 1)
                    act.activation(std[:], ve[:], ACT.Sqrt).then_inc(ln_std, 1)
            act.wait_ge(split_filled, F_TAIL + 1)
            act.copy(ctailT[:, HI], bank[F_TAIL % 2][:].rearrange("p (k r) -> p k r", k=DC)).then_inc(hi_made, 1)

            def x_hi(n):
                half, k = divmod(n, DC)
                act.wait_ge(xt_filled, n + 1)
                act.copy(xnT[:, k, half * BANK:(half + 1) * BANK], bank[6 + n % 2][:]).then_inc(xt_hi, 1)

            for n in range(DC):
                x_hi(n)
            for k in range(DC):
                act.wait_ge(wq_filled, k + 1)
                act.copy(wqT[HI][:, k, :], bank[2 + k % 2][:]).then_inc(wq_hi, 1)
            act.wait_ge(vt_filled, 1)
            act.wait_ge(tail_in, 16)
            act.copy(vt_sb, bank[4][:]).then_inc(vt_made, 1)
            act.wait_ge(vt_filled, 2)
            act.copy(tkeys_sb, bank[5][:]).then_inc(vt_made, 1)
            act.wait_ge(bq_made, 1)

            def queries_out(n):
                half, g = divmod(n, G)
                act.wait_ge(q_filled, n + 1)
                act.activation(qT[:, g, half * BANK:(half + 1) * BANK], bank[2 + n % 2][:], ACT.Identity,
                               bias=bqs[:, g:g + 1], scale=SCALE).then_inc(q_made, 1)

            queries_out(0)
            act.wait_ge(split_filled, F_TAIL + 2)
            for g in range(G):
                ins = act.activation(ktail[:, HI, g, :], bank[(F_TAIL + 1) % 2][:, g * P:g * P + NB], ACT.Identity,
                                     bias=bkc[:, g:g + 1])
            ins.then_inc(hi_made, 1)
            act.wait_ge(vt_filled, 3)
            act.copy(vtailT[:].rearrange("p b g -> p g b"),
                     bank[4][:].rearrange("p (g r) -> p g r", g=G)[:, :, 0:NB]).then_inc(vt_made, 1)
            for n in (1, 2):
                queries_out(n)
                x_hi(2 * n + 2)
                x_hi(2 * n + 3)
            for n in range(3, 8):
                queries_out(n)

            def exps(p, b):
                act.wait_ge(max_made, 2 * p + b + 1)
                for g in range(G):
                    act.activation(Pn[:, b, g, 0:S], Pn[:, b, g, 0:S], ACT.Exp, bias=nmax[:, b, g:g + 1],
                                   accum_out=ssum[:, b, g:g + 1]).then_inc(exp_done, 1)

            def out_move(p, b):
                act.wait_ge(o_filled, 2 * p + b + 1)
                for h in range(HG):
                    rows = slice(h * Q32, (h + 1) * Q32)
                    src = bank[O_BANK[b]][rows, :].rearrange("p (g h t) -> p g h t", g=G, h=HG)[:, :, h, :]
                    ins = act.copy(oT[rows, :, :, bass.ds(2 * p + b, 1)], src.unsqueeze(3))
                ins.then_inc(o_moved, 1)


            for m in range(DC):
                turn_hi(1, m)

            def step(p, par, more=True):
                keys_hi(p + 1, 0)
                keys_hi(p + 1, 1)
                exps(p, 0)
                keys_hi(p + 1, 2)
                keys_hi(p + 1, 3)
                exps(p, 1)
                for i in range(4):
                    values_out(p + 1, 1 - par, i)
                if more:
                    turn_hi(p + 2, 0)
                    turn_hi(p + 2, 1)
                out_move(p, 0)
                if more:
                    turn_hi(p + 2, 2)
                    turn_hi(p + 2, 3)
                out_move(p, 1)

            step(0, 0)
            with act.Fori(0, (NPAIR - 4) // 2) as it:
                for u in range(2):
                    step(2 * it + 1 + u, (1 + u) % 2)
            step(NPAIR - 3, 1)
            step(NPAIR - 2, 0, more=False)
            last = NPAIR - 1

            def weight_out(n):
                dst, k = (woT, owT, w2)[n // DC], n % DC
                act.wait_ge(wt_filled, n + 1)
                act.copy(dst[:, k, :], bank[n % 2][:]).then_inc(wt_made, 1)

            for n in range(4):
                weight_out(n)
            exps(last, 0)
            exps(last, 1)
            for n in range(4, 8):
                weight_out(n)
            out_move(last, 0)
            out_move(last, 1)
            for n in range(8, 12):
                weight_out(n)

            def sqrt_(half, n):
                act.wait_ge(ln_var, n)
                act.activation(std[:, 4 * half:4 * half + 4], ve[:, 4 * half:4 * half + 4], ACT.Sqrt
                               ).then_inc(ln_std, 1)

            def x2t_out(half):
                for k in range(DC):
                    act.wait_ge(x2t_filled, DC * half + k + 1)
                    act.copy(xn2_hi[:, half, k, :], bank[X2_BANK[k]][:]).then_inc(x2t_hi, 1)

            def q2_out(half, groups):
                for g in groups:
                    n = G * half + g
                    act.wait_ge(q2_filled, n + 1)
                    act.copy(q2T[:, g, half * BANK:(half + 1) * BANK], bank[5 + n % 2][:]).then_inc(q2_made, 1)

            def qn_out(i):
                act.wait_ge(qn_filled, i + 1)
                act.copy(q2n[:, i, :], bank[QN_BANK[i]][:])
                if i >= 2:
                    act.wait_ge(sq_read, i - 1)
                act.activation(sq[:, i % 2], bank[QN_BANK[i]][:], ACT.Square).then_inc(qn_made, 1)

            def z_out(i):
                act.wait_ge(z_filled, i + 1)
                if i >= 1:
                    act.wait_ge(y_filled, i)
                act.copy(zT[:].rearrange("p g c -> p (g c)"), bank[2][:]).then_inc(z_moved, 1)

            def exps2(i):
                act.wait_ge(l2_made, i + 1)
                act.activation(e2[:], lg2[:], ACT.Exp, scale=2.0 * INV).then_inc(e2_made, 1)

            def pbd_out(i):
                act.wait_ge(p2T_made, i + 1)
                if i >= 1:
                    act.wait_ge(z_filled, i)
                for n in range(4):
                    rows = slice(n * Q32, (n + 1) * Q32)
                    ins = act.copy(pbd[rows, :, n, :], p2T[rows, :, :])
                ins.then_inc(pbd_made, 1)

            def x3_out(half):
                for k in range(DC):
                    n = DC * half + k
                    act.wait_ge(x3_filled, n + 1)
                    b = bank[X3_BANK[half][k]]
                    act.copy(xn3T[:, HI, k, half * BANK:(half + 1) * BANK], b[:]).then_inc(x3_hi, 1)

            act.wait_ge(m_filled, 1)
            for k in range(DC):
                act.copy(qwp[:, HI, k, :], qw[:, k, :]).then_inc(qw_hi, 1)
            sqrt_(0, 2)
            x2t_out(0)
            sqrt_(1, 3)
            q2_out(0, (0, 1))
            x2t_out(1)
            q2_out(0, (2, 3))
            q2_out(1, (0,))
            for i in range(4):
                qn_out(i)
            q2_out(1, (1,))
            exps2(0)
            q2_out(1, (2,))
            act.wait_ge(zero_made, 2)
            pbd_out(0)
            q2_out(1, (3,))
            for i in range(NT):
                if i + 1 < NT:
                    exps2(i + 1)
                z_out(i)
                if i == 6:
                    sqrt_(0, 4)
                if i < 4:
                    qn_out(4 + i)
                if i + 1 < NT:
                    pbd_out(i + 1)

            def w_hi(n, par, w, saved=False):
                if saved:
                    act.wait_ge((g_filled, u_filled, d_done)[w], n - 1)
                    act.copy(wT[:, par, w:w + 1, HI, :], w_saved[:, bass.ds(n - NJ, 1), w, :]).then_inc(fw_hi, 1)
                    return
                act.wait_ge(fw_filled, 3 * n + w + 1)
                if w == 2 and not (isinstance(n, int) and n < 2):
                    act.wait_ge(d_done, n - 1)
                act.copy(wT[:, par, w, HI, :], bank[(3 * par + w) % 2][:]).then_inc(fw_hi, 1)

            def ffn_step(n, par, more=True, saved=False, tokens=False, root=False):
                if more:
                    w_hi(n + 1, 1 - par, 0, saved)
                if root:
                    w_hi(n + 1, 1 - par, 1)
                    sqrt_(1, 5)
                act.wait_ge(g_filled, n + 1)
                if not (isinstance(n, int) and n < 1):
                    act.wait_ge(h_made, n)
                act.activation(sg[:], bank[2][:], ACT.Silu, scale=WSCALE).then_inc(g_made, 1)
                if root:
                    w_hi(n + 1, 1 - par, 2)
                elif more:
                    w_hi(n + 1, 1 - par, 1, saved)
                if tokens:
                    x3_out(1)
                act.wait_ge(h_made, n + 1)
                act.copy(hT[:, par, HI, :], hf[:]).then_inc(h_hi, 1)
                if more and not root:
                    w_hi(n + 1, 1 - par, 2, saved)

            w_hi(0, 0, 0)
            w_hi(0, 0, 1)
            x3_out(0)
            w_hi(0, 0, 2)
            ffn_step(0, 0, root=True)
            ffn_step(1, 1, tokens=True)
            with act.Fori(1, NJ // 2 - 1) as it:
                for u in range(2):
                    ffn_step(2 * it + u, u)
            ffn_step(NJ - 2, 0)
            ffn_step(NJ - 1, 1, saved=True)
            with act.Fori(NJ // 2, NJ - 1) as it:
                for u in range(2):
                    ffn_step(2 * it + u, u, saved=True)
            ffn_step(2 * NJ - 2, 0, saved=True)
            ffn_step(2 * NJ - 1, 1, more=False)

        @block.vector
        def _(dve):
            ln_n = [0]

            def link(ins):
                ln_n[0] += 1
                ins.then_inc(ln_step, 1)
                dve.wait_ge(ln_step, ln_n[0])

            def newton(r):
                link(dve.reciprocal(r0[:, r], std[:, r]))
                link(dve.tensor_tensor(r1[:, r], r0[:, r], r0[:, r], ALU.mult))
                link(dve.tensor_tensor(r2[:, r], r1[:, r], ve[:, r], ALU.mult))
                link(dve.tensor_scalar(r1[:, r], r2[:, r], -0.5, 1.5, ALU.mult, ALU.add))
                link(dve.tensor_tensor(rstd[:, r], r1[:, r], r0[:, r], ALU.mult))

            def layernorm(tiles, dst, slot, stds):
                lo, n = tiles[0], len(tiles)
                for i in tiles:
                    ins = dve.bn_stats(stats[:, i, :], xres[:, i, :])
                link(ins)
                for i in tiles:
                    ins = dve.bn_aggr(mv[:, i, :], stats[:, i, :])
                link(ins)
                r = slice(lo, lo + n)
                dve.tensor_scalar(ve[:, r], mv[:, r, 1], EPS, None, ALU.add).then_inc(ln_var, 1)
                dve.wait_ge(ln_std, stds)
                newton(r)
                for i in tiles:
                    dve.tensor_scalar(dst[:, i - slot, :], xres[:, i, :], mv[:, i, 0:1], rstd[:, i:i + 1],
                                      ALU.subtract, ALU.mult).then_inc(xh_made, 1)

            def turn_lo(q, m):
                dve.wait_ge(hi_made, at(q) + m + 1)
                dve.tensor_tensor(ctxT[:, LO, m, :], bank[m % 2][:], ctxT[:, HI, m, :].bitcast(F32), ALU.subtract
                                  ).then_inc(lo_made, 1)

            def keys_lo(q, g):
                dve.wait_ge(hi_made, at(q) + 4 + g + 1)
                dve.scalar_tensor_tensor(kT[:, LO, g, :, 0:SF], bank[g % 2][:].rearrange("p (b s) -> p b s", b=2),
                                         bkc[:, g:g + 1], kT[:, HI, g, :, 0:SF].bitcast(F32),
                                         ALU.add, ALU.subtract).then_inc(lo_made, 1)

            def weight_lo(dst, fill, k):
                dve.wait_ge(hi_made, fill + 1)
                dve.tensor_tensor(dst[:, LO, k, :], bank[fill % 2][:], dst[:, HI, k, :].bitcast(F32), ALU.subtract
                                  ).then_inc(lo_made, 1)

            for k in range(DC):
                weight_lo(wkT, k, k)
            for m in range(DC):
                turn_lo(0, m)
            for g in range(G):
                keys_lo(0, g)
                for k in WV_AFTER[g]:
                    dve.wait_ge(wv_hi, k + 1)
                    dve.tensor_tensor(wvT[:, LO, k, :], bank[4 + k % 2][:], wvT[:, HI, k, :].bitcast(F32),
                                      ALU.subtract).then_inc(wv_lo, 1)
            dve.wait_ge(x_in, 16)
            layernorm(range(NT), xres, 0, 1)
            dve.wait_ge(hi_made, F_TAIL + 1)
            dve.tensor_tensor(ctailT[:, LO], bank[F_TAIL % 2][:].rearrange("p (k r) -> p k r", k=DC),
                              ctailT[:, HI].bitcast(F32), ALU.subtract).then_inc(lo_made, 1)

            def x_lo(n):
                half, k = divmod(n, DC)
                dve.wait_ge(xt_hi, n + 1)
                dve.tensor_tensor(xnT_lo[half][:, k, :], bank[6 + n % 2][:],
                                  xnT[:, k, half * BANK:(half + 1) * BANK].bitcast(F32), ALU.subtract
                                  ).then_inc(xt_lo, 1)

            for n in range(DC):
                x_lo(n)
            for k in range(DC):
                dve.wait_ge(wq_hi, k + 1)
                dve.tensor_tensor(wqT[LO][:, k, :], bank[2 + k % 2][:], wqT[HI][:, k, :].bitcast(F32), ALU.subtract
                                  ).then_inc(wq_lo, 1)
            dve.wait_ge(hi_made, F_TAIL + 2)
            for g in range(G):
                ins = dve.scalar_tensor_tensor(ktail[:, LO, g, :], bank[(F_TAIL + 1) % 2][:, g * P:g * P + NB],
                                               bkc[:, g:g + 1], ktail[:, HI, g, :].bitcast(F32), ALU.add, ALU.subtract)
            ins.then_inc(lo_made, 1)
            dve.wait_ge(vt_filled, 2)
            for n in range(DC, 2 * DC):
                x_lo(n)

            def bias_in_(p, n):
                b, g = ORDER[n]
                dve.wait_ge(s_filled, 8 * p + n + 1)
                if g == 0:
                    dve.wait_ge(bm_made, 2 * p + b + 1)
                dve.tensor_tensor(Pn[:, b, g, 0:S], bank[4 + n % 2][:, 0:S], biasmask[:, b, g, :], ALU.add
                                  ).then_inc(s_biased, 1)

            def maxes(p, b):
                dve.wait_ge(s_biased, 8 * p + 6 + 2 * b)
                dve.tensor_reduce(nmax[:, b, :], Pn[:, b, :, 0:S], AX.X, ALU.max, negate=True).then_inc(max_made, 1)

            def norm(p, b):
                dve.wait_ge(exp_done, 8 * p + 4 * b + 4)
                dve.reciprocal(rsum[:, b, :], ssum[:, b, :]).then_inc(rs_made, 1)
                dve.wait_ge(rs_made, 2 * p + b + 1)
                for g in range(G):
                    ins = dve.tensor_scalar(Pn[:, b, g, 0:S], Pn[:, b, g, 0:S], rsum[:, b, g:g + 1], None, ALU.mult)
                ins.then_inc(norm_done, 1)

            def probs_out(p, n):
                dve.wait_ge(pt_filled, 4 * p + n + 1)
                dve.tensor_copy(PT[:, n // 2, n % 2, :], bank[(6, 5)[n % 2]][:]).then_inc(pt_made, 1)

            for m in range(DC):
                turn_lo(1, m)

            def step(p, first=False, keys_more=True, turn_more=True):
                for n in range(8):
                    bias_in_(p, n)
                    if keys_more and n in (2, 4):
                        keys_lo(p + 1, n // 2 - 1)
                    if n == 5:
                        maxes(p, 0)
                if keys_more:
                    keys_lo(p + 1, 2)
                maxes(p, 1)
                if keys_more:
                    keys_lo(p + 1, 3)
                norm(p, 0)
                probs_out(p, 0)
                norm(p, 1)
                dve.wait_ge(norm_done, 2 * p + 2)
                dve.tensor_tensor(ptdiag[:], Pn[:, :, :, SF].unsqueeze(3).to_broadcast([P, 2, G, T]),
                                  eye32[:].unsqueeze(1).unsqueeze(1).to_broadcast([P, 2, G, T]), ALU.mult
                                  ).then_inc(ptdiag_made, 1)
                probs_out(p, 1)
                dve.wait_ge(scan_in, 48 * p + 48)
                dve.tensor_reduce(wmax[:, bass.ds(p, 1)], w_scan[:], AX.XY, ALU.max,
                                  apply_absolute_value=True).then_inc(scanned, 1)
                probs_out(p, 2)
                probs_out(p, 3)
                if turn_more:
                    turn_lo(p + 2, 0)
                dve.wait_ge(tail_filled, p + 1)
                if not first:
                    dve.wait_ge(tail_added, p)
                dve.tensor_tensor(otail[:], bank[4][:, 0:2 * G * T].rearrange("p (b g t) -> p b g t", b=2, g=G),
                                  vtailT[:, bass.ds(2 * p, 2), :].unsqueeze(3).to_broadcast([P, 2, G, T]), ALU.mult
                                  ).then_inc(otail_made, 1)
                if turn_more:
                    for m in range(1, DC):
                        turn_lo(p + 2, m)

            dve.wait_ge(vt_made, 3)
            step(0, first=True)
            with dve.Fori(1, NPAIR - 2) as p:
                step(p)
            step(NPAIR - 2, turn_more=False)
            step(NPAIR - 1, keys_more=False, turn_more=False)
            dve.wait_ge(scanned, NPAIR)
            dve.tensor_reduce(wtop[:], wmax[:], AX.X, ALU.max).then_inc(wtop_made, 1)

            dve.wait_ge(m_filled, 1)
            dve.scalar_tensor_tensor(mbd[:], bank[3][:].rearrange("p (g c) -> p g c", g=G), INV,
                                     blockmask[:].unsqueeze(1).to_broadcast([P, G, P]), ALU.mult, ALU.mult
                                     ).then_inc(m_made, 1)

            dve.wait_ge(wtop_filled, 1)
            dve.tensor_reduce(wtop1[:], bank[6][0:1, 0:P], AX.X, ALU.max).then_inc(wide_made, 1)
            dve.wait_ge(wide_made, 1)
            dve.tensor_scalar(wide[:], wtop1[:], float(W_EXACT), None, ALU.is_gt).then_inc(wide_made, 1)

            dve.wait_ge(tail_added, NPAIR)
            for g in range(G):
                dve.tensor_scalar(oT2[:, g, :], oT2[:, g, :], bvc[:, g:g + 1], None, ALU.add).then_inc(ob_made, 1)

            def ln_start(half):
                lo = 4 * half
                for i in range(lo, lo + 4):
                    ins = dve.bn_aggr(mv[:, i, :], stats[:, i, :])
                link(ins)
                dve.tensor_scalar(ve[:, lo:lo + 4], mv[:, lo:lo + 4, 1], EPS, None, ALU.add).then_inc(ln_var, 1)

            def ln_rstd(half, stds):
                dve.wait_ge(ln_std, stds)
                newton(slice(4 * half, 4 * half + 4))

            def ln_end(half, dst):
                lo = 4 * half
                for i in range(lo, lo + 4):
                    dve.tensor_scalar(dst[:, i - lo, :], xres[:, i, :], mv[:, i, 0:1], rstd[:, i:i + 1],
                                      ALU.subtract, ALU.mult).then_inc(xh_made, 1)

            def ln_tiles(half, dst, stds):
                ln_start(half)
                ln_rstd(half, stds)
                ln_end(half, dst)

            def x2_low(half):
                for k in range(DC):
                    dve.wait_ge(x2t_hi, DC * half + k + 1)
                    cols = slice(half * BANK, (half + 1) * BANK)
                    dve.tensor_tensor(xn2_lo[:, k, cols], bank[X2_BANK[k]][:], xn2_hi[:, half, k, :].bitcast(F32),
                                      ALU.subtract).then_inc(x2t_lo, 1)

            for i in range(NT):
                dve.wait_ge(r1_filled, i + 1)
                dve.wait_ge(xb_made, i + 1)
                dve.tensor_tensor(xres[:, i, :], bank[2 + i % 2][:], xres[:, i, :], ALU.add).then_inc(x1_made, 1)
                dve.wait_ge(x1_made, i + 1)
                link(dve.bn_stats(stats[:, i, :], xres[:, i, :]))
                if i == 3:
                    ln_tiles(0, xh_first, 2)
                    for k in range(DC):
                        dve.wait_ge(qw_hi, k + 1)
                        dve.tensor_tensor(qwp[:, LO, k, :], qw[:, k, :], qwp[:, HI, k, :].bitcast(F32), ALU.subtract
                                          ).then_inc(qw_lo, 1)

                if i == 5:
                    x2_low(0)
            ln_tiles(1, wo_nat, 3)
            x2_low(1)
            steps = [0]

            def link2(ins):
                steps[0] += 1
                ins.then_inc(dve2, 1)
                dve.wait_ge(dve2, steps[0])

            def hs(ap):
                return ap.unsqueeze(2).to_broadcast([P, H, Q32])

            def squares(i):
                dve.wait_ge(qn_made, i + 1)
                dve.tensor_reduce(qsq[:, i, :], sq[:, i % 2].rearrange("p (h d) -> p h d", h=H), AX.X, ALU.add
                                  ).then_inc(sq_read, 1)

            def norms(i):
                dve.wait_ge(sq_read, i + 1)
                if i >= 2:
                    dve.wait_ge(l_filled, i - 1)
                dve.tensor_tensor(dq[:, i % 2], hs(qsq[:, i, :]), eye32[:].unsqueeze(1).to_broadcast([P, H, Q32]),
                                  ALU.mult).then_inc(dq_made, 1)
                link2(dve.tensor_scalar(hqsq[:, i % 2], qsq[:, i, :], -0.5, None, ALU.mult))

            def block2_out(i):
                dve.wait_ge(y_filled, i + 1)
                dve.wait_ge(xb_made, NT + i + 1)
                dve.tensor_tensor(xres[:, i, :], bank[3 + i % 2][:], xres[:, i, :], ALU.add).then_inc(x2_made, 1)
                dve.wait_ge(x2_made, i + 1)
                link(dve.bn_stats(stats[:, i, :], xres[:, i, :]))

            for i in range(2):
                squares(i)
                norms(i)
            for i in range(NT):
                dve.wait_ge(l_filled, i + 1)
                dve.tensor_tensor(lg[:], bank[i % 2][:].rearrange("p (h s) -> p h s", h=H), hs(hqsq[:, i % 2]),
                                  ALU.add).then_inc(l_read, 1)
                dve.wait_ge(l_read, i + 1)
                link2(dve.tensor_reduce(m2[:], lg[:], AX.X, ALU.max))
                dve.tensor_tensor(lg2[:], lg[:], hs(m2[:]), ALU.subtract).then_inc(l2_made, 1)
                if i + 2 < NT:
                    squares(i + 2)
                if i >= 2:
                    block2_out(i - 2)
                dve.wait_ge(e2_made, i + 1)
                link2(dve.tensor_reduce(s2[:], e2[:], AX.X, ALU.add))
                link2(dve.reciprocal(rs2[:], s2[:]))
                link2(dve.tensor_tensor(p2[:], e2[:], hs(rs2[:]), ALU.mult))
                if i:
                    dve.wait_ge(pbd_made, i)
                dve.transpose(p2T[:].rearrange("p h s -> p (h s)"), p2[:].rearrange("p h s -> p (h s)")
                              ).then_inc(p2T_made, 1)
                if i + 2 < NT:
                    norms(i + 2)
                if i == 7:
                    ln_rstd(0, 4)
                    ln_end(0, xh3[:, 0:4])
                    block2_out(6)
                if i == 5:
                    ln_start(0)
            def x3_low(half):
                cols = slice(half * BANK, (half + 1) * BANK)
                for k in range(DC):
                    b = bank[X3_BANK[half][k]]
                    dve.wait_ge(x3_hi, 4 * half + k + 1)
                    dve.tensor_tensor(xn3T[:, LO, k, cols], b[:], xn3T[:, HI, k, cols].bitcast(F32),
                                      ALU.subtract).then_inc(x3_lo, 1)

            def w_lo(n, par, w, saved=False):
                dve.wait_ge(fw_hi, 3 * n + w + 1)
                if not saved:
                    dve.tensor_copy(w_saved[:, bass.ds(n, 1), w, :], bank[(3 * par + w) % 2][:].unsqueeze(1)
                                    ).then_inc(w_kept, 1)
                whole = w_saved[:, bass.ds(n - NJ, 1), w, :] if saved else bank[(3 * par + w) % 2][:].unsqueeze(1)
                dve.tensor_tensor(wT[:, par, w:w + 1, LO, :], whole, wT[:, par, w:w + 1, HI, :].bitcast(F32),
                                  ALU.subtract).then_inc(fw_lo, 1)

            def ffn_step(n, par, more=True, saved=False, tokens=None):
                if more:
                    w_lo(n + 1, 1 - par, 0, saved)
                    w_lo(n + 1, 1 - par, 1, saved)
                if tokens == "normalise":
                    w_lo(n + 1, 1 - par, 2)
                    ln_rstd(1, 5)
                    ln_end(1, xh3[:, 4:8])
                if tokens == "split":
                    x3_low(1)
                dve.wait_ge(u_filled, n + 1)
                dve.wait_ge(g_made, n + 1)
                if not (isinstance(n, int) and n < 1):
                    dve.wait_ge(h_lo, n)
                dve.scalar_tensor_tensor(hf[:], bank[3][:], WSCALE, sg[:], ALU.mult, ALU.mult).then_inc(h_made, 1)
                dve.wait_ge(h_hi, n + 1)
                dve.tensor_tensor(hT[:, par, LO, :], hf[:], hT[:, par, HI, :].bitcast(F32), ALU.subtract
                                  ).then_inc(h_lo, 1)
                if more and tokens != "normalise":
                    w_lo(n + 1, 1 - par, 2, saved)

            w_lo(0, 0, 0)
            w_lo(0, 0, 1)
            x3_low(0)
            w_lo(0, 0, 2)
            block2_out(NT - 1)
            ln_start(1)
            for half in range(2):
                base = half * NJ
                if half:
                    dve.wait_ge(w_kept, 3 * NJ)
                ffn_step(base, 0, saved=half, tokens=None if half else "normalise")
                ffn_step(base + 1, 1, saved=half, tokens=None if half else "split")
                with dve.Fori(1, NJ // 2 - 1) as it:
                    for u in range(2):
                        ffn_step(2 * it + (base + u), u, saved=half)
                ffn_step(base + NJ - 2, 0, saved=half)
                ffn_step(base + NJ - 1, 1, more=half == 0, saved=True)
                for t in range(4):
                    i = 4 * half + t
                    dve.wait_ge(*((acc_filled, 3 * half + t + 1) if t < 3 else (d_done, base + NJ)))
                    dve.scalar_tensor_tensor(xres[:, i, :], bank[4 + t][:], WSCALE, xres[:, i, :],
                                             ALU.mult, ALU.add).then_inc(x3_made, 1)


_INS = ["x", "ctx_1024", "mask_Bx1xSxS2_bf1", "L0_xattn_Wq", "L0_xattn_bq", "L0_xattn_Wk", "L0_xattn_bk",
        "L0_xattn_Wv", "L0_xattn_bv", "L0_xattn_Wo", "L0_xattn_bo", "L0_xattn_rel_emb", "L0_attn_q_weight",
        "L0_attn_v_weight", "L0_attn_out_w", "L0_attn_out_b", "L0_ffn_w_gate", "L0_ffn_w_up", "L0_ffn_w_down"]
_OUTS = [((32, 32, 512), "float32")]


def kernel(**inputs):
    import numpy as _np
    import concourse.bacc as _bacc
    from concourse.bass_utils import run_bass_kernel_spmd as _run

    nc = _bacc.Bacc("TRN2", target_bir_lowering=False, num_devices=1)
    arrays, args = {}, []
    for name in _INS:
        a = _np.ascontiguousarray(inputs[name])
        if a.dtype == _np.bool_:
            a = a.view(_np.uint8)
        arrays[f"in_{name}"] = a
        args.append(nc.dram_tensor(f"in_{name}", a.shape, mybir.dt.from_np(a.dtype), kind="ExternalInput").ap())
    for i, (shape, dtype) in enumerate(_OUTS):
        args.append(nc.dram_tensor(f"out_{i}", shape, mybir.dt.from_np(_np.dtype(dtype)), kind="ExternalOutput").ap())
    perceiver_kernel(nc, *args)
    r = _run(nc, [arrays], core_ids=[0])
    return r.results[0]["out_0"]
```
